# Optimizing a Trainium2 kernel written in Bass

```python
import numpy as np
import jax
import jax.numpy as jnp

def _softmax(x, axis=-1):
    return jax.nn.softmax(x, axis=axis)

def _gelu(x):
    return jax.nn.gelu(x, approximate=True)

def _silu(x):
    return jax.nn.silu(x)

def _sigmoid(x):
    return jax.nn.sigmoid(x)

def _layernorm(x, axis=-1, eps=1e-05):
    m = jnp.mean(x, axis=axis, keepdims=True)
    v = jnp.var(x, axis=axis, keepdims=True)
    return (x - m) / jnp.sqrt(v + eps)

def _scatter_add(tgt, idx, src, axis=0):
    return tgt.at[idx].add(src)

def _segment_sum(src, seg, n):
    return jax.ops.segment_sum(src, seg, n)
kernel_name = 'mk_gnn_preln_d4_gnn_r32_9aa2c1'

def setup_inputs(seed: int=0):
    np.random.seed(seed)
    _w = jnp.asarray

    def _rec_inputs():
        import jax
        import jax.numpy as jnp
        _gk = jax.random.key(seed)
        x = -0.0002117 + 1 * jax.random.normal(jax.random.fold_in(_gk, 1), (3125, 256), jnp.float32)
        src = jax.random.randint(jax.random.fold_in(_gk, 2), (50000,), 0, 3125, jnp.int32)
        dst = jnp.minimum((3125 * jax.random.uniform(jax.random.fold_in(_gk, 3), (50000,)) ** 2.0).astype(jnp.int32), 99999)
        _o = jnp.argsort(dst, stable=True)
        src = src[_o]
        dst = dst[_o]
        edge_attr_5 = 0.000704708 + 1.00024 * jax.random.normal(jax.random.fold_in(_gk, 11), (50000, 5), jnp.float32)
        edge_weight = jax.random.uniform(jax.random.fold_in(_gk, 13), (50000,), jnp.float32, 0.0, 0.999998)
        return (x, src, dst, edge_attr_5, edge_weight)
    x, src, dst, edge_attr_5, edge_weight = _rec_inputs()

    def _L0_gnn_setup():
        import jax, jax.numpy as jnp
        import numpy as np
        N, M, E, H = (3125, 6250, 12500, 256)
        BN_EPS = 1e-05

        def _bn_relu(x, gamma, beta):
            mu = jnp.mean(x, axis=0)
            var = jnp.var(x, axis=0)
            return jax.nn.relu((x - mu) * jax.lax.rsqrt(var + BN_EPS) * gamma + beta)
        key = jax.random.key(seed)
        ks = jax.random.split(key, 12)
        node_rep = jax.random.normal(ks[0], (N, H), dtype=jnp.float32)
        edge_rep = jax.random.normal(ks[1], (M, H), dtype=jnp.float32)
        src = jax.random.randint(ks[2], (E,), 0, N)
        dst = jax.random.randint(ks[3], (E,), 0, M)
        node2edge_index = jnp.stack([src, dst], axis=0)
        s1 = 1.0 / np.sqrt(2 * H)
        s2 = 1.0 / np.sqrt(H)
        s3 = 1.0 / np.sqrt(2 * H)
        W1 = jax.random.uniform(ks[4], (2 * H, H), jnp.float32, -s1, s1)
        W2a = jax.random.uniform(ks[5], (H, 2 * H), jnp.float32, -s2, s2)
        W2b = jax.random.uniform(ks[6], (2 * H, H), jnp.float32, -s3, s3)
        g1 = jnp.ones((H,), jnp.float32)
        b1 = jnp.zeros((H,), jnp.float32)
        g2a = jnp.ones((2 * H,), jnp.float32)
        b2a = jnp.zeros((2 * H,), jnp.float32)
        g2b = jnp.ones((H,), jnp.float32)
        b2b = jnp.zeros((H,), jnp.float32)
        epsilon = jnp.zeros((), jnp.float32)
        return {'node_rep': node_rep, 'node2edge_index': node2edge_index, 'edge_rep': edge_rep, 'W1': W1, 'g1': g1, 'b1': b1, 'W2a': W2a, 'g2a': g2a, 'b2a': b2a, 'W2b': W2b, 'g2b': g2b, 'b2b': b2b, 'epsilon': epsilon}
    _L0_gnn_all = _L0_gnn_setup()
    _L0_gnn_in = {k: v for k, v in _L0_gnn_all.items() if k in ('edge_rep', 'W1', 'g1', 'b1', 'W2a', 'g2a', 'b2a', 'W2b', 'g2b', 'b2b', 'epsilon')}
    del _L0_gnn_all

    def _L1_gnn_setup():
        import jax, jax.numpy as jnp
        import numpy as np
        ALPHA = 0.9

        def _gcn_norm(edge_index, edge_weight, num_nodes):
            row, col = (edge_index[0], edge_index[1])
            deg = jax.ops.segment_sum(edge_weight, col, num_segments=num_nodes)
            dinv = jnp.where(deg > 0, jax.lax.rsqrt(jnp.where(deg > 0, deg, 1.0)), 0.0)
            return dinv[row] * edge_weight * dinv[col]

        def _propagate(h, edge_index, norm, num_nodes):
            row, col = (edge_index[0], edge_index[1])
            msg = h[row] * norm[:, None]
            return jax.ops.segment_sum(msg, col, num_segments=num_nodes)
        key = jax.random.key(seed)
        ks = jax.random.split(key, 7)
        N, E, C, G, L = (50000, 25000, 256, 5, 3)
        x = jax.random.normal(ks[0], (N, C), dtype=jnp.float32)
        edge_index = jax.random.randint(ks[1], (2, E), 0, N, dtype=jnp.int64)
        edge_weight = jax.random.uniform(ks[2], (E,), dtype=jnp.float32)
        edge_attr = jax.random.normal(ks[3], (E, G), dtype=jnp.float32)
        sc = 1.0 / np.sqrt(C)
        lin0_w = jax.random.normal(ks[4], (C, C), dtype=jnp.float32) * sc
        lin0_b = jax.random.normal(ks[5], (C,), dtype=jnp.float32) * sc
        conv_w = jax.random.normal(ks[6], (L, C, C), dtype=jnp.float32) * sc
        return {'x': x, 'edge_index': edge_index, 'edge_weight': edge_weight, 'edge_attr': edge_attr, 'lin0_w': lin0_w, 'lin0_b': lin0_b, 'conv_w': conv_w}
    _L1_gnn_all = _L1_gnn_setup()
    _L1_gnn_in = {k: v for k, v in _L1_gnn_all.items() if k in ('lin0_w', 'lin0_b', 'conv_w')}
    del _L1_gnn_all

    def _L2_gnn_setup():
        import jax, jax.numpy as jnp
        import numpy as np
        N, IN_CH, HEADS, OUT_CH, E = (50000, 256, 4, 64, 25000)
        key = jax.random.key(seed)
        k1, k2, k3, k4, k5 = jax.random.split(key, 5)
        x = jax.random.normal(k1, (N, IN_CH), dtype=jnp.float32)
        edge_index = jax.random.randint(k2, (2, E), 0, N, dtype=jnp.int64)
        bw = float(np.sqrt(6.0 / (IN_CH + HEADS * OUT_CH)))
        ba = float(np.sqrt(6.0 / (HEADS + OUT_CH)))
        weight = jax.random.uniform(k3, (IN_CH, HEADS * OUT_CH), jnp.float32, -bw, bw)
        attn_l = jax.random.uniform(k4, (HEADS, OUT_CH), jnp.float32, -ba, ba)
        attn_r = jax.random.uniform(k5, (HEADS, OUT_CH), jnp.float32, -ba, ba)
        return {'x': x, 'edge_index': edge_index, 'weight': weight, 'attn_l': attn_l, 'attn_r': attn_r}
    _L2_gnn_all = _L2_gnn_setup()
    _L2_gnn_in = {k: v for k, v in _L2_gnn_all.items() if k in ('weight', 'attn_l', 'attn_r')}
    del _L2_gnn_all

    def _L3_gnn_setup():
        import jax, jax.numpy as jnp
        import numpy as np
        N = 10000
        E = 10000
        D = 256
        key = jax.random.key(seed)
        ks = jax.random.split(key, 10)
        s = 1.0 / np.sqrt(D)
        return {'x0': jax.random.normal(ks[0], (N, D), jnp.float32), 'edge_index': jax.random.randint(ks[1], (2, E), 0, N, jnp.int32), 'W1': jax.random.normal(ks[2], (D, D), jnp.float32) * s, 'b1': jax.random.normal(ks[3], (D,), jnp.float32) * s, 'W2': jax.random.normal(ks[4], (D, D), jnp.float32) * s, 'b2': jax.random.normal(ks[5], (D,), jnp.float32) * s, 'wa1': jax.random.normal(ks[6], (D,), jnp.float32) * s, 'ba1': jax.random.normal(ks[7], (1,), jnp.float32) * s, 'wa2': jax.random.normal(ks[8], (D,), jnp.float32) * s, 'ba2': jax.random.normal(ks[9], (1,), jnp.float32) * s}
    _L3_gnn_all = _L3_gnn_setup()
    _L3_gnn_in = {k: v for k, v in _L3_gnn_all.items() if k in ('W1', 'b1', 'W2', 'b2', 'wa1', 'ba1', 'wa2', 'ba2')}
    del _L3_gnn_all
    return {'x': x, 'src': src, 'dst': dst, 'edge_attr_5': edge_attr_5, 'edge_weight': edge_weight, 'L0_gnn_edge_rep': _L0_gnn_in['edge_rep'], 'L0_gnn_W1': _L0_gnn_in['W1'], 'L0_gnn_g1': _L0_gnn_in['g1'], 'L0_gnn_b1': _L0_gnn_in['b1'], 'L0_gnn_W2a': _L0_gnn_in['W2a'], 'L0_gnn_g2a': _L0_gnn_in['g2a'], 'L0_gnn_b2a': _L0_gnn_in['b2a'], 'L0_gnn_W2b': _L0_gnn_in['W2b'], 'L0_gnn_g2b': _L0_gnn_in['g2b'], 'L0_gnn_b2b': _L0_gnn_in['b2b'], 'L0_gnn_epsilon': _L0_gnn_in['epsilon'], 'L1_gnn_lin0_w': _L1_gnn_in['lin0_w'], 'L1_gnn_lin0_b': _L1_gnn_in['lin0_b'], 'L1_gnn_conv_w': _L1_gnn_in['conv_w'], 'L2_gnn_weight': _L2_gnn_in['weight'], 'L2_gnn_attn_l': _L2_gnn_in['attn_l'], 'L2_gnn_attn_r': _L2_gnn_in['attn_r'], 'L3_gnn_W1': _L3_gnn_in['W1'], 'L3_gnn_b1': _L3_gnn_in['b1'], 'L3_gnn_W2': _L3_gnn_in['W2'], 'L3_gnn_b2': _L3_gnn_in['b2'], 'L3_gnn_wa1': _L3_gnn_in['wa1'], 'L3_gnn_ba1': _L3_gnn_in['ba1'], 'L3_gnn_wa2': _L3_gnn_in['wa2'], 'L3_gnn_ba2': _L3_gnn_in['ba2']}

def reference(x, src, dst, edge_attr_5, edge_weight, L0_gnn_edge_rep, L0_gnn_W1, L0_gnn_g1, L0_gnn_b1, L0_gnn_W2a, L0_gnn_g2a, L0_gnn_b2a, L0_gnn_W2b, L0_gnn_g2b, L0_gnn_b2b, L0_gnn_epsilon, L1_gnn_lin0_w, L1_gnn_lin0_b, L1_gnn_conv_w, L2_gnn_weight, L2_gnn_attn_l, L2_gnn_attn_r, L3_gnn_W1, L3_gnn_b1, L3_gnn_W2, L3_gnn_b2, L3_gnn_wa1, L3_gnn_ba1, L3_gnn_wa2, L3_gnn_ba2):
    import jax
    import jax.numpy as jnp

    def _L0_gnn_ref(node_rep, node2edge_index, edge_rep, W1, g1, b1, W2a, g2a, b2a, W2b, g2b, b2b, epsilon):
        import jax, jax.numpy as jnp
        import numpy as np
        N, M, E, H = (3125, 6250, 12500, 256)
        BN_EPS = 1e-05

        def _bn_relu(x, gamma, beta):
            mu = jnp.mean(x, axis=0)
            var = jnp.var(x, axis=0)
            return jax.nn.relu((x - mu) * jax.lax.rsqrt(var + BN_EPS) * gamma + beta)
        src = node2edge_index[0]
        dst = node2edge_index[1]
        messages = jnp.concatenate([node_rep[src], edge_rep[dst]], axis=-1)
        messages = _bn_relu(messages @ W1, g1, b1)
        edge_new = jax.ops.segment_sum(messages, dst, num_segments=edge_rep.shape[0])
        aggregate = jax.ops.segment_sum(edge_new[dst], src, num_segments=node_rep.shape[0])
        h = (1.0 + epsilon) * node_rep + aggregate
        h = _bn_relu(h @ W2a, g2a, b2a)
        out = _bn_relu(h @ W2b, g2b, b2b)
        return out

    def _L1_gnn_ref(x, edge_index, edge_weight, edge_attr, lin0_w, lin0_b, conv_w):
        import jax, jax.numpy as jnp
        import numpy as np
        ALPHA = 0.9

        def _gcn_norm(edge_index, edge_weight, num_nodes):
            row, col = (edge_index[0], edge_index[1])
            deg = jax.ops.segment_sum(edge_weight, col, num_segments=num_nodes)
            dinv = jnp.where(deg > 0, jax.lax.rsqrt(jnp.where(deg > 0, deg, 1.0)), 0.0)
            return dinv[row] * edge_weight * dinv[col]

        def _propagate(h, edge_index, norm, num_nodes):
            row, col = (edge_index[0], edge_index[1])
            msg = h[row] * norm[:, None]
            return jax.ops.segment_sum(msg, col, num_segments=num_nodes)
        del edge_attr
        N = x.shape[0]
        norm = _gcn_norm(edge_index, edge_weight, N)
        x0 = jax.nn.relu(x @ lin0_w + lin0_b)
        out = x0
        for li in range(conv_w.shape[0]):
            agg = _propagate(out, edge_index, norm, N)
            sup = (1.0 - ALPHA) * agg + ALPHA * x0
            h = sup @ conv_w[li]
            out = out + jax.nn.relu(h)
        return out

    def _L2_gnn_ref(x, edge_index, weight, attn_l, attn_r):
        import jax, jax.numpy as jnp
        import numpy as np
        N, IN_CH, HEADS, OUT_CH, E = (50000, 256, 4, 64, 25000)
        heads, out_ch = attn_l.shape
        n = x.shape[0]
        xt = jnp.matmul(x, weight).reshape(-1, heads, out_ch)
        row, col = (edge_index[0], edge_index[1])
        alpha_l = jnp.einsum('ehd,hd->eh', xt[row], attn_l)
        alpha_r = jnp.einsum('ehd,hd->eh', xt[col], attn_r)
        alpha = jax.nn.softmax(jax.nn.leaky_relu(alpha_l + alpha_r, 0.01), axis=1)
        tmp = jnp.einsum('nh,nhd->nd', alpha[:n], xt[col[:n]])
        out = jnp.broadcast_to(tmp[:, None, :], (n, heads, out_ch))
        return out.reshape(n, heads * out_ch)

    def _L3_gnn_ref(x0, edge_index, W1, b1, W2, b2, wa1, ba1, wa2, ba2):
        import jax, jax.numpy as jnp
        import numpy as np
        N = 10000
        E = 10000
        D = 256
        n = x0.shape[0]
        leaky = lambda v: jax.nn.leaky_relu(v, 0.2)
        x0_i = leaky(x0 @ W1 + b1)
        x0_j = leaky(x0 @ W2 + b2)
        a1 = x0_i @ wa1 + ba1[0]
        a2 = x0_j @ wa2 + ba2[0]
        row, col = (edge_index[0], edge_index[1])
        att = jax.nn.sigmoid(a1[row] + a2[col])
        msg = att[:, None] * x0_j[col]
        out = jax.ops.segment_sum(msg, row, num_segments=n)
        return out + x0
    edge_index = jnp.stack([src, dst])
    h = jnp.maximum(_layernorm(x, axis=-1), 0.0)
    x = x + _L0_gnn_ref(h, edge_index, L0_gnn_edge_rep, L0_gnn_W1, L0_gnn_g1, L0_gnn_b1, L0_gnn_W2a, L0_gnn_g2a, L0_gnn_b2a, L0_gnn_W2b, L0_gnn_g2b, L0_gnn_b2b, L0_gnn_epsilon)
    h = jnp.maximum(_layernorm(x, axis=-1), 0.0)
    x = x + _L1_gnn_ref(h, edge_index, edge_weight, edge_attr_5, L1_gnn_lin0_w, L1_gnn_lin0_b, L1_gnn_conv_w)
    h = jnp.maximum(_layernorm(x, axis=-1), 0.0)
    x = x + _L2_gnn_ref(h, edge_index, L2_gnn_weight, L2_gnn_attn_l, L2_gnn_attn_r)
    h = jnp.maximum(_layernorm(x, axis=-1), 0.0)
    x = x + _L3_gnn_ref(h, edge_index, L3_gnn_W1, L3_gnn_b1, L3_gnn_W2, L3_gnn_b2, L3_gnn_wa1, L3_gnn_ba1, L3_gnn_wa2, L3_gnn_ba2)
    return x

_drawn_inputs = setup_inputs


def setup_inputs(seed=0):
    import zlib

    import numpy as np

    out = dict(_drawn_inputs(seed))
    spreads = {'L0_gnn_g1': (1.0, 0.2),
     'L0_gnn_b1': (0.0, 0.1),
     'L0_gnn_g2a': (1.0, 0.2),
     'L0_gnn_b2a': (0.0, 0.31),
     'L0_gnn_g2b': (1.0, 0.2),
     'L0_gnn_b2b': (0.0, 0.1)}
    factors = {'edge_weight': 8.0, 'L3_gnn_b1': 8.0}
    for name, (base, spread) in spreads.items():
        noise = np.random.default_rng([zlib.crc32(name.encode()), seed]).standard_normal(out[name].shape)
        drawn = base * np.exp(spread * noise) if base else spread * noise
        out[name] = jnp.asarray(drawn.astype(out[name].dtype))
    for name, factor in factors.items():
        out[name] = (out[name] * factor).astype(out[name].dtype)
    return out
```

```python
from contextlib import ExitStack

import concourse.bass as bass
from concourse import mybir

ALU = mybir.AluOpType
ACT = mybir.ActivationFunctionType
F32 = mybir.dt.float32
I32 = mybir.dt.int32
AX_X = mybir.AxisListType.X

P = 128
N = 3125
E = 50000
H = 256
NT = -(-N // P)
NP = NT * P
LAST = N - (NT - 1) * P
BLK = 448
NB = -(-N // BLK)
LD = NB * BLK
JH = H // P
HALF = 7
CH = 392
ITER = CH // (2 * HALF)
NHALF = 2 * ITER
PER = -(-E // P)
LASTE = E - (P - 1) * PER
TC = CH + HALF
FIELDS = 7
BN_EPS = 1e-5
SPARE = NP * LD
MROWS = NP + P
COPIES = 3
HEADS = 4
OC = H // HEADS
XW = H + 2 * HEADS
GROUPS = ((0, 4), (4, 3))
RING = 3
RINGW = 4 * BLK
ALPHA = 0.9
VECS = (("g2a", 4), ("b2a", 4), ("g2b", 2), ("b2b", 2), ("lin0_b", 2), ("ab1", 2), ("wa1", 2))
V0 = {name: sum(n for _, n in VECS[:k]) for k, (name, _) in enumerate(VECS)}
LOADS = 7 + len(VECS) + 3


def chain_per(c):
    return len([j for j in range(2 * HALF) if j % COPIES == c])


def chain_before(i, j):
    return chain_per(j % COPIES) * i + j // COPIES


def chain_total(c):
    return chain_per(c) * ITER


class Signal:

    def __init__(self, sem):
        self.sem, self.n, self.extra = sem, 0, 0

    def on(self, ins, by=1):
        ins.then_inc(self.sem, by)
        self.n += by
        return self.n + self.extra


def wait(eng, sem, value):
    if isinstance(value, int) and value <= 0:
        return
    eng.wait_ge(sem, value)


def loop(eng, count, body, signals=()):
    start = {s: s.n for s in signals}
    body(0)
    per = {s: s.n - start[s] for s in signals}
    with eng.Fori(1, count) as i:
        for s in signals:
            s.extra = per[s] * (i - 1)
        body(i)
    for s in signals:
        assert s.n == start[s] + 2 * per[s]
        s.extra = 0
        s.n = start[s] + per[s] * count


def psum_plan():
    tg = [(j, g) for j in range(JH) for g in range(-(-NT // 4))]
    pairs = [(g,) for g in range(-(-NT // 2))]
    dense = [(b0, j, b) for b0, nb in GROUPS for j in range(JH) for b in range(b0, b0 + nb)]
    plan = []

    def add(stage, keys, who):
        plan.extend((stage, k, who) for k in keys)

    add("hT", tg, "V")
    add("P", pairs, "A")
    add("erT", tg, "V")
    add("Q", pairs, "A")
    add("mean", [(0,), (1,)], "V")
    add("agg0", dense, "V")
    add("h2", [(j, b) for j in range(2 * JH) for b in range(NB)], "A")
    add("h3", [(j, b) for j in range(JH) for b in range(NB)], "A")
    add("back0", pairs, "V")
    add("gT1", tg, "V")
    add("x0", [(j, b) for j in range(JH) for b in range(NB)], "A")
    add("x0n", pairs, "V")
    add("dinv", [(g,) for g in range(-(-NT // 4))], "V")
    for li in range(3):
        add(f"agg1{li}", dense, "V")
        add(f"cv{li}", pairs, "V")
    add("gT2", tg, "V")
    add("xt", [(t,) for t in range(NT)], "A")
    add("gT3", tg, "V")
    add("xi", [(j, b) for j in range(JH) for b in range(NB)], "A")
    add("a1", [(b,) for b in range(NB)], "A")
    add("xj", pairs, "V")
    add("agg3", dense, "V")
    add("back3", pairs, "V")
    return plan


def gnn_kernel(nc, x, src, dst, edge_weight, edge_rep, W1, g1, b1, W2a, g2a, b2a, W2b, g2b, b2b,
               epsilon, lin0_w, lin0_b, conv_w, gat_w, attn_l, attn_r, aW1, ab1, aW2, ab2,
               wa1, ba1, wa2, ba2, out):
    plan = psum_plan()
    number = {(s, k): g for g, (s, k, _) in enumerate(plan)}
    nth, seen = [], {"A": 0, "V": 0}
    for _, _, who in plan:
        seen[who] += 1
        nth.append(seen[who])

    with ExitStack() as ctx:
        def sb(name, shape, dt=F32):
            return ctx.enter_context(nc.sbuf_tensor(name, shape, dt))

        def sem(name):
            return ctx.enter_context(nc.semaphore(name))

        ctx.enter_context(nc.allow_non_contiguous_dma(reason="channel vectors onto partitions"))

        counts = nc.dram_tensor("counts", (SPARE + P, 1), F32).ap()
        weights = nc.dram_tensor("weights", (SPARE + P, 1), F32).ap()
        tab_p = nc.dram_tensor("tab_p", (NP, H), F32).ap()
        tab_q = nc.dram_tensor("tab_q", (NP, H), F32).ap()
        zbuf = nc.dram_tensor("zbuf", (P, CH, H), F32).ap()
        msum = [nc.dram_tensor(f"msum{c}", (MROWS, H), F32).ap() for c in range(COPIES)]
        tab_x = nc.dram_tensor("tab_x", (NP, XW), F32).ap()
        tab_l = nc.dram_tensor("tab_l", (NP, HEADS), F32).ap()
        counts_rows = counts[0:SPARE].rearrange("(r c) o -> r (c o)", c=LD)
        weights_rows = weights[0:SPARE].rearrange("(r c) o -> r (c o)", c=LD)

        W_ = NT * H
        reg = sb("reg", [P, 6 * W_])

        def view(at, *dims):
            n = 1
            for d in dims:
                n *= d
            v = reg[:, at:at + n]
            if len(dims) == 1:
                return v
            if len(dims) == 2:
                return v.rearrange("p (a b) -> p a b", a=dims[0])
            return v.rearrange("p (a b c) -> p a b c", a=dims[0], b=dims[1])

        RA, RB, RC, RD, RE, RF = (k * W_ for k in range(6))
        x_nat = view(RA, NT, H)
        g_nat = view(RB, NT, H)
        gT = view(RC, JH, NP)
        ring_t = sb("ring", [P, RING * RINGW])
        ring = [ring_t[:, k * RINGW:(k + 1) * RINGW] for k in range(RING)]

        at = RD
        gp = view(at, 2 * HALF, H); at += 2 * HALF * H
        gq = view(at, 2 * HALF, H); at += 2 * HALF * H
        zz = view(at, 2 * HALF, 2 * H); at += 4 * HALF * H
        table = view(at, TC, FIELDS); at += TC * FIELDS
        midx = view(at, TC); at += TC
        g1row = view(at, H); at += H
        b1row = view(at, H); at += H
        arow = view(at, H); at += H
        brow = view(at, H); at += H
        assert at <= 6 * W_
        zin = view(RD, 2 * HALF, H)
        mo = view(RD + 2 * HALF * H, 2 * HALF, H)
        p_nat, er_nat, erT = view(RD, NT, H), view(RE, NT, H), view(RF, JH, NP)
        mean_row = view(RE + TC, H)
        tmp_i = view(RE, TC).bitcast(I32)
        zeros = ring_t[:, 0:LD]
        raw_src = ring_t[:, LD:LD + PER].bitcast(I32)
        raw_dst = ring_t[:, LD + PER:LD + 2 * PER].bitcast(I32)
        raw_w = ring_t[:, LD + 2 * PER:LD + 3 * PER]
        at = LD + 3 * PER
        eqd = [ring_t[:, at + k * P:at + (k + 1) * P] for k in range(2)]; at += 2 * P
        eqp = [ring_t[:, at + k * P:at + (k + 1) * P] for k in range(2)]; at += 2 * P
        low = [ring_t[:, at + k * P:at + (k + 1) * P] for k in range(2)]; at += 2 * P
        junk = ring_t[:, at:at + P]; at += P
        assert at <= RING * RINGW
        uT, h2T, h3T = view(RD, JH, NP), view(RE, 2 * JH, NP), view(RD, JH, NP)
        xs, supT, x0T, dinv_row = view(RC, NT, H), view(RD, JH, NP), view(RE, JH, NP), view(RF, LD)
        xt_nat, xt_edge = view(RD, NT, XW), view(RD + NT * XW, NT, XW)
        mix = view(RD, NT, H)
        xiT, xj_nat, a1row = view(RD, JH, NP), view(RE, NT, H), view(RF, LD)
        att = [view(RD + k * RINGW, RINGW) for k in range(2)]
        xj_tmp, oT = view(RD, NT, H), view(RC, JH, NP)

        w1 = sb("w1", [P, 2 * JH, H])
        w2a = sb("w2a", [P, JH, 2 * H])
        w2b = sb("w2b", [P, 2 * JH, H])
        lin0 = sb("lin0", [P, JH, H])
        conv = sb("conv", [P, 3 * JH, H])
        gatw = sb("gatw", [P, JH, XW])
        w31 = sb("w31", [P, JH, H])
        w32 = sb("w32", [P, JH, H])
        attn = w1[:, 0:2, :]
        attn_tmp = w1[:, 2:4, :]
        ab2row, wa2row = w2b[:, 0, :], w2b[:, 1, :]
        ident = sb("ident", [P, P])
        ones = sb("ones", [P, P])
        cols = sb("cols", [P, P])
        prior = sb("prior", [P, P])
        rank = sb("rank", [P, 4])
        vec = sb("vec", [P, 24])
        slot = sb("slot", [P, 2, HALF, FIELDS])
        pair_ix = sb("pair_ix", [P, 2 * HALF * 2], I32)
        cw = sb("cw", [P, 2, HALF, 2])
        high = sb("high", [P, 2, NT])
        first_p = sb("first_p", [P, 2, HALF])
        first_d = sb("first_d", [P, 2, HALF])
        vals = sb("vals", [P, 2 * HALF * 2])
        cell_f = sb("cell_f", [P, 2, HALF, 2])
        cell_ix = sb("cell_ix", [P, 2 * HALF * 2], I32)
        mslot = sb("mslot", [P, 2, HALF])
        m_ix = sb("m_ix", [P, 2 * HALF], I32)
        stats = sb("stats", [P, 28, 6])
        mv = sb("mv", [P, NT, 2])
        sc = sb("sc", [P, 4, NT])
        dinv = sb("dinv", [P, NT])
        a2 = sb("a2", [P, NT])
        epsc = sb("epsc", [P, 4])
        i_src = sb("i_src", [P, NT], I32)
        i_dst = sb("i_dst", [P, NT], I32)
        el = sb("el", [P, NT, HEADS])
        al = sb("al", [P, NT, HEADS])
        am = sb("am", [P, 2, NT])

        ps = [ctx.enter_context(nc.psum_tensor(f"ps{k}", [P, 512], F32)) for k in range(8)]

        memset_done = sem("memset_done")
        consts_ready = sem("consts_ready")
        raw_ready = sem("raw_ready")
        x_loaded = sem("x_loaded")
        er_loaded = sem("er_loaded")
        w_loaded = sem("w_loaded")
        w1_loaded = sem("w1_loaded")
        zeroed = sem("zeroed")
        filled, drained_v, drained_a = sem("filled"), sem("drained_v"), sem("drained_a")
        drained = {"V": drained_v, "A": drained_a}
        ln_var, ln_std, ln_scale, ln_out = sem("ln_var"), sem("ln_std"), sem("ln_scale"), sem("ln_out")
        centred, tables_stored = sem("centred"), sem("tables_stored")
        prep_done, rows_ready, eq_ready, cnt_done, cell_ready = (
            sem("prep_done"), sem("rows_ready"), sem("eq_ready"), sem("cnt_done"), sem("cell_ready"))
        z_ready, sq_ready, stat_done = sem("z_ready"), sem("sq_ready"), sem("stat_done")
        gathered = [sem(f"gathered{k}") for k in range(2 * HALF)]
        count_added, weight_added = sem("count_added"), sem("weight_added")
        z_stored = [sem(f"z_stored{h}") for h in range(2)]
        pool_go = sem("pool_go")
        bn_var, bn_std, edge_bn, deg_var, deg_std = (
            sem("bn_var"), sem("bn_std"), sem("edge_bn"), sem("deg_var"), sem("deg_std"))
        z_loaded = [sem(f"z_loaded{h}") for h in range(2)]
        affine, relu_done, m_rows, m_eq, m_sum, m_out, m_prep = (
            sem("affine"), sem("relu_done"), sem("m_rows"), sem("m_eq"), sem("m_sum"), sem("m_out"), sem("m_prep"))
        m_added = [sem(f"m_added{c}") for c in range(COPIES)]
        en_loaded, en_ready = sem("en_loaded"), sem("en_ready")
        ring_full = [sem(f"ring_full{k}") for k in range(RING)]
        ring_used, att_sig, att_ready, att_used = sem("ring_used"), sem("att_sig"), sem("att_ready"), sem("att_used")
        bnn_var, bnn_std, bnn_scale, bnn_relu = sem("bnn_var"), sem("bnn_std"), sem("bnn_scale"), sem("bnn_relu")
        xs_ready, sup_tail = sem("xs_ready"), sem("sup_tail")
        gat_w_ready, xt_stored, gi_ready, gat_loaded, edge_l, edge_x = (
            sem("gat_w_ready"), sem("xt_stored"), sem("gi_ready"), sem("gat_loaded"), sem("edge_l"), sem("edge_x"))
        gi_cleared = sem("gi_cleared")
        exp_in, exp_out = sem("exp_in"), sem("exp_out")
        late_rows, xi_ready, xj_ready, out_t, out_ready, stored = (
            sem("late_rows"), sem("xi_ready"), sem("xj_ready"), sem("out_t"), sem("out_ready"), sem("stored"))
        row_free, tail0 = sem("row_free"), sem("tail0")

        def nat(d, rows=NP):
            return d[0:(NT - 1) * P].rearrange("(t p) c -> p t c", p=P)

        def bcast(v, n):
            return v.unsqueeze(2).to_broadcast([v.shape[0], v.shape[1], n])

        def empty_bank(eng, g, also=()):
            eng.wait_ge(filled, g + 1)
            return ps[g % 8]

        def tiles_of(key, per):
            return range(key[-1] * per, min(NT, key[-1] * per + per))

        dense_last = {}
        passes = ["agg0", "agg10", "agg11", "agg12", "agg3"]
        for pi, name in enumerate(passes):
            for gi, (b0, nb) in enumerate(GROUPS):
                dense_last[pi, gi] = number[name, (b0, JH - 1, b0 + nb - 1)]

        def tile_seq(pi, gi, t):
            return (pi * 2 + gi) * NT + t

        def uses_before(q):
            return q + 1 - (q + 1) // NT

        FIRST3 = tile_seq(4, 0, 0)

        def wait_tile_used(eng, q):
            if q >= FIRST3:
                eng.wait_ge(att_ready, q - FIRST3 + 1)
            elif q % NT == NT - 1:
                eng.wait_ge(filled, dense_last[q // NT // 2, q // NT % 2] + 1)
            else:
                eng.wait_ge(ring_used, uses_before(q))

        block = ctx.enter_context(nc.Block())

        @block.sync
        def _(sp):
            sp.wait_ge(memset_done, 1)
            for dst_t, dram, s in ((x_nat, x, x_loaded), (er_nat, edge_rep[0:N], er_loaded)):
                sp.dma_start(dst_t[:, 0:NT - 1, :], nat(dram)).then_inc(s, 16)
                sp.dma_start(dst_t[0:48, NT - 1, :], dram[(NT - 1) * P:(NT - 1) * P + 48]).then_inc(s, 16)
                sp.dma_start(dst_t[48:LAST, NT - 1, :], dram[(NT - 1) * P + 48:N]).then_inc(s, 16)
                if s is x_loaded:
                    sp.dma_start(w1[:, :, :], W1.rearrange("(j p) n -> p j n", p=P)).then_inc(w1_loaded, 16)
            for raw, dram in ((raw_src, src), (raw_dst, dst), (raw_w, edge_weight)):
                sp.dma_start(raw[0:P - 1, :], dram[0:(P - 1) * PER].rearrange("(p c) -> p c", c=PER)).then_inc(raw_ready, 16)
                sp.dma_start(raw[P - 1:P, 0:LASTE], dram[(P - 1) * PER:E].unsqueeze(0)).then_inc(raw_ready, 16)
            sp.wait_ge(memset_done, 2)
            for m in (counts, weights):
                rows = m[0:SPARE].rearrange("(t p c) o -> p t (c o)", p=P, c=LD)
                for t in range(NT):
                    sp.dma_start(rows[:, t, :], zeros[:, :]).then_inc(zeroed, 16)
                sp.dma_start(m[SPARE:SPARE + P], zeros[:, 0:1]).then_inc(zeroed, 16)
            for m in msum:
                rows = m.rearrange("(p a) c -> p (a c)", p=P)
                width = MROWS * H // P // 4
                for a in range(4):
                    sp.dma_start(rows[:, a * width:(a + 1) * width], zeros[:, 0:width]).then_inc(zeroed, 16)
            for tab in (tab_p, tab_q):
                sp.dma_start(tab[N:NP], zeros[0:NP - N, 0:H]).then_inc(tables_stored, 16)
            sp.dma_start(w2a[:, :, :], W2a.rearrange("(j p) n -> p j n", p=P)).then_inc(w_loaded, 16)
            sp.dma_start(w2b[:, :, :], W2b.rearrange("(j p) n -> p j n", p=P)).then_inc(w_loaded, 16)
            sp.dma_start(lin0[:, :, :], lin0_w.rearrange("(j p) n -> p j n", p=P)).then_inc(w_loaded, 16)
            sp.dma_start(conv[:, :, :], conv_w.rearrange("l (j p) n -> p (l j) n", p=P)).then_inc(w_loaded, 16)
            sp.dma_start(gatw[:, :, 0:H], gat_w.rearrange("(j p) n -> p j n", p=P)).then_inc(w_loaded, 16)
            sp.dma_start(w31[:, :, :], aW1.rearrange("(j p) n -> p j n", p=P)).then_inc(w_loaded, 16)
            sp.dma_start(w32[:, :, :], aW2.rearrange("(j p) n -> p j n", p=P)).then_inc(w_loaded, 16)
            for (name, n), v in zip(VECS, (g2a, b2a, g2b, b2b, lin0_b, ab1, wa1)):
                o = V0[name]
                sp.dma_start(vec[:, o:o + n], v.rearrange("(j p) -> p j", p=P)).then_inc(w_loaded, 16)
            sp.dma_start(epsc[:, 0:1], epsilon.unsqueeze(0).to_broadcast([P, 1])).then_inc(w_loaded, 16)
            sp.dma_start(epsc[:, 1:2], ba1.unsqueeze(0).to_broadcast([P, 1])).then_inc(w_loaded, 16)
            sp.dma_start(epsc[:, 2:3], ba2.unsqueeze(0).to_broadcast([P, 1])).then_inc(w_loaded, 16)

            for k, (tab, nat_t) in enumerate(((tab_p, p_nat), (tab_q, g_nat))):
                sp.wait_ge(centred, k + 1)
                sp.dma_start(nat(tab), nat_t[:, 0:NT - 1, :]).then_inc(tables_stored, 16)
                sp.dma_start(tab[(NT - 1) * P:(NT - 1) * P + 48], nat_t[0:48, NT - 1, :]).then_inc(tables_stored, 16)
                sp.dma_start(tab[(NT - 1) * P + 48:N], nat_t[48:LAST, NT - 1, :]).then_inc(tables_stored, 16)
            sp.wait_ge(row_free, 1)
            sp.dma_start(g1row, g1.unsqueeze(0).to_broadcast([P, H])).then_inc(late_rows, 16)
            sp.dma_start(b1row, b1.unsqueeze(0).to_broadcast([P, H])).then_inc(late_rows, 16)

            def store_z(i):
                for h in range(2):
                    n = 2 * i + h
                    wait(sp, z_ready, HALF * (n + 1))
                    sp.dma_start(zbuf[:, bass.ds(HALF * n, HALF), :],
                                 zz[:, h * HALF:(h + 1) * HALF, 0:H]).then_inc(z_stored[h], 16)
            loop(sp, ITER, store_z)

            for h in range(2):
                sp.wait_ge(z_stored[h], 16 * ITER)
            sp.wait_ge(stat_done, CH)
            sp.wait_ge(z_ready, CH)

            def load_z(i):
                for h in range(2):
                    n = 2 * i + h
                    wait(sp, m_sum, HALF * (n - 1) if isinstance(n, int) else HALF * (n - 1))
                    sp.dma_start(zin[:, h * HALF:(h + 1) * HALF, :],
                                 zbuf[:, bass.ds(HALF * n, HALF), :]).then_inc(z_loaded[h], 16)
            loop(sp, ITER, load_z)

            for c in range(COPIES):
                sp.wait_ge(m_added[c], 16 * chain_total(c))
            sp.wait_ge(m_prep, NHALF + 1)
            sp.wait_ge(m_out, CH)
            for c, r in enumerate((RB, RE, RF)):
                sp.dma_start(view(r, NT, H), msum[c][0:NP].rearrange("(t p) c -> p t c", p=P)).then_inc(en_loaded, 16)

            def stream(pi):
                rows = counts_rows if pi in (0, 4) else weights_rows
                for gi, (b0, nb) in enumerate(GROUPS):
                    for t in range(NT):
                        q = tile_seq(pi, gi, t)
                        if q == 0:
                            sp.wait_ge(count_added, 16 * CH)
                            sp.wait_ge(m_sum, CH)
                        if pi == 1 and q % NT == 0:
                            sp.wait_ge(weight_added, 16 * CH)
                        if q >= RING:
                            wait_tile_used(sp, q - RING)
                        sp.dma_start(ring[q % RING][:, 0:nb * BLK],
                                     rows[t * P:(t + 1) * P, b0 * BLK:(b0 + nb) * BLK]).then_inc(ring_full[q % RING], 16)

            for pi in range(4):
                stream(pi)
                if pi == 0:
                    sp.wait_ge(filled, number["Q", (12,)] + 1)
                    sp.dma_start(attn[:, 0, :], attn_l.rearrange("h d -> (h d)").unsqueeze(0).to_broadcast([P, H])).then_inc(gat_loaded, 16)
                    sp.dma_start(attn[:, 1, :], attn_r.rearrange("h d -> (h d)").unsqueeze(0).to_broadcast([P, H])).then_inc(gat_loaded, 16)
            sp.wait_ge(drained_a, nth[number["xt", (NT - 1,)]])
            sp.dma_start(tab_x.rearrange("(t p) c -> p t c", p=P), xt_nat).then_inc(xt_stored, 16)
            sp.dma_start(tab_l.rearrange("(t p) c -> p t c", p=P), xt_nat[:, :, H:H + HEADS]).then_inc(xt_stored, 16)
            sp.wait_ge(filled, number["h3", (JH - 1, NB - 1)] + 1)
            sp.dma_start(ab2row, ab2.unsqueeze(0).to_broadcast([P, H])).then_inc(gat_loaded, 16)
            sp.dma_start(wa2row, wa2.unsqueeze(0).to_broadcast([P, H])).then_inc(gat_loaded, 16)
            stream(4)
            sp.wait_ge(out_ready, 1)
            sp.dma_start(nat(out), x_nat[:, 0:NT - 1, :]).then_inc(stored, 16)
            sp.dma_start(out[(NT - 1) * P:(NT - 1) * P + 48], x_nat[0:48, NT - 1, :]).then_inc(stored, 16)
            sp.dma_start(out[(NT - 1) * P + 48:N], x_nat[48:LAST, NT - 1, :]).then_inc(stored, 16)
            sp.wait_ge(stored, 48)

        @block.gpsimd
        def _(pool):
            pool.memset(ident[:, :], 0.0).then_inc(consts_ready, 1)
            pool.memset(ones[:, :], 1.0).then_inc(consts_ready, 1)
            pool.wait_ge(consts_ready, 2)
            pool.affine_select(out=ident[:, :], in_=ident[:, :], compare_op=ALU.not_equal, fill=1.0,
                               base=0, pattern=[[-1, P]], channel_multiplier=1).then_inc(consts_ready, 1)
            pool.iota(cols[:, :], [[1, P]], base=0, channel_multiplier=0, allow_small_or_imprecise_dtypes=True).then_inc(consts_ready, 1)
            pool.affine_select(out=prior[:, :], in_=ones[:, :], compare_op=ALU.is_gt, fill=0.0,
                               base=0, pattern=[[-1, P]], channel_multiplier=1).then_inc(consts_ready, 1)
            pool.memset(rank[:, 0:1], 0.0).then_inc(consts_ready, 1)
            pool.iota(rank[:, 1:2], [[0, 1]], base=SPARE, channel_multiplier=1, allow_small_or_imprecise_dtypes=True).then_inc(consts_ready, 1)
            pool.iota(rank[:, 2:3], [[0, 1]], base=NP, channel_multiplier=1, allow_small_or_imprecise_dtypes=True).then_inc(consts_ready, 1)

            pool.wait_ge(tables_stored, 16 * 8)
            pool.wait_ge(zeroed, 16 * (2 * (NT + 1) + 4 * COPIES))

            def edges(i):
                for h in range(2):
                    n = 2 * i + h
                    wait(pool, prep_done, n + 1)
                    wait(pool, cell_ready, n + 1)
                    for k in range(HALF):
                        j = h * HALF + k
                        c = 2 * HALF * i + j
                        wait(pool, z_ready, c - 2 * HALF + 1)
                        pool.sem_inc(pool_go, 1)
                        for buf, tab, f in ((gp, tab_p, 0), (gq, tab_q, 1)):
                            pool.indirect_dma_start(
                                buf[:, j, :], None, tab,
                                bass.IndirectOffsetOnAxis(ap=pair_ix[:, 2 * j + f:2 * j + f + 1], axis=0),
                            ).then_inc(gathered[j], 16)
                        for mat, f, s in ((counts, 0, count_added), (weights, 1, weight_added)):
                            wait(pool, s, 16 * c)
                            pool.sem_inc(pool_go, 1)
                            pool.indirect_dma_start(
                                mat, bass.IndirectOffsetOnAxis(ap=cell_ix[:, 2 * j + f:2 * j + f + 1], axis=0),
                                vals[:, 2 * j + f:2 * j + f + 1], None, compute_op=ALU.add,
                            ).then_inc(s, 16)
            loop(pool, ITER, edges)

            def messages(i):
                for h in range(2):
                    n = 2 * i + h
                    wait(pool, m_prep, n + 1)
                    for k in range(HALF):
                        j = h * HALF + k
                        wait(pool, m_out, 2 * HALF * i + j + 1)
                        wait(pool, m_added[j % COPIES], 16 * chain_before(i, j))
                        pool.sem_inc(pool_go, 1)
                        pool.indirect_dma_start(
                            msum[j % COPIES], bass.IndirectOffsetOnAxis(ap=m_ix[:, j:j + 1], axis=0),
                            mo[:, j, :], None, compute_op=ALU.add,
                        ).then_inc(m_added[j % COPIES], 16)
            loop(pool, ITER, messages)

            pool.memset(i_src[:, :], N).then_inc(gi_cleared, 1)
            pool.memset(i_dst[:, :], N).then_inc(gi_cleared, 1)
            pool.wait_ge(gi_cleared, 2)
            full = (NT - 1) * P
            for ix, dram in ((i_src, src), (i_dst, dst)):
                pool.dma_start(ix[:, 0:NT - 1], dram[0:full].rearrange("(t p) -> p t", p=P)).then_inc(gi_ready, 16)
                pool.dma_start(ix[0:LAST, NT - 1:NT], dram[full:N].unsqueeze(1)).then_inc(gi_ready, 16)
            pool.wait_ge(gi_ready, 64)
            pool.wait_ge(xt_stored, 32)
            for t in range(NT):
                pool.indirect_dma_start(el[:, t, :], None, tab_l,
                                        bass.IndirectOffsetOnAxis(ap=i_src[:, t:t + 1], axis=0)).then_inc(edge_l, 16)
                pool.indirect_dma_start(xt_edge[:, t, :], None, tab_x,
                                        bass.IndirectOffsetOnAxis(ap=i_dst[:, t:t + 1], axis=0)).then_inc(edge_x, 16)

        @block.scalar
        def _(act):
            act_step = Signal(ctx.enter_context(nc.semaphore("act_step")))

            def emptied(ins):
                ins.then_inc(drained_a, 1)

            def layernorm(k):
                act.wait_ge(ln_var, k + 1)
                act.activation(sc[:, 1, :], sc[:, 0, :], ACT.Sqrt).then_inc(ln_std, 1)
                act.wait_ge(ln_scale, k + 1)
                for t in range(NT):
                    act.activation(g_nat[:, t, :], x_nat[:, t, :], ACT.Relu, bias=sc[:, 3, t:t + 1],
                                   scale=sc[:, 2, t:t + 1]).then_inc(ln_out, 1)

            def copy_pairs(stage, dest):
                for g in range(-(-NT // 2)):
                    q = number[stage, (g,)]
                    bank = empty_bank(act, q)
                    ts = tiles_of((g,), 2)
                    emptied(act.activation(dest[:, ts[0]:ts[-1] + 1, :],
                                           bank[:, 0:len(ts) * H].rearrange("p (t c) -> p t c", c=H), ACT.Copy))

            layernorm(0)
            copy_pairs("P", p_nat)
            act.wait_ge(drained_v, nth[number["hT", (JH - 1, 6)]])
            copy_pairs("Q", g_nat)

            def squares(i):
                for h in range(2):
                    n = 2 * i + h
                    wait(act, stat_done, HALF * (n - 1))
                    for k in range(HALF):
                        j = h * HALF + k
                        wait(act, z_ready, 2 * HALF * i + j + 1)
                        act.activation(zz[:, j, H:2 * H], zz[:, j, 0:H], ACT.Square).then_inc(sq_ready, 1)
            loop(act, ITER, squares)
            act.wait_ge(bn_var, 1)
            act.activation(arow, arow, ACT.Sqrt).then_inc(bn_std, 1)
            act.wait_ge(deg_var, 1)
            act.activation(sc[:, 1, :], sc[:, 0, :], ACT.Sqrt).then_inc(deg_std, 1)

            def relu_half(n, h):
                wait(act, affine, n + 1)
                act.activation(zin[:, h * HALF:(h + 1) * HALF, :], zin[:, h * HALF:(h + 1) * HALF, :],
                               ACT.Relu).then_inc(relu_done, 1)

            def sums(i):
                for h in range(2):
                    n = 2 * i + h
                    for k in range(HALF):
                        j = h * HALF + k
                        c = 2 * HALF * i + j
                        wait(act, m_sum, c + 1)
                        wait(act, m_added[j % COPIES], 16 * (chain_before(i, j) + 1 - chain_per(j % COPIES)))
                        act.activation(mo[:, j, :], ps[5 + j % 2][:, 0:H], ACT.Copy).then_inc(m_out, 1)
                    if h == 0:
                        relu_half(n + 1, 1)
                    else:
                        relu_half(n + 1, 0)
            relu_half(0, 0)
            loop(act, ITER - 1, sums)
            i = ITER - 1
            for h in range(2):
                for k in range(HALF):
                    j = h * HALF + k
                    c = 2 * HALF * i + j
                    act.wait_ge(m_sum, c + 1)
                    act.wait_ge(m_added[j % COPIES], 16 * (chain_before(i, j) + 1 - chain_per(j % COPIES)))
                    act.activation(mo[:, j, :], ps[5 + j % 2][:, 0:H], ACT.Copy).then_inc(m_out, 1)
                if h == 0:
                    relu_half(NHALF - 1, 1)

            act.wait_ge(en_ready, 1)
            for stage, dest, nj in (("h2", h2T, 2 * JH), ("h3", h3T, JH)):
                if stage == "h3":
                    act.wait_ge(filled, number["h2", (2 * JH - 1, NB - 1)] + 1)
                for j in range(nj):
                    for b in range(NB):
                        bank = empty_bank(act, number[stage, (j, b)])
                        emptied(act.activation(dest[:, j, b * BLK:(b + 1) * BLK], bank[:, 0:BLK], ACT.Copy))
                r = 0 if stage == "h2" else 1
                act.wait_ge(bnn_var, r + 1)
                act.activation(sc[:, 1, 0:nj], sc[:, 0, 0:nj], ACT.Sqrt).then_inc(bnn_std, 1)
                act.wait_ge(bnn_scale, r + 1)
                for j in range(nj):
                    act.activation(dest[:, j, 0:LD], dest[:, j, 0:LD], ACT.Relu, bias=sc[:, 3, j:j + 1],
                                   scale=sc[:, 2, j:j + 1]).then_inc(bnn_relu, 1)

            layernorm(1)
            act.wait_ge(w_loaded, 16 * LOADS)
            act.wait_ge(bnn_relu, 3 * JH)
            act.wait_ge(filled, number["h3", (JH - 1, NB - 1)] + 1)
            for j in range(JH):
                for b in range(NB):
                    bank = empty_bank(act, number["x0", (j, b)])
                    emptied(act.activation(x0T[:, j, b * BLK:(b + 1) * BLK], bank[:, 0:BLK], ACT.Relu,
                                           bias=vec[:, V0["lin0_b"] + j:V0["lin0_b"] + j + 1]))

            layernorm(2)
            for t in range(NT):
                bank = empty_bank(act, number["xt", (t,)])
                emptied(act.activation(xt_nat[:, t, :], bank[:, 0:XW], ACT.Copy))
            act.wait_ge(exp_in, 1)
            act.activation(al[:, :, :], al[:, :, :], ACT.Exp).then_inc(exp_out, 1)

            layernorm(3)
            for j in range(JH):
                for b in range(NB):
                    bank = empty_bank(act, number["xi", (j, b)])
                    emptied(act.activation(xiT[:, j, b * BLK:(b + 1) * BLK], bank[:, 0:BLK], ACT.Identity,
                                           bias=vec[:, V0["ab1"] + j:V0["ab1"] + j + 1]))
            for b in range(NB):
                bank = empty_bank(act, number["a1", (b,)])
                emptied(act.activation(a1row[:, b * BLK:(b + 1) * BLK], bank[:, 0:BLK], ACT.Identity,
                                       bias=epsc[:, 1:2]))
            act.wait_ge(xj_ready, 1)
            act.wait_ge(drained_a, nth[number["a1", (NB - 1,)]])
            u = 0
            for b0, nb in GROUPS:
                for t in range(NT):
                    if u >= 2 and (u - 2) % NT == NT - 1:
                        act.wait_ge(filled, dense_last[4, (u - 2) // NT] + 1)
                    elif u >= 2:
                        act.wait_ge(att_used, uses_before(u - 2))
                    act.activation(att[u % 2][:, 0:nb * BLK], a1row[:, b0 * BLK:(b0 + nb) * BLK], ACT.Sigmoid,
                                   bias=a2[:, t:t + 1]).then_inc(att_sig, 1)
                    u += 1

        @block.tensor
        def _(pe):
            def open_bank(g):
                if g >= 8:
                    who = plan[g - 8][2]
                    pe.wait_ge(drained[who], nth[g - 8])
                return ps[g % 8]

            def to_T(stage, src_nat, done, base):
                for j in range(JH):
                    for gi in range(-(-NT // 4)):
                        bank = open_bank(number[stage, (j, gi)])
                        ts = tiles_of((gi,), 4)
                        for t in ts:
                            if done is not None:
                                pe.wait_ge(done, base + t + 1)
                            m = pe.transpose(bank[:, (t - ts[0]) * P:(t - ts[0] + 1) * P],
                                             src_nat[:, t, j * P:(j + 1) * P], ident[:, :])
                        m.then_inc(filled, 1)

            def node_rows(stage, lhs, rhs, width=H, per=2, nk=JH, base=0):
                for gi in range(-(-NT // per)):
                    bank = open_bank(number[stage, (gi,)])
                    ts = tiles_of((gi,), per)
                    for t in ts:
                        for k in range(nk):
                            m = pe.matmul(bank[:, (t - ts[0]) * width:(t - ts[0] + 1) * width],
                                          lhs[:, k, t * P:(t + 1) * P], rhs[:, base + k, :],
                                          start=(k == 0), stop=(k == nk - 1))
                    m.then_inc(filled, 1)

            def node_cols(stage, w, rhs, nj, nk, ready=None):
                for j in range(nj):
                    for b in range(NB):
                        bank = open_bank(number[stage, (j, b)])
                        for k in range(nk):
                            if ready is not None and j == 0 and b == 0:
                                pe.wait_ge(*ready(k))
                            m = pe.matmul(bank[:, 0:BLK], w[:, k, j * P:(j + 1) * P], rhs[:, k, b * BLK:(b + 1) * BLK],
                                          start=(k == 0), stop=(k == nk - 1))
                        m.then_inc(filled, 1)

            def back(stage, src_T):
                for gi in range(-(-NT // 2)):
                    bank = open_bank(number[stage, (gi,)])
                    ts = tiles_of((gi,), 2)
                    for t in ts:
                        for j in range(JH):
                            o = (t - ts[0]) * H + j * P
                            m = pe.transpose(bank[:, o:o + P], src_T[:, j, t * P:(t + 1) * P], ident[:, :])
                    m.then_inc(filled, 1)

            def dense(pi, lhs):
                name = passes[pi]
                for gi, (b0, nb) in enumerate(GROUPS):
                    for t in range(NT):
                        q = tile_seq(pi, gi, t)
                        u = q - FIRST3
                        if pi == 4:
                            pe.wait_ge(att_ready, u + 1)
                            rows = att[u % 2]
                        else:
                            pe.wait_ge(ring_full[q % RING], 16 * (q // RING + 1))
                            rows = ring[q % RING]
                        for j in range(JH):
                            for b in range(b0, b0 + nb):
                                g = number[name, (b0, j, b)]
                                bank = open_bank(g) if t == 0 else ps[g % 8]
                                m = pe.matmul(bank[:, 0:BLK], lhs[:, t, j * P:(j + 1) * P],
                                              rows[:, (b - b0) * BLK:(b - b0 + 1) * BLK],
                                              start=(t == 0), stop=(t == NT - 1))
                                if t == NT - 1:
                                    m.then_inc(filled, 1)
                        if t < NT - 1:
                            m.then_inc(att_used if pi == 4 else ring_used, 1)

            pe.wait_ge(consts_ready, 8)
            to_T("hT", g_nat, ln_out, 0)
            pe.wait_ge(w1_loaded, 16)
            pe.wait_ge(drained_v, nth[number["hT", (JH - 1, 6)]])
            node_rows("P", gT, w1)
            pe.wait_ge(er_loaded, 48)
            to_T("erT", er_nat, None, 0)
            pe.wait_ge(drained_v, nth[number["erT", (JH - 1, 6)]])
            node_rows("Q", erT, w1, base=JH)
            for k, nat_t in enumerate((p_nat, g_nat)):
                bank = open_bank(number["mean", (k,)])
                pe.wait_ge(drained_a, nth[number["P" if k == 0 else "Q", (12,)]])
                for t in range(NT):
                    m = pe.matmul(bank[:, 0:H], ones[:, :], nat_t[:, t, :], start=(t == 0), stop=(t == NT - 1))
                m.then_inc(filled, 1)
            g = number["mean", (1,)]
            pe.wait_ge(drained_v, nth[g])
            pe.wait_ge(drained_a, nth[number["Q", (12,)]])

            rows_bank, cnt_bank, deg_bank, stat_bank = (ps[0], ps[1]), ps[2], ps[3], ps[4]
            pe.wait_ge(memset_done, 3)
            pe.matmul(deg_bank[:, 0:NT], junk[:, :], ones[:, 0:NT], start=True, stop=False, skip_group_check=True)
            pe.matmul(stat_bank[:, :], junk[:, :], x_nat[:, 0:2, :], start=True, stop=False, skip_group_check=True)

            def chunk_rows(n, h, k):
                c = HALF * n + k
                if k == 0:
                    wait(pe, prep_done, n + 1)
                wait(pe, eq_ready, c - 1)
                bank = rows_bank[(h * HALF + k) % 2]
                pe.matmul(bank[:, 0:P], slot[:, h, k, 0:1].to_broadcast([P, P]), ident[:, :], start=True, stop=True)
                pe.matmul(bank[:, P:2 * P], slot[:, h, k, 1:2].to_broadcast([P, P]), ident[:, :],
                          start=True, stop=True).then_inc(rows_ready, 1)

            def chunk_counts(n, h, k):
                c = HALF * n + k
                s = (h * HALF + k) % 2
                if k == 0:
                    wait(pe, cell_ready, n)
                wait(pe, eq_ready, c + 1)
                pe.matmul(cnt_bank[:, 2 * k:2 * k + 2], eqp[s], cw[:, h, k, :], start=True, stop=True,
                          skip_group_check=True)
                pe.matmul(deg_bank[:, 0:NT], low[s], high[:, s, :], start=False, stop=False,
                          skip_group_check=True).then_inc(cnt_done, 1)

            def chunk_stats(c, j):
                wait(pe, sq_ready, c + 1)
                pe.matmul(stat_bank[:, :], ones[:, :], zz[:, j, :], start=False, stop=False,
                          skip_group_check=True).then_inc(stat_done, 1)

            for k in range(HALF):
                chunk_rows(0, 0, k)
                chunk_counts(0, 0, k)

            def phase1(i):
                for h in range(2):
                    n = 2 * i + h
                    for k in range(HALF):
                        chunk_rows(n + 1, 1 - h, k)
                        chunk_counts(n + 1, 1 - h, k)
                        chunk_stats(2 * HALF * i + h * HALF + k, h * HALF + k)
            loop(pe, ITER, phase1)

            pe.wait_ge(bn_var, 1)
            pe.wait_ge(deg_var, 1)

            def phase2(i):
                for h in range(2):
                    n = 2 * i + h
                    for k in range(HALF):
                        j = h * HALF + k
                        c = 2 * HALF * i + j
                        if k == 0:
                            wait(pe, m_prep, n + 1)
                            for kk in range(2):
                                m_row(c + kk, j + kk, h, kk)
                        elif k + 1 < HALF:
                            m_row(c + 1, j + 1, h, k + 1)
                        if k == 0:
                            wait(pe, relu_done, n + 1)
                        wait(pe, m_eq, c + 1)
                        wait(pe, m_out, c - 1)
                        pe.matmul(ps[5 + j % 2][:, 0:H], eqd[j % 2], zin[:, j, :], start=True, stop=True).then_inc(m_sum, 1)

            def m_row(c, j, h, k):
                wait(pe, m_eq, c - 1)
                pe.matmul(ps[j % 2][:, 0:P], mslot[:, h, k:k + 1].to_broadcast([P, P]), ident[:, :],
                          start=True, stop=True).then_inc(m_rows, 1)
            loop(pe, ITER, phase2)

            pe.wait_ge(en_ready, 1)
            dense(0, g_nat)
            pe.wait_ge(w_loaded, 16 * LOADS)
            pe.wait_ge(drained_v, nth[dense_last[0, 1]])
            node_cols("h2", w2a, uT, 2 * JH, JH)
            node_cols("h3", w2b, h2T, JH, 2 * JH, ready=lambda k: (bnn_relu, k + 1))
            pe.wait_ge(bnn_relu, 3 * JH)
            pe.wait_ge(tail0, 1)
            back("back0", h3T)

            to_T("gT1", g_nat, ln_out, NT)
            pe.wait_ge(drained_v, nth[number["gT1", (JH - 1, 6)]])
            node_cols("x0", lin0, gT, JH, JH)
            pe.wait_ge(drained_a, nth[number["x0", (JH - 1, NB - 1)]])
            pe.wait_ge(sup_tail, 1)
            back("x0n", x0T)
            for gi in range(-(-NT // 4)):
                bank = open_bank(number["dinv", (gi,)])
                ts = tiles_of((gi,), 4)
                for t in ts:
                    m = pe.matmul(bank[:, (t - ts[0]) * P:(t - ts[0] + 1) * P],
                                  dinv[:, t:t + 1].to_broadcast([P, P]), ident[:, :], start=True, stop=True)
                m.then_inc(filled, 1)
            for li in range(3):
                pe.wait_ge(xs_ready, li + 1)
                dense(1 + li, xs)
                pe.wait_ge(drained_v, nth[dense_last[1 + li, 1]])
                node_rows(f"cv{li}", supT, conv, base=li * JH)

            to_T("gT2", g_nat, ln_out, 2 * NT)
            pe.wait_ge(drained_v, nth[number["gT2", (JH - 1, 6)]])
            pe.wait_ge(gat_w_ready, 1)
            node_rows("xt", gT, gatw, width=XW, per=1)

            to_T("gT3", g_nat, ln_out, 3 * NT)
            pe.wait_ge(drained_v, nth[number["gT3", (JH - 1, 6)]])
            node_cols("xi", w31, gT, JH, JH)
            pe.wait_ge(xi_ready, 1)
            for b in range(NB):
                bank = open_bank(number["a1", (b,)])
                for k in range(JH):
                    m = pe.matmul(bank[:, 0:BLK], vec[:, V0["wa1"] + k:V0["wa1"] + k + 1].to_broadcast([P, P]),
                                  xiT[:, k, b * BLK:(b + 1) * BLK], start=(k == 0), stop=(k == JH - 1))
                m.then_inc(filled, 1)
            node_rows("xj", gT, w32)
            dense(4, xj_nat)
            pe.wait_ge(drained_v, nth[dense_last[4, 1]])
            pe.wait_ge(out_t, 1)
            back("back3", oT)

        @block.vector
        def _(v):
            step = Signal(ctx.enter_context(nc.semaphore("dve_step")))
            loop_signals = [step]

            def do(ins):
                v.wait_ge(step.sem, step.on(ins))

            def emptied(ins):
                ins.then_inc(drained_v, 1)

            def after(g):
                v.wait_ge(drained_v, nth[g])

            def layernorm(k):
                for t in range(NT):
                    last = v.bn_stats(stats[:, t, :], x_nat[:, t, :])
                do(last)
                for t in range(NT):
                    last = v.bn_aggr(mv[:, t, :], stats[:, t, :])
                do(last)
                v.tensor_scalar(sc[:, 0, :], mv[:, :, 1], BN_EPS, None, ALU.add).then_inc(ln_var, 1)
                v.wait_ge(ln_std, k + 1)
                do(v.reciprocal(sc[:, 2, :], sc[:, 1, :]))
                v.scalar_tensor_tensor(sc[:, 3, :], mv[:, :, 0], -1.0, sc[:, 2, :], ALU.mult, ALU.mult).then_inc(ln_scale, 1)

            def copy_T(stage, dest):
                for j in range(JH):
                    for gi in range(-(-NT // 4)):
                        bank = empty_bank(v, number[stage, (j, gi)])
                        ts = tiles_of((gi,), 4)
                        emptied(v.tensor_copy(dest[:, j, ts[0] * P:(ts[-1] + 1) * P], bank[:, 0:len(ts) * P]))

            def pair_bank(stage, gi):
                bank = empty_bank(v, number[stage, (gi,)])
                ts = tiles_of((gi,), 2)
                return slice(ts[0], ts[-1] + 1), bank[:, 0:len(ts) * H].rearrange("p (t c) -> p t c", c=H)

            def add_pairs(stage):
                for gi in range(-(-NT // 2)):
                    ts, got = pair_bank(stage, gi)
                    emptied(v.tensor_tensor(x_nat[:, ts, :], x_nat[:, ts, :], got, ALU.add))
                after(number[stage, (12,)])

            v.memset(x_nat[:, NT - 1, :], 0.0)
            v.memset(er_nat[:, NT - 1, :], 0.0).then_inc(memset_done, 1)
            v.memset(zeros, 0.0).then_inc(memset_done, 1)
            v.memset(junk, 0.0).then_inc(memset_done, 1)
            v.wait_ge(x_loaded, 48)
            layernorm(0)
            copy_T("hT", gT)
            copy_T("erT", erT)
            for k, nat_t in enumerate((p_nat, g_nat)):
                bank = empty_bank(v, number["mean", (k,)])
                v.tensor_scalar(mean_row, bank[:, 0:H], 1.0 / N, None, ALU.mult).then_inc(drained_v, 1)
                after(number["mean", (k,)])
                v.tensor_tensor(nat_t, nat_t, mean_row.unsqueeze(1).to_broadcast([P, NT, H]), ALU.subtract).then_inc(centred, 1)
                v.wait_ge(centred, k + 1)

            v.wait_ge(raw_ready, 96)
            v.wait_ge(filled, number["Q", (12,)] + 1)
            do(v.memset(table[:, :, 0:2], float(N)))
            do(v.memset(table[:, :, 2:3], 0.0))
            do(v.memset(table[:, :, 3:FIELDS], 0.0))
            for f, raw in ((0, raw_src), (1, raw_dst), (2, raw_w)):
                for prt, n, o in ((slice(0, P), LASTE, 0), (slice(0, 96), PER - LASTE, LASTE),
                                  (slice(96, P - 1), PER - LASTE, LASTE)):
                    do(v.tensor_copy(table[prt, o:o + n, f], raw[prt, o:o + n]))
            do(v.tensor_copy(tmp_i, table[:, :, 1]))
            do(v.tensor_scalar(tmp_i, tmp_i, 7, None, ALU.arith_shift_right))
            do(v.tensor_copy(table[:, :, 4], tmp_i))
            do(v.scalar_tensor_tensor(table[:, :, 3], table[:, :, 4], -float(P), table[:, :, 1], ALU.mult, ALU.add))
            v.wait_ge(consts_ready, 8)
            for f, hi, lo in ((5, 1, 0), (6, 0, 1)):
                do(v.scalar_tensor_tensor(table[:, :, f], table[:, :, hi], float(LD), table[:, :, lo], ALU.mult, ALU.add))
                do(v.tensor_scalar(table[:, :, f], table[:, :, f], rank[:, 1:2], None, ALU.subtract))
            do(v.memset(cw[:, :, :, 0:1], 1.0))
            v.memset(stats[:, 0, 0:1], 0.0).then_inc(row_free, 1)

            def prep(n, h):
                wait(v, cnt_done, HALF * (n - 1))
                cs = bass.ds(HALF * n, HALF)
                do(v.tensor_copy(slot[:, h], table[:, cs, :]))
                v.tensor_copy(cw[:, h, :, 1], slot[:, h, :, 2])
                v.tensor_copy(pair_ix[:, 2 * h * HALF:2 * (h + 1) * HALF].rearrange("p (k f) -> p k f", f=2),
                              slot[:, h, :, 0:2]).then_inc(prep_done, 1)

            def equal(n, h, k):
                c = HALF * n + k
                s = (h * HALF + k) % 2
                bank = ps[s]
                wait(v, rows_ready, c + 1)
                wait(v, cnt_done, c - 1)
                sd = step.on(v.tensor_scalar(eqd[s], bank[:, P:2 * P], slot[:, h, k, 1:2], None, ALU.is_equal))
                v.tensor_scalar(low[s], cols[:, :], slot[:, h, k, 3:4], slot[:, h, k, 2:3], ALU.is_equal, ALU.mult)
                v.tensor_scalar(high[:, s, :], cols[:, 0:NT], slot[:, h, k, 4:5], None, ALU.is_equal)
                v.wait_ge(step.sem, sd)
                v.scalar_tensor_tensor(eqp[s], bank[:, 0:P], slot[:, h, k, 0:1], eqd[s], ALU.is_equal,
                                       ALU.mult).then_inc(eq_ready, 1)
                do(v.tensor_tensor_reduce(junk, eqd[s], prior[:, :], 1.0, 0.0, ALU.mult, ALU.add, first_d[:, h, k:k + 1]))
                wait(v, eq_ready, c + 1)
                do(v.tensor_tensor_reduce(junk, eqp[s], prior[:, :], 1.0, 0.0, ALU.mult, ALU.add, first_p[:, h, k:k + 1]))

            def cells(n, h):
                hs = slice(2 * h * HALF, 2 * (h + 1) * HALF)
                wait(v, cnt_done, HALF * (n + 1))
                wait(v, count_added, 16 * HALF * (n - 1))
                wait(v, weight_added, 16 * HALF * (n - 1))
                v.tensor_copy(vals[:, hs], ps[2][:, 0:2 * HALF])
                v.tensor_scalar(first_p[:, h, :], first_p[:, h, :], 0.0, None, ALU.is_equal)
                do(v.tensor_scalar(first_d[:, h, :], first_d[:, h, :], 0.0, None, ALU.is_equal))
                for f in range(2):
                    v.tensor_tensor(cell_f[:, h, :, f], slot[:, h, :, 5 + f], first_p[:, h, :], ALU.mult)
                do(v.tensor_scalar(mslot[:, h, :], slot[:, h, :, 1], rank[:, 2:3], None, ALU.subtract))
                do(v.tensor_tensor(mslot[:, h, :], mslot[:, h, :], first_d[:, h, :], ALU.mult))
                v.tensor_scalar(midx[:, bass.ds(HALF * n, HALF)], mslot[:, h, :], rank[:, 2:3], None, ALU.add)
                v.tensor_scalar(cell_ix[:, hs].rearrange("p (k f) -> p k f", f=2), cell_f[:, h, :, :],
                                rank[:, 1:2], None, ALU.add).then_inc(cell_ready, 1)

            def add_z(i, h, k):
                j = h * HALF + k
                n = 2 * i + h
                wait(v, gathered[j], 32 * (i + 1))
                if k == 0:
                    wait(v, z_stored[h], 16 * i)
                    wait(v, stat_done, HALF * (n - 1))
                v.tensor_tensor(zz[:, j, 0:H], gp[:, j, :], gq[:, j, :], ALU.add).then_inc(z_ready, 1)

            prep(0, 0)
            for k in range(HALF):
                equal(0, 0, k)
            cells(0, 0)

            def phase1(i):
                for h in range(2):
                    n = 2 * i + h
                    prep(n + 1, 1 - h)
                    for k in range(HALF):
                        equal(n + 1, 1 - h, k)
                        add_z(i, h, k)
                    cells(n + 1, 1 - h)
            loop(v, ITER, phase1, loop_signals)

            v.wait_ge(stat_done, CH)
            v.wait_ge(late_rows, 32)
            v.wait_ge(cell_ready, NHALF + 1)
            do(v.tensor_scalar(brow, ps[4][:, 0:H], 1.0 / E, None, ALU.mult))
            do(v.tensor_tensor(arow, brow, brow, ALU.mult))
            do(v.scalar_tensor_tensor(arow, ps[4][:, H:2 * H], 1.0 / E, arow, ALU.mult, ALU.subtract))
            do(v.tensor_scalar(arow, arow, 0.0, None, ALU.max))
            v.tensor_scalar(arow, arow, BN_EPS, None, ALU.add).then_inc(bn_var, 1)
            v.wait_ge(cnt_done, HALF * (NHALF + 1))
            do(v.tensor_scalar(dinv[:, :], ps[3][:, 0:NT], 0.0, None, ALU.is_gt))
            do(v.tensor_tensor(sc[:, 2, :], ps[3][:, 0:NT], dinv[:, :], ALU.mult))
            do(v.tensor_tensor(sc[:, 2, :], sc[:, 2, :], dinv[:, :], ALU.subtract))
            v.tensor_scalar(sc[:, 0, :], sc[:, 2, :], 1.0, None, ALU.add).then_inc(deg_var, 1)
            v.wait_ge(bn_std, 1)
            do(v.reciprocal(arow, arow))
            do(v.tensor_tensor(arow, arow, g1row, ALU.mult))
            do(v.tensor_tensor(brow, brow, arow, ALU.mult))
            do(v.tensor_tensor(brow, b1row, brow, ALU.subtract))
            v.wait_ge(deg_std, 1)
            do(v.reciprocal(sc[:, 2, :], sc[:, 1, :]))
            do(v.tensor_tensor(dinv[:, :], dinv[:, :], sc[:, 2, :], ALU.mult))

            def m_half(n, h, i_of):
                wait(v, m_sum, HALF * (n - 1))
                for c in range(COPIES):
                    last = max(j for j in range((h + 1) * HALF) if j % COPIES == c)
                    wait(v, m_added[c], 16 * (chain_before(i_of, last) + 1 - chain_per(c)))
                do(v.tensor_copy(m_ix[:, h * HALF:(h + 1) * HALF], midx[:, bass.ds(HALF * n, HALF)]))
                v.tensor_copy(mslot[:, h, :], table[:, bass.ds(HALF * n, HALF), 1]).then_inc(m_prep, 1)
                hs = slice(h * HALF, (h + 1) * HALF)
                wait(v, z_loaded[h], 16 * (i_of + 1))
                do(v.tensor_tensor(zin[:, hs, :], zin[:, hs, :], arow.unsqueeze(1).to_broadcast([P, HALF, H]), ALU.mult))
                v.tensor_tensor(zin[:, hs, :], zin[:, hs, :], brow.unsqueeze(1).to_broadcast([P, HALF, H]),
                                ALU.add).then_inc(affine, 1)

            def m_equal(i, h):
                for k in range(HALF):
                    j = h * HALF + k
                    c = 2 * HALF * i + j
                    wait(v, m_rows, c + 1)
                    wait(v, m_sum, c - 1)
                    v.tensor_scalar(eqd[j % 2], ps[j % 2][:, 0:P], mslot[:, h, k:k + 1], None, ALU.is_equal).then_inc(m_eq, 1)

            m_half(0, 0, 0)

            def phase2(i):
                m_equal(i, 0)
                m_half(2 * i + 1, 1, i)
                m_equal(i, 1)
                m_half(2 * i + 2, 0, i + 1)
            loop(v, ITER - 1, phase2, loop_signals)
            m_equal(ITER - 1, 0)
            m_half(NHALF - 1, 1, ITER - 1)
            m_equal(ITER - 1, 1)
            v.memset(stats[:, 0, 0:1], 0.0).then_inc(m_prep, 1)

            v.wait_ge(en_loaded, 48)
            do(v.tensor_tensor(g_nat, g_nat, view(RE, NT, H), ALU.add))
            v.tensor_tensor(g_nat, g_nat, view(RF, NT, H), ALU.add).then_inc(en_ready, 1)
            v.wait_ge(w_loaded, 16 * LOADS)
            do(v.tensor_scalar(epsc[:, 3:4], epsc[:, 0:1], 1.0, None, ALU.add))
            for b0, nb in GROUPS:
                for j in range(JH):
                    for b in range(b0, b0 + nb):
                        bank = empty_bank(v, number["agg0", (b0, j, b)])
                        bs = slice(b * BLK, (b + 1) * BLK)
                        emptied(v.scalar_tensor_tensor(uT[:, j, bs], gT[:, j, bs], epsc[:, 3:4], bank[:, 0:BLK],
                                                       ALU.mult, ALU.add))
            for r, (stage, src_T, nj, gam, bet) in enumerate((("h2", h2T, 2 * JH, "g2a", "b2a"), ("h3", h3T, JH, "g2b", "b2b"))):
                for j in range(nj):
                    for b in range(NB):
                        v.wait_ge(drained_a, nth[number[stage, (j, b)]])
                        last = v.bn_stats(stats[:, j * NB + b, :], src_T[:, j, b * BLK:min(N, (b + 1) * BLK)])
                do(last)
                for j in range(nj):
                    last = v.bn_aggr(mv[:, j, :], stats[:, j * NB:(j + 1) * NB, :])
                do(last)
                v.tensor_scalar(sc[:, 0, 0:nj], mv[:, 0:nj, 1], BN_EPS, None, ALU.add).then_inc(bnn_var, 1)
                v.wait_ge(bnn_std, r + 1)
                do(v.reciprocal(sc[:, 2, 0:nj], sc[:, 1, 0:nj]))
                do(v.tensor_tensor(sc[:, 2, 0:nj], sc[:, 2, 0:nj], vec[:, V0[gam]:V0[gam] + nj], ALU.mult))
                do(v.tensor_tensor(sc[:, 3, 0:nj], mv[:, 0:nj, 0], sc[:, 2, 0:nj], ALU.mult))
                v.tensor_tensor(sc[:, 3, 0:nj], vec[:, V0[bet]:V0[bet] + nj], sc[:, 3, 0:nj], ALU.subtract).then_inc(bnn_scale, 1)
            v.memset(h3T[:, :, LD:NP], 0.0).then_inc(tail0, 1)
            add_pairs("back0")

            layernorm(1)
            copy_T("gT1", gT)
            v.wait_ge(filled, number["h3", (JH - 1, NB - 1)] + 1)
            v.memset(x0T[:, :, LD:NP], 0.0)
            v.memset(supT[:, :, LD:NP], 0.0).then_inc(sup_tail, 1)
            for gi in range(-(-NT // 2)):
                ts, got = pair_bank("x0n", gi)
                emptied(v.tensor_copy(g_nat[:, ts, :], got))
            for gi in range(-(-NT // 4)):
                bank = empty_bank(v, number["dinv", (gi,)])
                o = gi * 4 * P
                n = min(4 * P, LD - o)
                emptied(v.tensor_scalar(dinv_row[:, o:o + n], bank[:, 0:n], 1.0 - ALPHA, None, ALU.mult))
            after(number["dinv", (6,)])
            v.wait_ge(filled, number["x0", (JH - 1, NB - 1)] + 1)
            for li in range(3):
                v.tensor_tensor(xs, g_nat, bcast(dinv[:, :], H), ALU.mult).then_inc(xs_ready, 1)
                for b0, nb in GROUPS:
                    for j in range(JH):
                        for b in range(b0, b0 + nb):
                            bank = empty_bank(v, number[f"agg1{li}", (b0, j, b)])
                            bs = slice(b * BLK, (b + 1) * BLK)
                            do(v.tensor_tensor(supT[:, j, bs], bank[:, 0:BLK], dinv_row[:, bs], ALU.mult))
                            emptied(v.scalar_tensor_tensor(supT[:, j, bs], x0T[:, j, bs], ALPHA, supT[:, j, bs],
                                                           ALU.mult, ALU.add))
                for gi in range(-(-NT // 2)):
                    ts, got = pair_bank(f"cv{li}", gi)
                    emptied(v.scalar_tensor_tensor(g_nat[:, ts, :], got, 0.0, g_nat[:, ts, :], ALU.max, ALU.add))
                after(number[f"cv{li}", (12,)])
            do(v.tensor_tensor(x_nat, x_nat, g_nat, ALU.add))

            layernorm(2)
            v.wait_ge(gat_loaded, 32)
            for side in range(2):
                for j in range(JH):
                    do(v.tensor_tensor(attn_tmp[:, 0, :], gatw[:, j, 0:H], attn[:, side, :], ALU.mult))
                    do(v.tensor_reduce(gatw[:, j, H + side * HEADS:H + (side + 1) * HEADS],
                                       attn_tmp[:, 0, :].rearrange("p (h d) -> p h d", h=HEADS), AX_X, ALU.add))
            v.memset(stats[:, 0, 0:1], 0.0).then_inc(gat_w_ready, 1)
            copy_T("gT2", gT)
            v.wait_ge(edge_l, 16 * NT)
            v.wait_ge(edge_x, 16 * NT)
            v.wait_ge(xt_stored, 32)
            do(v.tensor_tensor(al[:, :, :], el[:, :, :], xt_edge[:, :, H + HEADS:XW], ALU.add))
            do(v.scalar_tensor_tensor(al[:, :, :], al[:, :, :], 0.01, al[:, :, :], ALU.mult, ALU.max))
            do(v.tensor_reduce(am[:, 0, :], al[:, :, :], AX_X, ALU.max))
            v.tensor_tensor(al[:, :, :], al[:, :, :], bcast(am[:, 0, :], HEADS), ALU.subtract).then_inc(exp_in, 1)
            v.wait_ge(exp_out, 1)
            do(v.tensor_reduce(am[:, 0, :], al[:, :, :], AX_X, ALU.add))
            do(v.reciprocal(am[:, 1, :], am[:, 0, :]))
            do(v.tensor_tensor(al[:, :, :], al[:, :, :], bcast(am[:, 1, :], HEADS), ALU.mult))
            for hd in range(HEADS):
                last = v.tensor_tensor(mix[:, :, hd * OC:(hd + 1) * OC], xt_edge[:, :, hd * OC:(hd + 1) * OC],
                                       al[:, :, hd:hd + 1].to_broadcast([P, NT, OC]), ALU.mult)
            do(last)
            do(v.tensor_tensor(mix[:, :, 0:2 * OC], mix[:, :, 0:2 * OC], mix[:, :, 2 * OC:H], ALU.add))
            do(v.tensor_tensor(mix[:, :, 0:OC], mix[:, :, 0:OC], mix[:, :, OC:2 * OC], ALU.add))
            for hd in range(HEADS):
                last = v.tensor_tensor(x_nat[:, :, hd * OC:(hd + 1) * OC], x_nat[:, :, hd * OC:(hd + 1) * OC],
                                       mix[:, :, 0:OC], ALU.add)
            do(last)

            layernorm(3)
            copy_T("gT3", gT)
            v.wait_ge(ln_out, 4 * NT)
            do(v.tensor_tensor(x_nat, x_nat, g_nat, ALU.add))
            for j in range(JH):
                for b in range(NB):
                    v.wait_ge(drained_a, nth[number["xi", (j, b)]])
                    bs = slice(b * BLK, (b + 1) * BLK)
                    last = v.scalar_tensor_tensor(xiT[:, j, bs], xiT[:, j, bs], 0.2, xiT[:, j, bs], ALU.mult, ALU.max)
            last.then_inc(xi_ready, 1)
            v.wait_ge(gat_loaded, 64)
            for gi in range(-(-NT // 2)):
                ts, got = pair_bank("xj", gi)
                n = ts.stop - ts.start
                emptied(v.tensor_tensor(xj_nat[:, ts, :], got, ab2row.unsqueeze(1).to_broadcast([P, n, H]), ALU.add))
            after(number["xj", (12,)])
            do(v.scalar_tensor_tensor(xj_nat, xj_nat, 0.2, xj_nat, ALU.mult, ALU.max))
            v.wait_ge(filled, number["a1", (NB - 1,)] + 1)
            do(v.tensor_tensor(xj_tmp, xj_nat, wa2row.unsqueeze(1).to_broadcast([P, NT, H]), ALU.mult))
            do(v.tensor_reduce(a2[:, :], xj_tmp, AX_X, ALU.add))
            v.tensor_scalar(a2[:, :], a2[:, :], epsc[:, 2:3], None, ALU.add).then_inc(xj_ready, 1)
            def drain_out(gi):
                b0, nb = GROUPS[gi]
                for j in range(JH):
                    for b in range(b0, b0 + nb):
                        bank = empty_bank(v, number["agg3", (b0, j, b)])
                        emptied(v.tensor_copy(oT[:, j, b * BLK:(b + 1) * BLK], bank[:, 0:BLK]))

            u = 0
            for gi, (b0, nb) in enumerate(GROUPS):
                for t in range(NT):
                    q = tile_seq(4, gi, t)
                    v.wait_ge(att_sig, u + 1)
                    v.wait_ge(ring_full[q % RING], 16 * (q // RING + 1))
                    v.tensor_tensor(att[u % 2][:, 0:nb * BLK], att[u % 2][:, 0:nb * BLK], ring[q % RING][:, 0:nb * BLK],
                                    ALU.mult).then_inc(att_ready, 1)
                    u += 1
                    if t == 1 and gi == 1:
                        drain_out(0)
            drain_out(1)
            v.memset(oT[:, :, LD:NP], 0.0).then_inc(out_t, 1)
            add_pairs("back3")
            v.memset(stats[:, 0, 0:1], 0.0).then_inc(out_ready, 1)


_INS = ['x', 'src', 'dst', 'edge_weight', 'L0_gnn_edge_rep', 'L0_gnn_W1', 'L0_gnn_g1', 'L0_gnn_b1', 'L0_gnn_W2a',
        'L0_gnn_g2a', 'L0_gnn_b2a', 'L0_gnn_W2b', 'L0_gnn_g2b', 'L0_gnn_b2b', 'L0_gnn_epsilon', 'L1_gnn_lin0_w',
        'L1_gnn_lin0_b', 'L1_gnn_conv_w', 'L2_gnn_weight', 'L2_gnn_attn_l', 'L2_gnn_attn_r', 'L3_gnn_W1',
        'L3_gnn_b1', 'L3_gnn_W2', 'L3_gnn_b2', 'L3_gnn_wa1', 'L3_gnn_ba1', 'L3_gnn_wa2', 'L3_gnn_ba2']


def kernel(**inputs):
    import numpy as _np
    import concourse.bacc as _bacc
    from concourse import mybir as _mybir
    from concourse.bass_utils import run_bass_kernel_spmd as _run

    nc = _bacc.Bacc("TRN2", target_bir_lowering=False, num_devices=1)
    arrays, args = {}, []
    for name in _INS:
        a = _np.ascontiguousarray(inputs[name])
        if a.ndim == 0:
            a = a.reshape(1)
        arrays[f"in_{name}_dram"] = a
        args.append(nc.dram_tensor(f"in_{name}_dram", a.shape, _mybir.dt.from_np(a.dtype), kind="ExternalInput").ap())
    args.append(nc.dram_tensor("out_0_dram", (N, H), F32, kind="ExternalOutput").ap())
    gnn_kernel(nc, *args)
    r = _run(nc, [arrays], core_ids=[0])
    return r.results[0]["out_0_dram"]
```

```python
from contextlib import ExitStack

import concourse.bass as bass
from concourse import mybir

ALU = mybir.AluOpType
ACT = mybir.ActivationFunctionType
F32 = mybir.dt.float32
I32 = mybir.dt.int32
AX_X = mybir.AxisListType.X

P = 128
N = 3125
E = 50000
H = 256
NT = -(-N // P)
NP = NT * P
LAST = N - (NT - 1) * P
BLK = 448
NB = -(-N // BLK)
LD = NB * BLK
JH = H // P
HALF = 7
CH = 392
ITER = CH // (2 * HALF)
NHALF = 2 * ITER
PER = -(-E // P)
LASTE = E - (P - 1) * PER
TC = CH + HALF
FIELDS = 7
BN_EPS = 1e-5
SPARE = NP * LD
MROWS = NP + P
COPIES = 3
HEADS = 4
OC = H // HEADS
XW = H + 2 * HEADS
GROUPS = ((0, 4), (4, 3))
RING = 3
RINGW = 4 * BLK
ALPHA = 0.9
VECS = (("g2a", 4), ("b2a", 4), ("g2b", 2), ("b2b", 2), ("lin0_b", 2), ("ab1", 2), ("wa1", 2))
V0 = {name: sum(n for _, n in VECS[:k]) for k, (name, _) in enumerate(VECS)}
LOADS = 6 + len(VECS) + 3
WP2 = 4
WTAIL = (CH - NHALF * WP2) // (2 * HALF)
assert WTAIL * 2 * HALF + NHALF * WP2 == CH
LAG = 3
NPAIR = -(-NT // 2)
LG = 5


def chain_per(c):
    return len([j for j in range(2 * HALF) if j % COPIES == c])


def chain_before(i, j):
    return chain_per(j % COPIES) * i + j // COPIES


def chain_total(c):
    return chain_per(c) * ITER


class Signal:

    def __init__(self, sem):
        self.sem, self.n, self.extra = sem, 0, 0

    def on(self, ins, by=1):
        ins.then_inc(self.sem, by)
        self.n += by
        return self.n + self.extra


def wait(eng, sem, value):
    if isinstance(value, int) and value <= 0:
        return
    eng.wait_ge(sem, value)


def loop(eng, count, body, signals=()):
    start = {s: s.n for s in signals}
    body(0)
    per = {s: s.n - start[s] for s in signals}
    with eng.Fori(1, count) as i:
        for s in signals:
            s.extra = per[s] * (i - 1)
        body(i)
    for s in signals:
        assert s.n == start[s] + 2 * per[s]
        s.extra = 0
        s.n = start[s] + per[s] * count


def psum_plan():
    tg = [(j, g) for j in range(JH) for g in range(-(-NT // 4))]
    pairs = [(g,) for g in range(-(-NT // 2))]
    dense = [(b0, j, b) for b0, nb in GROUPS for j in range(JH) for b in range(b0, b0 + nb)]
    plan = []

    def add(stage, keys, who):
        plan.extend((stage, k, who) for k in keys)

    add("hT", tg, "V")
    add("P", pairs, "A")
    add("erT", tg, "V")
    add("Q", pairs, "A")
    add("mean", [(0,), (1,)], "V")
    add("agg0", dense, "V")
    add("h2", [(j, b) for j in range(2 * JH) for b in range(NB)], "A")
    add("h3", [(j, b) for j in range(JH) for b in range(NB)], "A")
    add("back0", pairs, "V")
    add("gT1", tg, "V")
    add("x0", [(j, b) for j in range(JH) for b in range(NB)], "A")
    add("x0n", pairs, "V")
    add("dinv", [(g,) for g in range(-(-NT // 4))], "V")
    for li in range(3):
        add(f"agg1{li}", dense, "V")
        add(f"cv{li}", pairs, "V")
    add("gT2", tg, "V")
    add("xt", [(t,) for t in range(NT)], "A")
    add("gT3", tg, "V")
    add("xi", [(j, b) for j in range(JH) for b in range(NB)], "A")
    add("a1", [(b,) for b in range(NB)], "A")
    add("xj", pairs, "V")
    add("agg3", dense, "V")
    add("back3", pairs, "V")
    return plan


def gnn_kernel(nc, x, src, dst, edge_weight, edge_rep, W1, g1, b1, W2a, g2a, b2a, W2b, g2b, b2b,
               epsilon, lin0_w, lin0_b, conv_w, gat_w, attn_l, attn_r, aW1, ab1, aW2, ab2,
               wa1, ba1, wa2, ba2, out):
    plan = psum_plan()
    number = {(s, k): g for g, (s, k, _) in enumerate(plan)}
    nth, seen = [], {"A": 0, "V": 0}
    for _, _, who in plan:
        seen[who] += 1
        nth.append(seen[who])

    with ExitStack() as ctx:
        def sb(name, shape, dt=F32):
            return ctx.enter_context(nc.sbuf_tensor(name, shape, dt))

        def sem(name):
            return ctx.enter_context(nc.semaphore(name))

        ctx.enter_context(nc.allow_non_contiguous_dma(reason="channel vectors onto partitions"))

        counts = nc.dram_tensor("counts", (SPARE + P, 1), F32).ap()
        weights = nc.dram_tensor("weights", (SPARE + P, 1), F32).ap()
        tab_p = nc.dram_tensor("tab_p", (NP, H), F32).ap()
        tab_q = nc.dram_tensor("tab_q", (NP, H), F32).ap()
        zbuf = nc.dram_tensor("zbuf", (P, CH, H), F32).ap()
        msum = [nc.dram_tensor(f"msum{c}", (MROWS, H), F32).ap() for c in range(COPIES)]
        tab_x = nc.dram_tensor("tab_x", (NP, XW), F32).ap()
        tab_l = nc.dram_tensor("tab_l", (NP, HEADS), F32).ap()
        counts_rows = counts[0:SPARE].rearrange("(r c) o -> r (c o)", c=LD)
        weights_rows = weights[0:SPARE].rearrange("(r c) o -> r (c o)", c=LD)

        W_ = NT * H
        reg = sb("reg", [P, 6 * W_])

        def view(at, *dims):
            n = 1
            for d in dims:
                n *= d
            v = reg[:, at:at + n]
            if len(dims) == 1:
                return v
            if len(dims) == 2:
                return v.rearrange("p (a b) -> p a b", a=dims[0])
            return v.rearrange("p (a b c) -> p a b c", a=dims[0], b=dims[1])

        RA, RB, RC, RD, RE, RF = (k * W_ for k in range(6))
        x_nat = view(RA, NT, H)
        g_nat = view(RB, NT, H)
        gT = view(RC, JH, NP)
        ring_t = sb("ring", [P, RING * RINGW])
        ring = [ring_t[:, k * RINGW:(k + 1) * RINGW] for k in range(RING)]

        at = RD
        gp = view(at, 2 * HALF, H); at += 2 * HALF * H
        gq = view(at, 2 * HALF, H); at += 2 * HALF * H
        zz = view(at, 2 * HALF, 2 * H); at += 4 * HALF * H
        table = view(at, TC, FIELDS); at += TC * FIELDS
        midx = view(at, TC).bitcast(I32); at += TC
        g1row = view(at, H); at += H
        b1row = view(at, H); at += H
        arow = view(at, H); at += H
        brow = view(at, H); at += H
        assert at <= 6 * W_
        zin = view(RD, 2 * HALF, H)
        mo = view(RD + 2 * HALF * H, 2 * HALF, H)
        p_nat, er_nat, erT = view(RD, NT, H), view(RE, NT, H), view(RF, JH, NP)
        mean_row = view(RE + TC, H)
        tmp_i = view(RE, TC).bitcast(I32)
        zeros = ring_t[:, 0:LD]
        raw_src = ring_t[:, LD:LD + PER].bitcast(I32)
        raw_dst = ring_t[:, LD + PER:LD + 2 * PER].bitcast(I32)
        raw_w = ring_t[:, LD + 2 * PER:LD + 3 * PER]
        at = LD + 3 * PER
        eqm = [ring_t[:, at + k * P:at + (k + 1) * P] for k in range(HALF)]
        eqd = [ring_t[:, at + k * P:at + (k + 1) * P] for k in range(2)]; at += 2 * P
        eqp = [ring_t[:, at + k * P:at + (k + 1) * P] for k in range(2)]; at += 2 * P
        low = [ring_t[:, at + k * P:at + (k + 1) * P] for k in range(2)]; at += 2 * P
        junk = ring_t[:, at:at + P]; at += P
        assert at <= RING * RINGW
        uT, h2T, h3T = view(RD, JH, NP), view(RE, 2 * JH, NP), view(RD, JH, NP)
        xs, supT, x0T, dinv_row = view(RC, NT, H), view(RD, JH, NP), view(RE, JH, NP), view(RF, LD)
        xt_nat, xt_edge = view(RD, NT, XW), view(RD + NT * XW, NT, XW)
        mix = view(RD, NT, H)
        xiT, xj_nat, a1row = view(RD, JH, NP), view(RE, NT, H), view(RF, LD)
        att = [view(RD + k * RINGW, RINGW) for k in range(2)]
        xj_tmp, oT = view(RD, NT, H), view(RC, JH, NP)

        w1 = sb("w1", [P, 2 * JH, H])
        w2a = sb("w2a", [P, JH, 2 * H])
        w2b = sb("w2b", [P, 2 * JH, H])
        lin0 = sb("lin0", [P, JH, H])
        conv = sb("conv", [P, 3 * JH, H])
        gatw = sb("gatw", [P, JH, XW])
        w31 = sb("w31", [P, JH, H])
        w32 = sb("w32", [P, JH, H])
        attn = w1[:, 0:2, :]
        attn_tmp = w1[:, 2:4, :]
        ab2row, wa2row = w2b[:, 0, :], w2b[:, 1, :]
        conv_flat = conv[:, :, :].rearrange("p a b -> p (a b)")
        wval = conv_flat[:, 0:TC]
        wcell = conv_flat[:, TC:2 * TC].bitcast(I32)
        ident = sb("ident", [P, P])
        ones = sb("ones", [P, P])
        cols = sb("cols", [P, P])
        prior = sb("prior", [P, P])
        rank = sb("rank", [P, 4])
        vec = sb("vec", [P, 24])
        slot = sb("slot", [P, 2, HALF, FIELDS])
        pair_ix = sb("pair_ix", [P, 2 * HALF * 2], I32)
        cw = sb("cw", [P, 2, HALF, 2])
        high = sb("high", [P, 2, NT])
        first_p = sb("first_p", [P, 2, HALF])
        first_d = sb("first_d", [P, 2, HALF])
        vals = sb("vals", [P, 2 * HALF])
        cell_f = sb("cell_f", [P, 2, HALF, 2])
        cell_ix = sb("cell_ix", [P, 2 * HALF], I32)
        w_vals = sb("w_vals", [P, 2 * HALF])
        w_ix = sb("w_ix", [P, 2 * HALF], I32)
        mslot = sb("mslot", [P, 2, HALF])
        m_ix = sb("m_ix", [P, 2 * HALF], I32)
        stats = sb("stats", [P, 28, 6])
        mv = sb("mv", [P, NT, 2])
        sc = sb("sc", [P, 4, NT])
        dinv = sb("dinv", [P, NT])
        a2 = sb("a2", [P, NT])
        epsc = sb("epsc", [P, 4])
        i_src = sb("i_src", [P, NT], I32)
        i_dst = sb("i_dst", [P, NT], I32)
        el = sb("el", [P, NT, HEADS])
        al = sb("al", [P, NT, HEADS])
        am = sb("am", [P, 2, NT])

        ps = [ctx.enter_context(nc.psum_tensor(f"ps{k}", [P, 512], F32)) for k in range(8)]

        def row_slot(k):
            return ps[(0, 1, 5, 6)[k // 2]][:, (k % 2) * 2 * P:(k % 2 + 1) * 2 * P]

        def rows_value(n, k):
            return HALF * n + min(HALF, k // 2 * 2 + 2)

        sum_bank = (ps[2], ps[7])

        memset_done = sem("memset_done")
        consts_ready = sem("consts_ready")
        raw_ready = sem("raw_ready")
        x_loaded = sem("x_loaded")
        er_loaded = sem("er_loaded")
        w_loaded = sem("w_loaded")
        w1_loaded = sem("w1_loaded")
        zeroed_c, zeroed_w, conv_loaded = sem("zeroed_c"), sem("zeroed_w"), sem("conv_loaded")
        pool_slots = sem("pool_slots")
        filled, drained_v, drained_a = sem("filled"), sem("drained_v"), sem("drained_a")
        drained = {"V": drained_v, "A": drained_a}
        ln_var, ln_std, ln_scale, ln_out = sem("ln_var"), sem("ln_std"), sem("ln_scale"), sem("ln_out")
        centred, tables_stored = sem("centred"), sem("tables_stored")
        prep_done, rows_ready, eq_ready, cnt_done, cell_ready = (
            sem("prep_done"), sem("rows_ready"), sem("eq_ready"), sem("cnt_done"), sem("cell_ready"))
        z_ready, sq_ready, stat_done = sem("z_ready"), sem("sq_ready"), sem("stat_done")
        gathered = [sem(f"gathered{k}") for k in range(2 * HALF)]
        count_added, weight_added = sem("count_added"), sem("weight_added")
        z_stored = [sem(f"z_stored{h}") for h in range(2)]
        pool_go = sem("pool_go")
        bn_var, bn_std, edge_bn, deg_var, deg_std = (
            sem("bn_var"), sem("bn_std"), sem("edge_bn"), sem("deg_var"), sem("deg_std"))
        z_loaded = [sem(f"z_loaded{h}") for h in range(2)]
        affine, relu_done, m_rows, m_eq, m_sum, m_out, m_prep = (
            sem("affine"), sem("relu_done"), sem("m_rows"), sem("m_eq"), sem("m_sum"), sem("m_out"), sem("m_prep"))
        m_added = [sem(f"m_added{c}") for c in range(COPIES)]
        en_loaded, en_ready = sem("en_loaded"), sem("en_ready")
        ring_full = [sem(f"ring_full{k}") for k in range(RING)]
        ring_used, att_sig, att_ready, att_used = sem("ring_used"), sem("att_sig"), sem("att_ready"), sem("att_used")
        bnn_var, bnn_std, bnn_scale, bnn_relu = sem("bnn_var"), sem("bnn_std"), sem("bnn_scale"), sem("bnn_relu")
        xs_ready, sup_tail = sem("xs_ready"), sem("sup_tail")
        gat_w_ready, xt_stored, gi_ready, gat_loaded, edge_l, edge_x = (
            sem("gat_w_ready"), sem("xt_stored"), sem("gi_ready"), sem("gat_loaded"), sem("edge_l"), sem("edge_x"))
        gi_cleared = sem("gi_cleared")
        exp_in, exp_out = sem("exp_in"), sem("exp_out")
        late_rows, xi_ready, xj_ready, out_t, out_ready, stored = (
            sem("late_rows"), sem("xi_ready"), sem("xj_ready"), sem("out_t"), sem("out_ready"), sem("stored"))
        row_free, tail0 = sem("row_free"), sem("tail0")

        def nat(d, rows=NP):
            return d[0:(NT - 1) * P].rearrange("(t p) c -> p t c", p=P)

        def bcast(v, n):
            return v.unsqueeze(2).to_broadcast([v.shape[0], v.shape[1], n])

        def empty_bank(eng, g, also=()):
            eng.wait_ge(filled, g + 1)
            return ps[g % 8]

        def tiles_of(key, per):
            return range(key[-1] * per, min(NT, key[-1] * per + per))

        dense_last = {}
        passes = ["agg0", "agg10", "agg11", "agg12", "agg3"]
        for pi, name in enumerate(passes):
            for gi, (b0, nb) in enumerate(GROUPS):
                dense_last[pi, gi] = number[name, (b0, JH - 1, b0 + nb - 1)]

        def tile_seq(pi, gi, t):
            return (pi * 2 + gi) * NT + t

        def uses_before(q):
            return q + 1 - (q + 1) // NT

        FIRST3 = tile_seq(4, 0, 0)

        def wait_tile_used(eng, q):
            if q >= FIRST3:
                eng.wait_ge(att_ready, q - FIRST3 + 1)
            elif q % NT == NT - 1:
                eng.wait_ge(filled, dense_last[q // NT // 2, q // NT % 2] + 1)
            else:
                eng.wait_ge(ring_used, uses_before(q))

        block = ctx.enter_context(nc.Block())

        @block.sync
        def _(sp):
            sp.wait_ge(memset_done, 1)
            for dst_t, dram, s in ((x_nat, x, x_loaded), (er_nat, edge_rep[0:N], er_loaded)):
                sp.dma_start(dst_t[:, 0:NT - 1, :], nat(dram)).then_inc(s, 16)
                sp.dma_start(dst_t[0:48, NT - 1, :], dram[(NT - 1) * P:(NT - 1) * P + 48]).then_inc(s, 16)
                sp.dma_start(dst_t[48:LAST, NT - 1, :], dram[(NT - 1) * P + 48:N]).then_inc(s, 16)
                if s is x_loaded:
                    sp.dma_start(w1[:, :, :], W1.rearrange("(j p) n -> p j n", p=P)).then_inc(w1_loaded, 16)
            for raw, dram in ((raw_src, src), (raw_dst, dst), (raw_w, edge_weight)):
                sp.dma_start(raw[0:P - 1, :], dram[0:(P - 1) * PER].rearrange("(p c) -> p c", c=PER)).then_inc(raw_ready, 16)
                sp.dma_start(raw[P - 1:P, 0:LASTE], dram[(P - 1) * PER:E].unsqueeze(0)).then_inc(raw_ready, 16)
            sp.wait_ge(memset_done, 2)
            def zero_matrix(m, done):
                rows = m[0:SPARE].rearrange("(t p c) o -> p t (c o)", p=P, c=LD)
                for t in range(NT):
                    sp.dma_start(rows[:, t, :], zeros[:, :]).then_inc(done, 16)
                sp.dma_start(m[SPARE:SPARE + P], zeros[:, 0:1]).then_inc(done, 16)
            zero_matrix(counts, zeroed_c)
            for tab in (tab_p, tab_q):
                sp.dma_start(tab[N:NP], zeros[0:NP - N, 0:H]).then_inc(tables_stored, 16)
            for k, (tab, nat_t) in enumerate(((tab_p, p_nat), (tab_q, g_nat))):
                sp.wait_ge(centred, k + 1)
                sp.dma_start(nat(tab), nat_t[:, 0:NT - 1, :]).then_inc(tables_stored, 16)
                sp.dma_start(tab[(NT - 1) * P:(NT - 1) * P + 48], nat_t[0:48, NT - 1, :]).then_inc(tables_stored, 16)
                sp.dma_start(tab[(NT - 1) * P + 48:N], nat_t[48:LAST, NT - 1, :]).then_inc(tables_stored, 16)
            sp.wait_ge(row_free, 1)
            sp.dma_start(g1row, g1.unsqueeze(0).to_broadcast([P, H])).then_inc(late_rows, 16)
            sp.dma_start(b1row, b1.unsqueeze(0).to_broadcast([P, H])).then_inc(late_rows, 16)

            sp.dma_start(w2a[:, :, :], W2a.rearrange("(j p) n -> p j n", p=P)).then_inc(w_loaded, 16)
            sp.dma_start(w2b[:, :, :], W2b.rearrange("(j p) n -> p j n", p=P)).then_inc(w_loaded, 16)
            sp.dma_start(lin0[:, :, :], lin0_w.rearrange("(j p) n -> p j n", p=P)).then_inc(w_loaded, 16)
            sp.dma_start(gatw[:, :, 0:H], gat_w.rearrange("(j p) n -> p j n", p=P)).then_inc(w_loaded, 16)
            sp.dma_start(w31[:, :, :], aW1.rearrange("(j p) n -> p j n", p=P)).then_inc(w_loaded, 16)
            sp.dma_start(w32[:, :, :], aW2.rearrange("(j p) n -> p j n", p=P)).then_inc(w_loaded, 16)
            for (name, n), v in zip(VECS, (g2a, b2a, g2b, b2b, lin0_b, ab1, wa1)):
                o = V0[name]
                sp.dma_start(vec[:, o:o + n], v.rearrange("(j p) -> p j", p=P)).then_inc(w_loaded, 16)
            sp.dma_start(epsc[:, 0:1], epsilon.unsqueeze(0).to_broadcast([P, 1])).then_inc(w_loaded, 16)
            sp.dma_start(epsc[:, 1:2], ba1.unsqueeze(0).to_broadcast([P, 1])).then_inc(w_loaded, 16)
            sp.dma_start(epsc[:, 2:3], ba2.unsqueeze(0).to_broadcast([P, 1])).then_inc(w_loaded, 16)

            for m in msum:
                rows = m.rearrange("(p a) c -> p (a c)", p=P)
                width = MROWS * H // P // 4
                for a in range(4):
                    sp.dma_start(rows[:, a * width:(a + 1) * width], zeros[:, 0:width]).then_inc(zeroed_w, 16)
            zero_matrix(weights, zeroed_w)

            def store_z(i):
                for h in range(2):
                    n = 2 * i + h
                    wait(sp, z_ready, HALF * (n + 1))
                    sp.dma_start(zbuf[:, bass.ds(HALF * n, HALF), :],
                                 zz[:, h * HALF:(h + 1) * HALF, 0:H]).then_inc(z_stored[h], 16)
            loop(sp, ITER, store_z)

            for h in range(2):
                sp.wait_ge(z_stored[h], 16 * ITER)
            sp.wait_ge(stat_done, CH)
            sp.wait_ge(z_ready, CH)

            def load_z(i):
                for h in range(2):
                    n = 2 * i + h
                    wait(sp, m_sum, HALF * (n - 1) if isinstance(n, int) else HALF * (n - 1))
                    sp.dma_start(zin[:, h * HALF:(h + 1) * HALF, :],
                                 zbuf[:, bass.ds(HALF * n, HALF), :]).then_inc(z_loaded[h], 16)
            loop(sp, ITER, load_z)

            for c in range(COPIES):
                sp.wait_ge(m_added[c], 16 * chain_total(c))
            sp.wait_ge(m_eq, CH)
            sp.wait_ge(m_out, CH)
            for c, r in enumerate((RB, RE, RF)):
                sp.dma_start(view(r, NT, H), msum[c][0:NP].rearrange("(t p) c -> p t c", p=P)).then_inc(en_loaded, 16)

            def stream(pi):
                rows = counts_rows if pi in (0, 4) else weights_rows
                for gi, (b0, nb) in enumerate(GROUPS):
                    for t in range(NT):
                        q = tile_seq(pi, gi, t)
                        if q == 0:
                            sp.wait_ge(count_added, 16 * CH)
                            sp.wait_ge(m_sum, CH)
                        if pi == 1 and gi == 0 and t == 0:
                            sp.wait_ge(weight_added, 16 * CH)
                            sp.dma_start(conv[:, :, :], conv_w.rearrange("l (j p) n -> p (l j) n", p=P)).then_inc(conv_loaded, 16)
                        if q >= RING:
                            wait_tile_used(sp, q - RING)
                        sp.dma_start(ring[q % RING][:, 0:nb * BLK],
                                     rows[t * P:(t + 1) * P, b0 * BLK:(b0 + nb) * BLK]).then_inc(ring_full[q % RING], 16)

            for pi in range(4):
                stream(pi)
                if pi == 0:
                    sp.wait_ge(filled, number["Q", (12,)] + 1)
                    sp.dma_start(attn[:, 0, :], attn_l.rearrange("h d -> (h d)").unsqueeze(0).to_broadcast([P, H])).then_inc(gat_loaded, 16)
                    sp.dma_start(attn[:, 1, :], attn_r.rearrange("h d -> (h d)").unsqueeze(0).to_broadcast([P, H])).then_inc(gat_loaded, 16)
            sp.wait_ge(drained_a, nth[number["xt", (NT - 1,)]])
            sp.dma_start(tab_x.rearrange("(t p) c -> p t c", p=P), xt_nat).then_inc(xt_stored, 16)
            sp.dma_start(tab_l.rearrange("(t p) c -> p t c", p=P), xt_nat[:, :, H:H + HEADS]).then_inc(xt_stored, 16)
            sp.wait_ge(filled, number["h3", (JH - 1, NB - 1)] + 1)
            sp.dma_start(ab2row, ab2.unsqueeze(0).to_broadcast([P, H])).then_inc(gat_loaded, 16)
            sp.dma_start(wa2row, wa2.unsqueeze(0).to_broadcast([P, H])).then_inc(gat_loaded, 16)
            stream(4)
            sp.wait_ge(out_ready, 1)
            sp.dma_start(nat(out), x_nat[:, 0:NT - 1, :]).then_inc(stored, 16)
            sp.dma_start(out[(NT - 1) * P:(NT - 1) * P + 48], x_nat[0:48, NT - 1, :]).then_inc(stored, 16)
            sp.dma_start(out[(NT - 1) * P + 48:N], x_nat[48:LAST, NT - 1, :]).then_inc(stored, 16)
            sp.wait_ge(stored, 48)

        @block.gpsimd
        def _(pool):
            pool.memset(ident[:, :], 0.0).then_inc(consts_ready, 1)
            pool.memset(ones[:, :], 1.0).then_inc(consts_ready, 1)
            pool.wait_ge(consts_ready, 2)
            pool.affine_select(out=ident[:, :], in_=ident[:, :], compare_op=ALU.not_equal, fill=1.0,
                               base=0, pattern=[[-1, P]], channel_multiplier=1).then_inc(consts_ready, 1)
            pool.iota(cols[:, :], [[1, P]], base=0, channel_multiplier=0, allow_small_or_imprecise_dtypes=True).then_inc(consts_ready, 1)
            pool.affine_select(out=prior[:, :], in_=ones[:, :], compare_op=ALU.is_gt, fill=0.0,
                               base=0, pattern=[[-1, P]], channel_multiplier=1).then_inc(consts_ready, 1)
            pool.memset(rank[:, 0:1], 0.0).then_inc(consts_ready, 1)
            pool.iota(rank[:, 1:2], [[0, 1]], base=SPARE, channel_multiplier=1, allow_small_or_imprecise_dtypes=True).then_inc(consts_ready, 1)
            pool.iota(rank[:, 2:3], [[0, 1]], base=NP, channel_multiplier=1, allow_small_or_imprecise_dtypes=True).then_inc(consts_ready, 1)

            pool.wait_ge(tables_stored, 16 * 8)
            pool.wait_ge(zeroed_c, 16 * (NT + 1))

            def edges(i):
                for h in range(2):
                    n = 2 * i + h
                    wait(pool, prep_done, n + 1)
                    wait(pool, cell_ready, n + 1)
                    for k in range(HALF):
                        j = h * HALF + k
                        c = 2 * HALF * i + j
                        wait(pool, z_ready, c - 2 * HALF + 1)
                        pool.sem_inc(pool_go, 1)
                        for buf, tab, f in ((gp, tab_p, 0), (gq, tab_q, 1)):
                            pool.indirect_dma_start(
                                buf[:, j, :], None, tab,
                                bass.IndirectOffsetOnAxis(ap=pair_ix[:, 2 * j + f:2 * j + f + 1], axis=0),
                            ).then_inc(gathered[j], 16)
                        wait(pool, count_added, 16 * c)
                        pool.sem_inc(pool_go, 1)
                        pool.indirect_dma_start(
                            counts, bass.IndirectOffsetOnAxis(ap=cell_ix[:, j:j + 1], axis=0),
                            vals[:, j:j + 1], None, compute_op=ALU.add,
                        ).then_inc(count_added, 16)
            loop(pool, ITER, edges)

            slots = Signal(pool_slots)

            def weight_slots(o, w, n):
                pool.tensor_copy(w_vals[:, o:o + n], wval[:, bass.ds(w, n)])
                pool.wait_ge(slots.sem, slots.on(pool.tensor_copy(w_ix[:, o:o + n], wcell[:, bass.ds(w, n)])))

            def add_weights(o, w):
                wait(pool, weight_added, 16 * w)
                pool.sem_inc(pool_go, 1)
                pool.indirect_dma_start(
                    weights, bass.IndirectOffsetOnAxis(ap=w_ix[:, o:o + 1], axis=0),
                    w_vals[:, o:o + 1], None, compute_op=ALU.add,
                ).then_inc(weight_added, 16)

            pool.wait_ge(zeroed_w, 16 * (NT + 1 + 4 * COPIES))
            pool.wait_ge(cell_ready, NHALF + 1)

            def messages(i):
                for h in range(2):
                    n = 2 * i + h
                    for c in range(COPIES):
                        last = max(j for j in range((h + 1) * HALF) if j % COPIES == c)
                        wait(pool, m_added[c], 16 * (chain_before(i, last) + 1 - chain_per(c)))
                    wait(pool, weight_added, 16 * WP2 * (n - 1))
                    pool.sem_inc(pool_go, 1)
                    pool.tensor_copy(m_ix[:, h * HALF:(h + 1) * HALF], midx[:, bass.ds(HALF * n, HALF)])
                    weight_slots(h * HALF, WP2 * n, WP2)
                    for k in range(HALF):
                        j = h * HALF + k
                        wait(pool, m_out, 2 * HALF * i + j + 1)
                        wait(pool, m_added[j % COPIES], 16 * chain_before(i, j))
                        pool.sem_inc(pool_go, 1)
                        pool.indirect_dma_start(
                            msum[j % COPIES], bass.IndirectOffsetOnAxis(ap=m_ix[:, j:j + 1], axis=0),
                            mo[:, j, :], None, compute_op=ALU.add,
                        ).then_inc(m_added[j % COPIES], 16)
                        if k % 2 == 1 or k == HALF - 1:
                            add_weights(h * HALF + k // 2, WP2 * n + k // 2)
            loop(pool, ITER, messages, [slots])

            def tail(i):
                for h in range(2):
                    w = NHALF * WP2 + HALF * (2 * i + h)
                    pool.wait_ge(weight_added, 16 * (w - HALF))
                    pool.sem_inc(pool_go, 1)
                    weight_slots(h * HALF, w, HALF)
                    for k in range(HALF):
                        add_weights(h * HALF + k, w + k)
            loop(pool, WTAIL, tail, [slots])

            pool.memset(i_src[:, :], N).then_inc(gi_cleared, 1)
            pool.memset(i_dst[:, :], N).then_inc(gi_cleared, 1)
            pool.wait_ge(gi_cleared, 2)
            full = (NT - 1) * P
            for ix, dram in ((i_src, src), (i_dst, dst)):
                pool.dma_start(ix[:, 0:NT - 1], dram[0:full].rearrange("(t p) -> p t", p=P)).then_inc(gi_ready, 16)
                pool.dma_start(ix[0:LAST, NT - 1:NT], dram[full:N].unsqueeze(1)).then_inc(gi_ready, 16)
            pool.wait_ge(gi_ready, 64)
            pool.wait_ge(xt_stored, 32)
            for t in range(NT):
                pool.indirect_dma_start(el[:, t, :], None, tab_l,
                                        bass.IndirectOffsetOnAxis(ap=i_src[:, t:t + 1], axis=0)).then_inc(edge_l, 16)
                pool.indirect_dma_start(xt_edge[:, t, :], None, tab_x,
                                        bass.IndirectOffsetOnAxis(ap=i_dst[:, t:t + 1], axis=0)).then_inc(edge_x, 16)

        @block.scalar
        def _(act):
            act_step = Signal(ctx.enter_context(nc.semaphore("act_step")))

            def emptied(ins):
                ins.then_inc(drained_a, 1)

            def layernorm(k):
                def apply(q):
                    act.wait_ge(ln_scale, k * (NT // LG) + q + 1)
                    for t in range(q * LG, (q + 1) * LG):
                        act.activation(g_nat[:, t, :], x_nat[:, t, :], ACT.Relu, bias=sc[:, 3, t:t + 1],
                                       scale=sc[:, 2, t:t + 1]).then_inc(ln_out, 1)
                for q in range(NT // LG):
                    act.wait_ge(ln_var, k * (NT // LG) + q + 1)
                    ts = slice(q * LG, (q + 1) * LG)
                    act.activation(sc[:, 1, ts], sc[:, 0, ts], ACT.Sqrt).then_inc(ln_std, 1)
                    if q:
                        apply(q - 1)
                apply(NT // LG - 1)

            def copy_pairs(stage, dest):
                for g in range(-(-NT // 2)):
                    q = number[stage, (g,)]
                    bank = empty_bank(act, q)
                    ts = tiles_of((g,), 2)
                    emptied(act.activation(dest[:, ts[0]:ts[-1] + 1, :],
                                           bank[:, 0:len(ts) * H].rearrange("p (t c) -> p t c", c=H), ACT.Copy))

            layernorm(0)
            copy_pairs("P", p_nat)
            act.wait_ge(drained_v, nth[number["hT", (JH - 1, 6)]])
            copy_pairs("Q", g_nat)

            def squares(i):
                for h in range(2):
                    n = 2 * i + h
                    wait(act, stat_done, HALF * (n - 1))
                    for k in range(HALF):
                        j = h * HALF + k
                        wait(act, z_ready, 2 * HALF * i + j + 1)
                        act.activation(zz[:, j, H:2 * H], zz[:, j, 0:H], ACT.Square).then_inc(sq_ready, 1)
            loop(act, ITER, squares)
            act.wait_ge(bn_var, 1)
            act.activation(arow, arow, ACT.Sqrt).then_inc(bn_std, 1)
            act.wait_ge(deg_var, 1)
            act.activation(sc[:, 1, :], sc[:, 0, :], ACT.Sqrt).then_inc(deg_std, 1)

            def relu_half(n, h):
                wait(act, affine, n + 1)
                act.activation(zin[:, h * HALF:(h + 1) * HALF, :], zin[:, h * HALF:(h + 1) * HALF, :],
                               ACT.Relu).then_inc(relu_done, 1)

            def sums(i):
                for h in range(2):
                    n = 2 * i + h
                    for k in range(HALF):
                        j = h * HALF + k
                        c = 2 * HALF * i + j
                        wait(act, m_sum, c + 1)
                        wait(act, m_added[j % COPIES], 16 * (chain_before(i, j) + 1 - chain_per(j % COPIES)))
                        act.activation(mo[:, j, :], sum_bank[j % 2][:, 0:H], ACT.Copy).then_inc(m_out, 1)
                    if h == 0:
                        relu_half(n + 1, 1)
                    else:
                        relu_half(n + 1, 0)
            relu_half(0, 0)
            loop(act, ITER - 1, sums)
            i = ITER - 1
            for h in range(2):
                for k in range(HALF):
                    j = h * HALF + k
                    c = 2 * HALF * i + j
                    act.wait_ge(m_sum, c + 1)
                    act.wait_ge(m_added[j % COPIES], 16 * (chain_before(i, j) + 1 - chain_per(j % COPIES)))
                    act.activation(mo[:, j, :], sum_bank[j % 2][:, 0:H], ACT.Copy).then_inc(m_out, 1)
                if h == 0:
                    relu_half(NHALF - 1, 1)

            act.wait_ge(en_ready, 1)
            for stage, dest, nj in (("h2", h2T, 2 * JH), ("h3", h3T, JH)):
                if stage == "h3":
                    act.wait_ge(filled, number["h2", (2 * JH - 1, NB - 1)] + 1)
                for j in range(nj):
                    for b in range(NB):
                        bank = empty_bank(act, number[stage, (j, b)])
                        emptied(act.activation(dest[:, j, b * BLK:(b + 1) * BLK], bank[:, 0:BLK], ACT.Copy))
                r = 0 if stage == "h2" else 1
                act.wait_ge(bnn_var, r + 1)
                act.activation(sc[:, 1, 0:nj], sc[:, 0, 0:nj], ACT.Sqrt).then_inc(bnn_std, 1)
                act.wait_ge(bnn_scale, r + 1)
                for j in range(nj):
                    act.activation(dest[:, j, 0:LD], dest[:, j, 0:LD], ACT.Relu, bias=sc[:, 3, j:j + 1],
                                   scale=sc[:, 2, j:j + 1]).then_inc(bnn_relu, 1)

            layernorm(1)
            act.wait_ge(w_loaded, 16 * LOADS)
            act.wait_ge(bnn_relu, 3 * JH)
            act.wait_ge(filled, number["h3", (JH - 1, NB - 1)] + 1)
            for j in range(JH):
                for b in range(NB):
                    bank = empty_bank(act, number["x0", (j, b)])
                    emptied(act.activation(x0T[:, j, b * BLK:(b + 1) * BLK], bank[:, 0:BLK], ACT.Relu,
                                           bias=vec[:, V0["lin0_b"] + j:V0["lin0_b"] + j + 1]))

            layernorm(2)
            for t in range(NT):
                bank = empty_bank(act, number["xt", (t,)])
                emptied(act.activation(xt_nat[:, t, :], bank[:, 0:XW], ACT.Copy))
            act.wait_ge(exp_in, 1)
            act.activation(al[:, :, :], al[:, :, :], ACT.Exp).then_inc(exp_out, 1)

            layernorm(3)
            for j in range(JH):
                for b in range(NB):
                    bank = empty_bank(act, number["xi", (j, b)])
                    emptied(act.activation(xiT[:, j, b * BLK:(b + 1) * BLK], bank[:, 0:BLK], ACT.Identity,
                                           bias=vec[:, V0["ab1"] + j:V0["ab1"] + j + 1]))
            for b in range(NB):
                bank = empty_bank(act, number["a1", (b,)])
                emptied(act.activation(a1row[:, b * BLK:(b + 1) * BLK], bank[:, 0:BLK], ACT.Identity,
                                       bias=epsc[:, 1:2]))
            act.wait_ge(xj_ready, 1)
            act.wait_ge(drained_a, nth[number["a1", (NB - 1,)]])
            u = 0
            for b0, nb in GROUPS:
                for t in range(NT):
                    if u >= 2 and (u - 2) % NT == NT - 1:
                        act.wait_ge(filled, dense_last[4, (u - 2) // NT] + 1)
                    elif u >= 2:
                        act.wait_ge(att_used, uses_before(u - 2))
                    act.activation(att[u % 2][:, 0:nb * BLK], a1row[:, b0 * BLK:(b0 + nb) * BLK], ACT.Sigmoid,
                                   bias=a2[:, t:t + 1]).then_inc(att_sig, 1)
                    u += 1

        @block.tensor
        def _(pe):
            def open_bank(g):
                if g >= 8:
                    who = plan[g - 8][2]
                    pe.wait_ge(drained[who], nth[g - 8])
                return ps[g % 8]

            def to_T(stage, src_nat, done, base):
                for j in range(JH):
                    for gi in range(-(-NT // 4)):
                        bank = open_bank(number[stage, (j, gi)])
                        ts = tiles_of((gi,), 4)
                        for t in ts:
                            if done is not None:
                                pe.wait_ge(done, base + t + 1)
                            m = pe.transpose(bank[:, (t - ts[0]) * P:(t - ts[0] + 1) * P],
                                             src_nat[:, t, j * P:(j + 1) * P], ident[:, :])
                        m.then_inc(filled, 1)

            def node_rows(stage, lhs, rhs, width=H, per=2, nk=JH, base=0, block_ready=None):
                for gi in range(-(-NT // per)):
                    bank = open_bank(number[stage, (gi,)])
                    ts = tiles_of((gi,), per)
                    if block_ready:
                        wait_block(block_ready, min(NB - 1, ((ts[-1] + 1) * P - 1) // BLK))
                    for t in ts:
                        for k in range(nk):
                            m = pe.matmul(bank[:, (t - ts[0]) * width:(t - ts[0] + 1) * width],
                                          lhs[:, k, t * P:(t + 1) * P], rhs[:, base + k, :],
                                          start=(k == 0), stop=(k == nk - 1))
                    m.then_inc(filled, 1)

            def wait_block(name, b):
                for b0, nb in GROUPS:
                    if b0 <= b < b0 + nb:
                        pe.wait_ge(drained_v, nth[number[name, (b0, JH - 1, b)]])

            def node_cols(stage, w, rhs, nj, nk, ready=None, block_ready=None):
                for j in range(nj):
                    for b in range(NB):
                        bank = open_bank(number[stage, (j, b)])
                        if block_ready and j == 0:
                            wait_block(block_ready, b)
                        for k in range(nk):
                            if ready is not None and j == 0 and b == 0:
                                pe.wait_ge(*ready(k))
                            m = pe.matmul(bank[:, 0:BLK], w[:, k, j * P:(j + 1) * P], rhs[:, k, b * BLK:(b + 1) * BLK],
                                          start=(k == 0), stop=(k == nk - 1))
                        m.then_inc(filled, 1)

            def back(stage, src_T):
                for gi in range(-(-NT // 2)):
                    bank = open_bank(number[stage, (gi,)])
                    ts = tiles_of((gi,), 2)
                    for t in ts:
                        for j in range(JH):
                            o = (t - ts[0]) * H + j * P
                            m = pe.transpose(bank[:, o:o + P], src_T[:, j, t * P:(t + 1) * P], ident[:, :])
                    m.then_inc(filled, 1)

            def dense(pi, lhs, ready=None):
                name = passes[pi]
                for gi, (b0, nb) in enumerate(GROUPS):
                    for t in range(NT):
                        q = tile_seq(pi, gi, t)
                        u = q - FIRST3
                        if ready is not None and gi == 0:
                            pe.wait_ge(*ready(t))
                        if pi == 4:
                            pe.wait_ge(att_ready, u + 1)
                            rows = att[u % 2]
                        else:
                            pe.wait_ge(ring_full[q % RING], 16 * (q // RING + 1))
                            rows = ring[q % RING]
                        for j in range(JH):
                            for b in range(b0, b0 + nb):
                                g = number[name, (b0, j, b)]
                                bank = open_bank(g) if t == 0 else ps[g % 8]
                                m = pe.matmul(bank[:, 0:BLK], lhs[:, t, j * P:(j + 1) * P],
                                              rows[:, (b - b0) * BLK:(b - b0 + 1) * BLK],
                                              start=(t == 0), stop=(t == NT - 1))
                                if t == NT - 1:
                                    m.then_inc(filled, 1)
                        if t < NT - 1:
                            m.then_inc(att_used if pi == 4 else ring_used, 1)

            pe.wait_ge(consts_ready, 8)
            to_T("hT", g_nat, ln_out, 0)
            pe.wait_ge(w1_loaded, 16)
            pe.wait_ge(drained_v, nth[number["hT", (JH - 1, 6)]])
            node_rows("P", gT, w1)
            pe.wait_ge(er_loaded, 48)
            to_T("erT", er_nat, None, 0)
            pe.wait_ge(drained_v, nth[number["erT", (JH - 1, 6)]])
            node_rows("Q", erT, w1, base=JH)
            for k, nat_t in enumerate((p_nat, g_nat)):
                bank = open_bank(number["mean", (k,)])
                pe.wait_ge(drained_a, nth[number["P" if k == 0 else "Q", (12,)]])
                for t in range(NT):
                    m = pe.matmul(bank[:, 0:H], ones[:, :], nat_t[:, t, :], start=(t == 0), stop=(t == NT - 1))
                m.then_inc(filled, 1)
            g = number["mean", (1,)]
            pe.wait_ge(drained_v, nth[g])
            pe.wait_ge(drained_a, nth[number["Q", (12,)]])

            cnt_bank, deg_bank, stat_bank = ps[2], ps[3], ps[4]
            pe.wait_ge(memset_done, 3)
            pe.matmul(deg_bank[:, 0:NT], junk[:, :], ones[:, 0:NT], start=True, stop=False, skip_group_check=True)
            pe.matmul(stat_bank[:, :], junk[:, :], x_nat[:, 0:2, :], start=True, stop=False, skip_group_check=True)

            def chunk_rows(n, h, k):
                c = HALF * n + k
                if k == 0:
                    wait(pe, prep_done, n + 1)
                wait(pe, eq_ready, rows_value(n - 1, k))
                bank = row_slot(k)
                pe.matmul(bank[:, 0:P], slot[:, h, k, 0:1].to_broadcast([P, P]), ident[:, :], start=True, stop=True)
                pe.matmul(bank[:, P:2 * P], slot[:, h, k, 1:2].to_broadcast([P, P]), ident[:, :],
                          start=True, stop=True).then_inc(rows_ready, 1)

            def chunk_counts(n, h, k):
                c = HALF * n + k
                s = (h * HALF + k) % 2
                if k == 0:
                    wait(pe, cell_ready, n)
                wait(pe, eq_ready, c + 1)
                pe.matmul(cnt_bank[:, 2 * k:2 * k + 2], eqp[s], cw[:, h, k, :], start=True, stop=True,
                          skip_group_check=True)
                pe.matmul(deg_bank[:, 0:NT], low[s], high[:, s, :], start=False, stop=False,
                          skip_group_check=True).then_inc(cnt_done, 1)

            def chunk_stats(c, j):
                wait(pe, sq_ready, c + 1)
                pe.matmul(stat_bank[:, :], ones[:, :], zz[:, j, :], start=False, stop=False,
                          skip_group_check=True).then_inc(stat_done, 1)

            def rows_ahead(n, h, k):
                if k % 2 == 0:
                    for kk in range(0 if k == 0 else k + 2, min(k + 4, HALF)):
                        chunk_rows(n, h, kk)

            for k in range(HALF):
                rows_ahead(0, 0, k)
                chunk_counts(0, 0, k)

            def phase1(i):
                for h in range(2):
                    n = 2 * i + h
                    for k in range(HALF):
                        rows_ahead(n + 1, 1 - h, k)
                        chunk_counts(n + 1, 1 - h, k)
                        if k >= LAG:
                            chunk_stats(2 * HALF * i + h * HALF + k - LAG, h * HALF + k - LAG)
                    for k in range(HALF - LAG, HALF):
                        chunk_stats(2 * HALF * i + h * HALF + k, h * HALF + k)
            loop(pe, ITER, phase1)

            pe.wait_ge(bn_var, 1)
            pe.wait_ge(deg_var, 1)

            def phase2(i):
                for h in range(2):
                    n = 2 * i + h
                    for k in range(HALF):
                        j = h * HALF + k
                        c = 2 * HALF * i + j
                        if k == 0:
                            wait(pe, m_prep, n + 1)
                            for kk in range(HALF):
                                m_row(n, h, kk)
                            wait(pe, relu_done, n + 1)
                        wait(pe, m_eq, c + 1)
                        wait(pe, m_out, c - 1)
                        pe.matmul(sum_bank[j % 2][:, 0:H], eqm[k], zin[:, j, :], start=True, stop=True).then_inc(m_sum, 1)

            def m_row(n, h, k):
                wait(pe, m_eq, rows_value(n - 1, k))
                pe.matmul(row_slot(k)[:, 0:P], mslot[:, h, k:k + 1].to_broadcast([P, P]), ident[:, :],
                          start=True, stop=True).then_inc(m_rows, 1)
            loop(pe, ITER, phase2)

            pe.wait_ge(en_ready, 1)
            dense(0, g_nat)
            pe.wait_ge(w_loaded, 16 * LOADS)
            node_cols("h2", w2a, uT, 2 * JH, JH, block_ready="agg0")
            node_cols("h3", w2b, h2T, JH, 2 * JH, ready=lambda k: (bnn_relu, k + 1))
            pe.wait_ge(bnn_relu, 3 * JH)
            pe.wait_ge(tail0, 1)
            back("back0", h3T)

            to_T("gT1", g_nat, ln_out, NT)
            pe.wait_ge(drained_v, nth[number["gT1", (JH - 1, 6)]])
            node_cols("x0", lin0, gT, JH, JH)
            pe.wait_ge(drained_a, nth[number["x0", (JH - 1, NB - 1)]])
            pe.wait_ge(sup_tail, 1)
            back("x0n", x0T)
            for gi in range(-(-NT // 4)):
                bank = open_bank(number["dinv", (gi,)])
                ts = tiles_of((gi,), 4)
                for t in ts:
                    m = pe.matmul(bank[:, (t - ts[0]) * P:(t - ts[0] + 1) * P],
                                  dinv[:, t:t + 1].to_broadcast([P, P]), ident[:, :], start=True, stop=True)
                m.then_inc(filled, 1)
            for li in range(3):
                dense(1 + li, xs, lambda t: (xs_ready, li * NPAIR + t // 2 + 1))
                if li == 0:
                    pe.wait_ge(conv_loaded, 16)
                node_rows(f"cv{li}", supT, conv, base=li * JH, block_ready=f"agg1{li}")

            to_T("gT2", g_nat, ln_out, 2 * NT)
            pe.wait_ge(drained_v, nth[number["gT2", (JH - 1, 6)]])
            pe.wait_ge(gat_w_ready, 1)
            node_rows("xt", gT, gatw, width=XW, per=1)

            to_T("gT3", g_nat, ln_out, 3 * NT)
            pe.wait_ge(drained_v, nth[number["gT3", (JH - 1, 6)]])
            node_cols("xi", w31, gT, JH, JH)
            pe.wait_ge(xi_ready, 1)
            for b in range(NB):
                bank = open_bank(number["a1", (b,)])
                for k in range(JH):
                    m = pe.matmul(bank[:, 0:BLK], vec[:, V0["wa1"] + k:V0["wa1"] + k + 1].to_broadcast([P, P]),
                                  xiT[:, k, b * BLK:(b + 1) * BLK], start=(k == 0), stop=(k == JH - 1))
                m.then_inc(filled, 1)
            node_rows("xj", gT, w32)
            dense(4, xj_nat)
            pe.wait_ge(drained_v, nth[dense_last[4, 1]])
            pe.wait_ge(out_t, 1)
            back("back3", oT)

        @block.vector
        def _(v):
            step = Signal(ctx.enter_context(nc.semaphore("dve_step")))
            loop_signals = [step]

            def do(ins):
                v.wait_ge(step.sem, step.on(ins))

            def emptied(ins):
                ins.then_inc(drained_v, 1)

            def after(g):
                v.wait_ge(drained_v, nth[g])

            def layernorm(k, ready=lambda q: None):
                def scales(q):
                    ts = slice(q * LG, (q + 1) * LG)
                    v.wait_ge(ln_std, k * (NT // LG) + q + 1)
                    do(v.reciprocal(sc[:, 2, ts], sc[:, 1, ts]))
                    v.scalar_tensor_tensor(sc[:, 3, ts], mv[:, ts, 0], -1.0, sc[:, 2, ts], ALU.mult, ALU.mult).then_inc(ln_scale, 1)
                for q in range(NT // LG):
                    ready(q)
                    ts = slice(q * LG, (q + 1) * LG)
                    for t in range(q * LG, (q + 1) * LG):
                        last = v.bn_stats(stats[:, t, :], x_nat[:, t, :])
                    do(last)
                    for t in range(q * LG, (q + 1) * LG):
                        last = v.bn_aggr(mv[:, t, :], stats[:, t, :])
                    do(last)
                    v.tensor_scalar(sc[:, 0, ts], mv[:, ts, 1], BN_EPS, None, ALU.add).then_inc(ln_var, 1)
                    if q:
                        scales(q - 1)
                scales(NT // LG - 1)

            def copy_T(stage, dest):
                for j in range(JH):
                    for gi in range(-(-NT // 4)):
                        bank = empty_bank(v, number[stage, (j, gi)])
                        ts = tiles_of((gi,), 4)
                        emptied(v.tensor_copy(dest[:, j, ts[0] * P:(ts[-1] + 1) * P], bank[:, 0:len(ts) * P]))

            def pair_bank(stage, gi):
                bank = empty_bank(v, number[stage, (gi,)])
                ts = tiles_of((gi,), 2)
                return slice(ts[0], ts[-1] + 1), bank[:, 0:len(ts) * H].rearrange("p (t c) -> p t c", c=H)

            def add_pairs(stage):
                for gi in range(-(-NT // 2)):
                    ts, got = pair_bank(stage, gi)
                    emptied(v.tensor_tensor(x_nat[:, ts, :], x_nat[:, ts, :], got, ALU.add))
                after(number[stage, (12,)])

            v.memset(x_nat[:, NT - 1, :], 0.0)
            v.memset(er_nat[:, NT - 1, :], 0.0).then_inc(memset_done, 1)
            v.memset(zeros, 0.0).then_inc(memset_done, 1)
            v.memset(junk, 0.0).then_inc(memset_done, 1)
            v.wait_ge(x_loaded, 48)
            layernorm(0)
            copy_T("hT", gT)
            copy_T("erT", erT)
            for k, nat_t in enumerate((p_nat, g_nat)):
                bank = empty_bank(v, number["mean", (k,)])
                v.tensor_scalar(mean_row, bank[:, 0:H], 1.0 / N, None, ALU.mult).then_inc(drained_v, 1)
                after(number["mean", (k,)])
                v.tensor_tensor(nat_t, nat_t, mean_row.unsqueeze(1).to_broadcast([P, NT, H]), ALU.subtract).then_inc(centred, 1)
                v.wait_ge(centred, k + 1)

            v.wait_ge(raw_ready, 96)
            v.wait_ge(filled, number["Q", (12,)] + 1)
            do(v.memset(table[:, :, 0:2], float(N)))
            do(v.memset(table[:, :, 2:3], 0.0))
            do(v.memset(table[:, :, 3:FIELDS], 0.0))
            for f, raw in ((0, raw_src), (1, raw_dst), (2, raw_w)):
                for prt, n, o in ((slice(0, P), LASTE, 0), (slice(0, 96), PER - LASTE, LASTE),
                                  (slice(96, P - 1), PER - LASTE, LASTE)):
                    do(v.tensor_copy(table[prt, o:o + n, f], raw[prt, o:o + n]))
            do(v.tensor_copy(tmp_i, table[:, :, 1]))
            do(v.tensor_scalar(tmp_i, tmp_i, 7, None, ALU.arith_shift_right))
            do(v.tensor_copy(table[:, :, 4], tmp_i))
            do(v.scalar_tensor_tensor(table[:, :, 3], table[:, :, 4], -float(P), table[:, :, 1], ALU.mult, ALU.add))
            v.wait_ge(consts_ready, 8)
            for f, hi, lo in ((5, 1, 0), (6, 0, 1)):
                do(v.scalar_tensor_tensor(table[:, :, f], table[:, :, hi], float(LD), table[:, :, lo], ALU.mult, ALU.add))
                do(v.tensor_scalar(table[:, :, f], table[:, :, f], rank[:, 1:2], None, ALU.subtract))
            do(v.memset(cw[:, :, :, 0:1], 1.0))
            v.memset(stats[:, 0, 0:1], 0.0).then_inc(row_free, 1)

            def prep(n, h):
                wait(v, cnt_done, HALF * (n - 1))
                cs = bass.ds(HALF * n, HALF)
                do(v.tensor_copy(slot[:, h], table[:, cs, :]))
                v.tensor_copy(cw[:, h, :, 1], slot[:, h, :, 2])
                v.tensor_copy(pair_ix[:, 2 * h * HALF:2 * (h + 1) * HALF].rearrange("p (k f) -> p k f", f=2),
                              slot[:, h, :, 0:2]).then_inc(prep_done, 1)

            def equal(n, h, k):
                c = HALF * n + k
                s = (h * HALF + k) % 2
                bank = row_slot(k)
                wait(v, rows_ready, rows_value(n, k))
                wait(v, cnt_done, c - 1)
                sd = step.on(v.tensor_scalar(eqd[s], bank[:, P:2 * P], slot[:, h, k, 1:2], None, ALU.is_equal))
                v.tensor_scalar(low[s], cols[:, :], slot[:, h, k, 3:4], slot[:, h, k, 2:3], ALU.is_equal, ALU.mult)
                v.tensor_scalar(high[:, s, :], cols[:, 0:NT], slot[:, h, k, 4:5], None, ALU.is_equal)
                v.wait_ge(step.sem, sd)
                v.scalar_tensor_tensor(eqp[s], bank[:, 0:P], slot[:, h, k, 0:1], eqd[s], ALU.is_equal,
                                       ALU.mult).then_inc(eq_ready, 1)
                do(v.tensor_tensor_reduce(junk, eqd[s], prior[:, :], 1.0, 0.0, ALU.mult, ALU.add, first_d[:, h, k:k + 1]))
                wait(v, eq_ready, c + 1)
                do(v.tensor_tensor_reduce(junk, eqp[s], prior[:, :], 1.0, 0.0, ALU.mult, ALU.add, first_p[:, h, k:k + 1]))

            def cells(n, h):
                cs = bass.ds(HALF * n, HALF)
                wait(v, cnt_done, HALF * (n + 1))
                wait(v, count_added, 16 * HALF * (n - 1))
                got = ps[2][:, 0:2 * HALF].rearrange("p (k f) -> p k f", f=2)
                v.tensor_copy(vals[:, h * HALF:(h + 1) * HALF], got[:, :, 0])
                v.tensor_copy(wval[:, cs], got[:, :, 1])
                v.tensor_scalar(first_p[:, h, :], first_p[:, h, :], 0.0, None, ALU.is_equal)
                v.tensor_scalar(mslot[:, h, :], slot[:, h, :, 1], rank[:, 2:3], None, ALU.subtract)
                do(v.tensor_scalar(first_d[:, h, :], first_d[:, h, :], 0.0, None, ALU.is_equal))
                v.tensor_tensor(mslot[:, h, :], mslot[:, h, :], first_d[:, h, :], ALU.mult)
                v.tensor_tensor(cell_f[:, h, :, 0], slot[:, h, :, 5], first_p[:, h, :], ALU.mult)
                do(v.tensor_tensor(cell_f[:, h, :, 1], slot[:, h, :, 6], first_p[:, h, :], ALU.mult))
                v.tensor_scalar(midx[:, cs], mslot[:, h, :], rank[:, 2:3], None, ALU.add)
                v.tensor_scalar(wcell[:, cs], cell_f[:, h, :, 1], rank[:, 1:2], None, ALU.add)
                v.tensor_scalar(cell_ix[:, h * HALF:(h + 1) * HALF], cell_f[:, h, :, 0],
                                rank[:, 1:2], None, ALU.add).then_inc(cell_ready, 1)

            def add_z(i, h, k):
                j = h * HALF + k
                n = 2 * i + h
                wait(v, gathered[j], 32 * (i + 1))
                if k == 0:
                    wait(v, z_stored[h], 16 * i)
                    wait(v, stat_done, HALF * (n - 1))
                v.tensor_tensor(zz[:, j, 0:H], gp[:, j, :], gq[:, j, :], ALU.add).then_inc(z_ready, 1)

            prep(0, 0)
            for k in range(HALF):
                equal(0, 0, k)
            cells(0, 0)

            def phase1(i):
                for h in range(2):
                    n = 2 * i + h
                    prep(n + 1, 1 - h)
                    for k in range(HALF):
                        equal(n + 1, 1 - h, k)
                        if k >= LAG:
                            add_z(i, h, k - LAG)
                    cells(n + 1, 1 - h)
                    for k in range(HALF - LAG, HALF):
                        add_z(i, h, k)
            loop(v, ITER, phase1, loop_signals)

            v.wait_ge(stat_done, CH)
            v.wait_ge(late_rows, 32)
            v.wait_ge(cell_ready, NHALF + 1)
            do(v.tensor_scalar(brow, ps[4][:, 0:H], 1.0 / E, None, ALU.mult))
            do(v.tensor_tensor(arow, brow, brow, ALU.mult))
            do(v.scalar_tensor_tensor(arow, ps[4][:, H:2 * H], 1.0 / E, arow, ALU.mult, ALU.subtract))
            do(v.tensor_scalar(arow, arow, 0.0, None, ALU.max))
            v.tensor_scalar(arow, arow, BN_EPS, None, ALU.add).then_inc(bn_var, 1)
            v.wait_ge(cnt_done, HALF * (NHALF + 1))
            do(v.tensor_scalar(dinv[:, :], ps[3][:, 0:NT], 0.0, None, ALU.is_gt))
            do(v.tensor_tensor(sc[:, 2, :], ps[3][:, 0:NT], dinv[:, :], ALU.mult))
            do(v.tensor_tensor(sc[:, 2, :], sc[:, 2, :], dinv[:, :], ALU.subtract))
            v.tensor_scalar(sc[:, 0, :], sc[:, 2, :], 1.0, None, ALU.add).then_inc(deg_var, 1)
            v.wait_ge(bn_std, 1)
            do(v.reciprocal(arow, arow))
            do(v.tensor_tensor(arow, arow, g1row, ALU.mult))
            do(v.tensor_tensor(brow, brow, arow, ALU.mult))
            do(v.tensor_tensor(brow, b1row, brow, ALU.subtract))
            v.wait_ge(deg_std, 1)
            do(v.reciprocal(sc[:, 2, :], sc[:, 1, :]))
            do(v.tensor_tensor(dinv[:, :], dinv[:, :], sc[:, 2, :], ALU.mult))

            def m_half(n, h, i_of):
                wait(v, m_sum, HALF * (n - 1))
                v.tensor_copy(mslot[:, h, :], table[:, bass.ds(HALF * n, HALF), 1]).then_inc(m_prep, 1)
                hs = slice(h * HALF, (h + 1) * HALF)
                wait(v, z_loaded[h], 16 * (i_of + 1))
                do(v.tensor_tensor(zin[:, hs, :], zin[:, hs, :], arow.unsqueeze(1).to_broadcast([P, HALF, H]), ALU.mult))
                v.tensor_tensor(zin[:, hs, :], zin[:, hs, :], brow.unsqueeze(1).to_broadcast([P, HALF, H]),
                                ALU.add).then_inc(affine, 1)

            def m_equal(i, h):
                for k in range(HALF):
                    j = h * HALF + k
                    c = 2 * HALF * i + j
                    wait(v, m_rows, rows_value(2 * i + h, k))
                    wait(v, m_sum, c - HALF + 1)
                    v.tensor_scalar(eqm[k], row_slot(k)[:, 0:P], mslot[:, h, k:k + 1], None, ALU.is_equal).then_inc(m_eq, 1)

            m_half(0, 0, 0)

            def phase2(i):
                m_equal(i, 0)
                m_half(2 * i + 1, 1, i)
                m_equal(i, 1)
                m_half(2 * i + 2, 0, i + 1)
            loop(v, ITER - 1, phase2, loop_signals)
            m_equal(ITER - 1, 0)
            m_half(NHALF - 1, 1, ITER - 1)
            m_equal(ITER - 1, 1)

            v.wait_ge(en_loaded, 48)
            do(v.tensor_tensor(g_nat, g_nat, view(RE, NT, H), ALU.add))
            v.tensor_tensor(g_nat, g_nat, view(RF, NT, H), ALU.add).then_inc(en_ready, 1)
            v.wait_ge(w_loaded, 16 * LOADS)
            do(v.tensor_scalar(epsc[:, 3:4], epsc[:, 0:1], 1.0, None, ALU.add))
            for b0, nb in GROUPS:
                for j in range(JH):
                    for b in range(b0, b0 + nb):
                        bank = empty_bank(v, number["agg0", (b0, j, b)])
                        bs = slice(b * BLK, (b + 1) * BLK)
                        emptied(v.scalar_tensor_tensor(uT[:, j, bs], gT[:, j, bs], epsc[:, 3:4], bank[:, 0:BLK],
                                                       ALU.mult, ALU.add))
            for r, (stage, src_T, nj, gam, bet) in enumerate((("h2", h2T, 2 * JH, "g2a", "b2a"), ("h3", h3T, JH, "g2b", "b2b"))):
                for j in range(nj):
                    for b in range(NB):
                        v.wait_ge(drained_a, nth[number[stage, (j, b)]])
                        last = v.bn_stats(stats[:, j * NB + b, :], src_T[:, j, b * BLK:min(N, (b + 1) * BLK)])
                do(last)
                for j in range(nj):
                    last = v.bn_aggr(mv[:, j, :], stats[:, j * NB:(j + 1) * NB, :])
                do(last)
                v.tensor_scalar(sc[:, 0, 0:nj], mv[:, 0:nj, 1], BN_EPS, None, ALU.add).then_inc(bnn_var, 1)
                v.wait_ge(bnn_std, r + 1)
                do(v.reciprocal(sc[:, 2, 0:nj], sc[:, 1, 0:nj]))
                do(v.tensor_tensor(sc[:, 2, 0:nj], sc[:, 2, 0:nj], vec[:, V0[gam]:V0[gam] + nj], ALU.mult))
                do(v.tensor_tensor(sc[:, 3, 0:nj], mv[:, 0:nj, 0], sc[:, 2, 0:nj], ALU.mult))
                v.tensor_tensor(sc[:, 3, 0:nj], vec[:, V0[bet]:V0[bet] + nj], sc[:, 3, 0:nj], ALU.subtract).then_inc(bnn_scale, 1)
            v.memset(h3T[:, :, LD:NP], 0.0).then_inc(tail0, 1)
            add_pairs("back0")

            layernorm(1)
            copy_T("gT1", gT)
            v.wait_ge(filled, number["h3", (JH - 1, NB - 1)] + 1)
            v.memset(x0T[:, :, LD:NP], 0.0)
            v.memset(supT[:, :, LD:NP], 0.0).then_inc(sup_tail, 1)
            for gi in range(-(-NT // 2)):
                ts, got = pair_bank("x0n", gi)
                emptied(v.tensor_copy(g_nat[:, ts, :], got))
            for gi in range(-(-NT // 4)):
                bank = empty_bank(v, number["dinv", (gi,)])
                o = gi * 4 * P
                n = min(4 * P, LD - o)
                emptied(v.tensor_scalar(dinv_row[:, o:o + n], bank[:, 0:n], 1.0 - ALPHA, None, ALU.mult))
            after(number["dinv", (6,)])
            def scale_pair(gi):
                ts = slice(2 * gi, min(NT, 2 * gi + 2))
                v.tensor_tensor(xs[:, ts, :], g_nat[:, ts, :], bcast(dinv[:, ts], H), ALU.mult).then_inc(xs_ready, 1)

            v.wait_ge(filled, number["x0", (JH - 1, NB - 1)] + 1)
            for gi in range(NPAIR):
                scale_pair(gi)
            for li in range(3):
                for b0, nb in GROUPS:
                    for j in range(JH):
                        for b in range(b0, b0 + nb):
                            bank = empty_bank(v, number[f"agg1{li}", (b0, j, b)])
                            bs = slice(b * BLK, (b + 1) * BLK)
                            do(v.tensor_tensor(supT[:, j, bs], bank[:, 0:BLK], dinv_row[:, bs], ALU.mult))
                            emptied(v.scalar_tensor_tensor(supT[:, j, bs], x0T[:, j, bs], ALPHA, supT[:, j, bs],
                                                           ALU.mult, ALU.add))
                for gi in range(-(-NT // 2)):
                    ts, got = pair_bank(f"cv{li}", gi)
                    emptied(v.scalar_tensor_tensor(g_nat[:, ts, :], got, 0.0, g_nat[:, ts, :], ALU.max, ALU.add))
                    if li < 2:
                        after(number[f"cv{li}", (gi,)])
                        scale_pair(gi)
                after(number[f"cv{li}", (12,)])
            do(v.tensor_tensor(x_nat, x_nat, g_nat, ALU.add))

            layernorm(2)
            v.wait_ge(gat_loaded, 32)
            for side in range(2):
                for j in range(JH):
                    do(v.tensor_tensor(attn_tmp[:, 0, :], gatw[:, j, 0:H], attn[:, side, :], ALU.mult))
                    do(v.tensor_reduce(gatw[:, j, H + side * HEADS:H + (side + 1) * HEADS],
                                       attn_tmp[:, 0, :].rearrange("p (h d) -> p h d", h=HEADS), AX_X, ALU.add))
            v.memset(stats[:, 0, 0:1], 0.0).then_inc(gat_w_ready, 1)
            copy_T("gT2", gT)
            v.wait_ge(edge_l, 16 * NT)
            v.wait_ge(edge_x, 16 * NT)
            v.wait_ge(xt_stored, 32)
            do(v.tensor_tensor(al[:, :, :], el[:, :, :], xt_edge[:, :, H + HEADS:XW], ALU.add))
            do(v.scalar_tensor_tensor(al[:, :, :], al[:, :, :], 0.01, al[:, :, :], ALU.mult, ALU.max))
            do(v.tensor_reduce(am[:, 0, :], al[:, :, :], AX_X, ALU.max))
            v.tensor_tensor(al[:, :, :], al[:, :, :], bcast(am[:, 0, :], HEADS), ALU.subtract).then_inc(exp_in, 1)
            v.wait_ge(exp_out, 1)
            do(v.tensor_reduce(am[:, 0, :], al[:, :, :], AX_X, ALU.add))
            do(v.reciprocal(am[:, 1, :], am[:, 0, :]))
            do(v.tensor_tensor(al[:, :, :], al[:, :, :], bcast(am[:, 1, :], HEADS), ALU.mult))
            for hd in range(HEADS):
                last = v.tensor_tensor(mix[:, :, hd * OC:(hd + 1) * OC], xt_edge[:, :, hd * OC:(hd + 1) * OC],
                                       al[:, :, hd:hd + 1].to_broadcast([P, NT, OC]), ALU.mult)
            do(last)
            do(v.tensor_tensor(mix[:, :, 0:2 * OC], mix[:, :, 0:2 * OC], mix[:, :, 2 * OC:H], ALU.add))
            do(v.tensor_tensor(mix[:, :, 0:OC], mix[:, :, 0:OC], mix[:, :, OC:2 * OC], ALU.add))
            for hd in range(HEADS):
                last = v.tensor_tensor(x_nat[:, :, hd * OC:(hd + 1) * OC], x_nat[:, :, hd * OC:(hd + 1) * OC],
                                       mix[:, :, 0:OC], ALU.add)
            do(last)

            layernorm(3)
            copy_T("gT3", gT)
            v.wait_ge(ln_out, 4 * NT)
            do(v.tensor_tensor(x_nat, x_nat, g_nat, ALU.add))
            for j in range(JH):
                for b in range(NB):
                    v.wait_ge(drained_a, nth[number["xi", (j, b)]])
                    bs = slice(b * BLK, (b + 1) * BLK)
                    last = v.scalar_tensor_tensor(xiT[:, j, bs], xiT[:, j, bs], 0.2, xiT[:, j, bs], ALU.mult, ALU.max)
            last.then_inc(xi_ready, 1)
            v.wait_ge(gat_loaded, 64)
            for gi in range(-(-NT // 2)):
                ts, got = pair_bank("xj", gi)
                n = ts.stop - ts.start
                emptied(v.tensor_tensor(xj_nat[:, ts, :], got, ab2row.unsqueeze(1).to_broadcast([P, n, H]), ALU.add))
            after(number["xj", (12,)])
            do(v.scalar_tensor_tensor(xj_nat, xj_nat, 0.2, xj_nat, ALU.mult, ALU.max))
            v.wait_ge(filled, number["a1", (NB - 1,)] + 1)
            do(v.tensor_tensor(xj_tmp, xj_nat, wa2row.unsqueeze(1).to_broadcast([P, NT, H]), ALU.mult))
            do(v.tensor_reduce(a2[:, :], xj_tmp, AX_X, ALU.add))
            v.tensor_scalar(a2[:, :], a2[:, :], epsc[:, 2:3], None, ALU.add).then_inc(xj_ready, 1)
            def drain_out(gi):
                b0, nb = GROUPS[gi]
                for j in range(JH):
                    for b in range(b0, b0 + nb):
                        bank = empty_bank(v, number["agg3", (b0, j, b)])
                        emptied(v.tensor_copy(oT[:, j, b * BLK:(b + 1) * BLK], bank[:, 0:BLK]))

            u = 0
            for gi, (b0, nb) in enumerate(GROUPS):
                for t in range(NT):
                    q = tile_seq(4, gi, t)
                    v.wait_ge(att_sig, u + 1)
                    v.wait_ge(ring_full[q % RING], 16 * (q // RING + 1))
                    v.tensor_tensor(att[u % 2][:, 0:nb * BLK], att[u % 2][:, 0:nb * BLK], ring[q % RING][:, 0:nb * BLK],
                                    ALU.mult).then_inc(att_ready, 1)
                    u += 1
                    if t == 1 and gi == 1:
                        drain_out(0)
            drain_out(1)
            v.memset(oT[:, :, LD:NP], 0.0).then_inc(out_t, 1)
            add_pairs("back3")
            v.memset(stats[:, 0, 0:1], 0.0).then_inc(out_ready, 1)


_INS = ['x', 'src', 'dst', 'edge_weight', 'L0_gnn_edge_rep', 'L0_gnn_W1', 'L0_gnn_g1', 'L0_gnn_b1', 'L0_gnn_W2a',
        'L0_gnn_g2a', 'L0_gnn_b2a', 'L0_gnn_W2b', 'L0_gnn_g2b', 'L0_gnn_b2b', 'L0_gnn_epsilon', 'L1_gnn_lin0_w',
        'L1_gnn_lin0_b', 'L1_gnn_conv_w', 'L2_gnn_weight', 'L2_gnn_attn_l', 'L2_gnn_attn_r', 'L3_gnn_W1',
        'L3_gnn_b1', 'L3_gnn_W2', 'L3_gnn_b2', 'L3_gnn_wa1', 'L3_gnn_ba1', 'L3_gnn_wa2', 'L3_gnn_ba2']


def kernel(**inputs):
    import numpy as _np
    import concourse.bacc as _bacc
    from concourse import mybir as _mybir
    from concourse.bass_utils import run_bass_kernel_spmd as _run

    nc = _bacc.Bacc("TRN2", target_bir_lowering=False, num_devices=1)
    arrays, args = {}, []
    for name in _INS:
        a = _np.ascontiguousarray(inputs[name])
        if a.ndim == 0:
            a = a.reshape(1)
        arrays[f"in_{name}_dram"] = a
        args.append(nc.dram_tensor(f"in_{name}_dram", a.shape, _mybir.dt.from_np(a.dtype), kind="ExternalInput").ap())
    args.append(nc.dram_tensor("out_0_dram", (N, H), F32, kind="ExternalOutput").ap())
    gnn_kernel(nc, *args)
    r = _run(nc, [arrays], core_ids=[0])
    return r.results[0]["out_0_dram"]
```

```python
from contextlib import ExitStack

import concourse.bass as bass
from concourse import mybir

ALU = mybir.AluOpType
ACT = mybir.ActivationFunctionType
F32 = mybir.dt.float32
F32R = mybir.dt.float32r
I32 = mybir.dt.int32
AX_X = mybir.AxisListType.X

P = 128
N = 3125
E = 50000
H = 256
NT = -(-N // P)
NP = NT * P
LAST = N - (NT - 1) * P
BLK = 448
NB = -(-N // BLK)
LD = NB * BLK
JH = H // P
HALF = 7
CH = 392
ITER = CH // (2 * HALF)
NHALF = 2 * ITER
PER = -(-E // P)
LASTE = E - (P - 1) * PER
TC = CH + HALF
FIELDS = 7
BN_EPS = 1e-5
SPARE = NP * LD
MROWS = ITER * P
assert MROWS >= NP + P
ZW = NP * LD // (ITER * P)
assert ZW * ITER * P == NP * LD and ZW <= LD
COPIES = 3
HEADS = 4
OC = H // HEADS
XW = H + 2 * HEADS
GROUPS = ((0, 4), (4, 3))
UW = 2 * BLK
RING = 6
ROWS = 4
ALPHA = 0.9
VECS = (("g2a", 4), ("b2a", 4), ("g2b", 2), ("b2b", 2), ("lin0_b", 2), ("ab1", 2), ("wa1", 2))
V0 = {name: sum(n for _, n in VECS[:k]) for k, (name, _) in enumerate(VECS)}
LOADS = 6 + len(VECS) + 3
EXTRA = ((0, 2, 3, 5, 6), (1, 3, 4, 6))
WP2 = len(EXTRA[0]) + len(EXTRA[1])
WPRE = HALF
WTAIL = (CH - WPRE - ITER * WP2) // HALF
assert WTAIL * HALF + WPRE + ITER * WP2 == CH and WTAIL % 2 == 1
LAG = 3
NPAIR = -(-NT // 2)
OUTT = 8
assert (NT - 1) % OUTT == 0
LG = 5
AHEAD = 1
DRAIN_AT = 3
NSPLIT = NT // LG


def chain_per(c):
    return len([j for j in range(2 * HALF) if j % COPIES == c])


def chain_before(i, j):
    return chain_per(j % COPIES) * i + j // COPIES


def chain_total(c):
    return chain_per(c) * ITER


class Signal:

    def __init__(self, sem):
        self.sem, self.n, self.extra = sem, 0, 0

    def on(self, ins, by=1):
        ins.then_inc(self.sem, by)
        self.n += by
        return self.n + self.extra


def wait(eng, sem, value):
    if isinstance(value, int) and value <= 0:
        return
    eng.wait_ge(sem, value)


def loop(eng, count, body, signals=()):
    start = {s: s.n for s in signals}
    body(0)
    per = {s: s.n - start[s] for s in signals}
    with eng.Fori(1, count) as i:
        for s in signals:
            s.extra = per[s] * (i - 1)
        body(i)
    for s in signals:
        assert s.n == start[s] + 2 * per[s]
        s.extra = 0
        s.n = start[s] + per[s] * count


def unit_blocks(gi, h):
    b0, nb = GROUPS[gi]
    return range(b0 + 2 * h, min(b0 + nb, b0 + 2 * h + 2))


def unit_keys(gi, h):
    return [(GROUPS[gi][0], j, b) for j in range(JH) for b in unit_blocks(gi, h)]


def group_keys(gi):
    return unit_keys(gi, 0) + unit_keys(gi, 1)


def psum_plan():
    tg = [(j, g) for g in range(-(-NT // 4)) for j in range(JH)]
    pairs = [(g,) for g in range(-(-NT // 2))]
    dense = [key for gi in range(len(GROUPS)) for key in group_keys(gi)]
    plan = []

    def add(stage, keys, who):
        plan.extend((stage, k, who) for k in keys)

    add("hT", tg, "V")
    add("P", pairs, "A")
    add("erT", tg, "V")
    add("Q", pairs, "A")
    add("mean", [(0,), (1,)], "V")
    add("agg0", dense, "V")
    add("h2", [(j, b) for j in range(2 * JH) for b in range(NB)], "A")
    add("h3", [(j, b) for j in range(JH) for b in range(NB)], "A")
    add("back0", pairs, "V")
    add("gT1", tg, "A")
    add("x0", [(j, b) for j in range(JH) for b in range(NB)], "A")
    add("x0n", pairs, "V")
    add("dinv", [(g,) for g in range(-(-NT // 4))], "V")
    for li in range(3):
        add(f"agg1{li}", dense, "V")
        add(f"cv{li}", pairs, "V")
    for g in range(-(-NT // 4)):
        add("gT2", [(j, g) for j in range(JH)], "A")
        if g:
            add("lg", [(g - 1,)], "A")
    add("lg", [(-(-NT // 4) - 1,)], "A")
    add("xt", pairs, "A")
    add("gT3", tg, "A")
    add("xj", pairs, "V")
    add("xi", [(j, b) for j in range(JH) for b in range(NB)], "A")
    add("a1", [(b,) for b in range(NB)], "A")
    add("agg3", dense, "V")
    add("back3", pairs, "V")
    return plan


def gnn_kernel(nc, x, src, dst, edge_weight, edge_rep, W1, g1, b1, W2a, g2a, b2a, W2b, g2b, b2b,
               epsilon, lin0_w, lin0_b, conv_w, gat_w, attn_l, attn_r, aW1, ab1, aW2, ab2,
               wa1, ba1, wa2, ba2, out):
    plan = psum_plan()
    number = {(s, k): g for g, (s, k, _) in enumerate(plan)}
    nth, seen = [], {"A": 0, "V": 0}
    for _, _, who in plan:
        seen[who] += 1
        nth.append(seen[who])

    with ExitStack() as ctx:
        def sb(name, shape, dt=F32):
            return ctx.enter_context(nc.sbuf_tensor(name, shape, dt))

        def sem(name):
            return ctx.enter_context(nc.semaphore(name))

        ctx.enter_context(nc.allow_non_contiguous_dma(reason="channel vectors onto partitions"))

        counts = nc.dram_tensor("counts", (SPARE + P, 1), F32).ap()
        weights = nc.dram_tensor("weights", (SPARE + P, 1), F32).ap()
        tab_p = nc.dram_tensor("tab_p", (NP, H), F32).ap()
        tab_q = nc.dram_tensor("tab_q", (NP, H), F32).ap()
        zbuf = nc.dram_tensor("zbuf", (P, CH, H), F32).ap()
        msum = [nc.dram_tensor(f"msum{c}", (MROWS, H), F32).ap() for c in range(COPIES)]
        tab_x = nc.dram_tensor("tab_x", (NP, XW), F32).ap()
        tab_l = nc.dram_tensor("tab_l", (NP, HEADS), F32).ap()
        counts_rows = counts[0:SPARE].rearrange("(r c) o -> r (c o)", c=LD)
        weights_rows = weights[0:SPARE].rearrange("(r c) o -> r (c o)", c=LD)

        W_ = NT * H
        reg_at = -(-nc.sbuf_base // 32) * 32
        reg = sb("reg", [P, 6 * W_])

        def rounded(name, at, n):
            return nc.alloc_sbuf_tensor_at(name, [P, n], F32R, offset=reg_at + 4 * at)

        def view(at, *dims):
            n = 1
            for d in dims:
                n *= d
            v = reg[:, at:at + n]
            if len(dims) == 1:
                return v
            if len(dims) == 2:
                return v.rearrange("p (a b) -> p a b", a=dims[0])
            return v.rearrange("p (a b c) -> p a b c", a=dims[0], b=dims[1])

        RA, RB, RC, RD, RE, RF = (k * W_ for k in range(6))
        x_nat = view(RA, NT, H)
        g_nat = view(RB, NT, H)
        gT = view(RC, JH, NP)
        ring_at = -(-nc.sbuf_base // 32) * 32
        ring_t = sb("ring", [P, RING * UW])
        ring_r = nc.alloc_sbuf_tensor_at("ring_r", [P, RING * UW], F32R, offset=ring_at)
        ring = [ring_t[:, k * UW:(k + 1) * UW] for k in range(RING)]

        at = RD
        gp = view(at, 2 * HALF, H); at += 2 * HALF * H
        gq = view(at, 2 * HALF, H); at += 2 * HALF * H
        zz = view(at, 2 * HALF, 2 * H); at += 4 * HALF * H
        table = view(at, TC, FIELDS); at += TC * FIELDS
        midx = view(at, TC).bitcast(I32); at += TC
        g1row = view(at, H); at += H
        b1row = view(at, H); at += H
        arow = view(at, H); at += H
        brow = view(at, H); at += H
        assert at <= 6 * W_
        zin = view(RD, 2 * HALF, H)
        mo = view(RD + 2 * HALF * H, 2 * HALF, H)
        p_nat, er_nat, erT = view(RD, NT, H), view(RE, NT, H), view(RF, JH, NP)
        mean_row = view(RE + TC, H)
        tmp_i = view(RE, TC).bitcast(I32)
        zeros = ring_t[:, 0:LD]
        raw_src = ring_t[:, LD:LD + PER].bitcast(I32)
        raw_dst = ring_t[:, LD + PER:LD + 2 * PER].bitcast(I32)
        raw_w = ring_t[:, LD + 2 * PER:LD + 3 * PER]
        at = LD + 3 * PER
        eqm = [ring_t[:, at + k * P:at + (k + 1) * P] for k in range(HALF)]
        eqd = [ring_t[:, at + k * P:at + (k + 1) * P] for k in range(2)]; at += 2 * P
        eqp = [ring_t[:, at + k * P:at + (k + 1) * P] for k in range(2)]; at += 2 * P
        low = [ring_t[:, at + k * P:at + (k + 1) * P] for k in range(2)]; at += 2 * P
        junk = ring_t[:, at:at + P]; at += P
        assert at <= RING * UW
        uT, h2T, h3T = view(RD, JH, NP), view(RE, 2 * JH, NP), view(RD, JH, NP)
        lhs_at = ((RB, RE), (RB, RC), (RB, RC), (RB, RC), (RB, RE))
        DR = (NB - 1) * BLK
        rows_at = (tuple(RF + DR + k * UW for k in range(ROWS)),) * 4 + (
            (RF + LD, RF + LD + UW, RD + ROWS * UW, RD + (ROWS + 1) * UW),)
        assert DR + ROWS * UW <= W_ and LD + 2 * UW <= W_ and (ROWS + 2) * UW <= W_
        supT, x0T, dinv_row = view(RD, JH, NP), view(RE, JH, NP), view(RF, DR)
        gT2 = view(RF, JH, NP)
        xt_nat, xt_edge = view(RD, NT, XW), view(RD + NT * XW, NT, XW)
        mix = view(RD, NT, H)
        xiT, xj_nat, a1row = view(RD, JH, NP), view(RE, NT, H), view(RF, LD)
        att = [view(RD + k * UW, UW) for k in range(ROWS)]
        oT = view(RC, JH, NP)

        w1 = sb("w1", [P, 2 * JH, H])
        w2a = sb("w2a", [P, JH, 2 * H])
        w2b = sb("w2b", [P, 2 * JH, H])
        w2a_flat = w2a[:, :, :].rearrange("p a b -> p (a b)")
        dinv_end = w2a_flat[:, 0:BLK]
        out_pair = [w2a_flat[:, BLK:BLK + 2 * H].rearrange("p (t c) -> p t c", c=H), w2b[:, 2:4, :]]
        lin0 = sb("lin0", [P, JH, H])
        conv = sb("conv", [P, 3 * JH, H])
        gatw = sb("gatw", [P, JH, XW])
        w31 = sb("w31", [P, JH, H])
        w32 = sb("w32", [P, JH, H])
        attn = w1[:, 0:2, :]
        attn_tmp = w1[:, 2:4, :]
        ab2row, wa2row = w2b[:, 0, :], w2b[:, 1, :]
        conv_flat = conv[:, :, :].rearrange("p a b -> p (a b)")
        wval = conv_flat[:, 0:TC]
        wcell = conv_flat[:, TC:2 * TC].bitcast(I32)
        ident = sb("ident", [P, P])
        ones = sb("ones", [P, P])
        cols = sb("cols", [P, P])
        prior = sb("prior", [P, P])
        rank = sb("rank", [P, 4])
        vec = sb("vec", [P, 24])
        slot = sb("slot", [P, 2, HALF, FIELDS])
        pair_ix = sb("pair_ix", [P, 2 * HALF * 2], I32)
        cw = sb("cw", [P, 2, HALF, 2])
        high = sb("high", [P, 2, NT])
        first_p = sb("first_p", [P, 2, HALF])
        first_d = sb("first_d", [P, 2, HALF])
        vals = sb("vals", [P, 2 * HALF])
        cell_f = sb("cell_f", [P, 2, HALF, 2])
        cell_ix = sb("cell_ix", [P, 2 * HALF], I32)
        w_vals = sb("w_vals", [P, 2 * HALF])
        w_ix = sb("w_ix", [P, 2 * HALF], I32)
        mslot = sb("mslot", [P, 2, HALF])
        m_ix = sb("m_ix", [P, 2 * HALF], I32)
        stats = sb("stats", [P, 28, 6])
        mv = sb("mv", [P, NT, 2])
        sc = sb("sc", [P, 4, NT])
        dinv = sb("dinv", [P, NT])
        a2 = sb("a2", [P, NT])
        epsc = sb("epsc", [P, 4])
        i_src = sb("i_src", [P, NT], I32)
        i_dst = sb("i_dst", [P, NT], I32)
        el = sb("el", [P, NT, HEADS])
        al = sb("al", [P, NT, HEADS])
        am = sb("am", [P, 2, NT])

        ps = [ctx.enter_context(nc.psum_tensor(f"ps{k}", [P, 512], F32)) for k in range(8)]

        def row_slot(k):
            return ps[(0, 1, 5, 6)[k // 2]][:, (k % 2) * 2 * P:(k % 2 + 1) * 2 * P]

        def rows_value(n, k):
            return HALF * n + min(HALF, k // 2 * 2 + 2)

        sum_bank = (ps[2], ps[7])

        memset_done = sem("memset_done")
        consts_ready = sem("consts_ready")
        raw_ready = sem("raw_ready")
        x_loaded = sem("x_loaded")
        er_loaded = sem("er_loaded")
        w_loaded = sem("w_loaded")
        w1_loaded = sem("w1_loaded")
        zeroed_c, zeroed_w, conv_loaded = sem("zeroed_c"), sem("zeroed_w"), sem("conv_loaded")
        pool_slots, slots_ready = sem("pool_slots"), sem("slots_ready")
        filled, drained_v, drained_a = sem("filled"), sem("drained_v"), sem("drained_a")
        drained = {"V": drained_v, "A": drained_a}
        ln_var, ln_std, ln_scale, ln_out = sem("ln_var"), sem("ln_std"), sem("ln_scale"), sem("ln_out")
        centred, tables_stored = sem("centred"), sem("tables_stored")
        prep_done, rows_ready, eq_ready, cnt_done, cell_ready = (
            sem("prep_done"), sem("rows_ready"), sem("eq_ready"), sem("cnt_done"), sem("cell_ready"))
        z_ready, sq_ready, stat_done = sem("z_ready"), sem("sq_ready"), sem("stat_done")
        gathered = [sem(f"gathered{k}") for k in range(2 * HALF)]
        count_added, weight_added = sem("count_added"), sem("weight_added")
        z_stored = [sem(f"z_stored{h}") for h in range(2)]
        pool_go = sem("pool_go")
        bn_var, bn_std, edge_bn, deg_var, deg_std = (
            sem("bn_var"), sem("bn_std"), sem("edge_bn"), sem("deg_var"), sem("deg_std"))
        z_loaded = [sem(f"z_loaded{h}") for h in range(2)]
        affine, relu_done, m_rows, m_eq, m_sum, m_out, m_prep = (
            sem("affine"), sem("relu_done"), sem("m_rows"), sem("m_eq"), sem("m_sum"), sem("m_out"), sem("m_prep"))
        m_added = [sem(f"m_added{c}") for c in range(COPIES)]
        en_loaded = [sem(f"en_loaded{s}") for s in range(NSPLIT)]
        ring_full = [sem(f"ring_full{k}") for k in range(RING)]
        ring_used, att_sig, att_mul = sem("ring_used"), sem("att_sig"), sem("att_mul")
        rows_high, rows_low = sem("rows_high"), sem("rows_low")
        lhs_in, lhs_high, lhs_low = sem("lhs_in"), sem("lhs_high"), sem("lhs_low")
        bnn_var, bnn_std, bnn_scale, bnn_relu = sem("bnn_var"), sem("bnn_std"), sem("bnn_scale"), sem("bnn_relu")
        sup_tail = sem("sup_tail")
        gat_w_ready, xt_stored, gi_ready, gat_loaded, edge_l, l_stored, x_plus = (
            sem("gat_w_ready"), sem("xt_stored"), sem("gi_ready"), sem("gat_loaded"), sem("edge_l"), sem("l_stored"), sem("x_plus"))
        edge_x = [sem(f"edge_x{s}") for s in range(NSPLIT)]
        gi_cleared = sem("gi_cleared")
        exp_in, exp_out = sem("exp_in"), sem("exp_out")
        late_rows, xi_ready, xj_ready, out_t, stored = (
            sem("late_rows"), sem("xi_ready"), sem("xj_ready"), sem("out_t"), sem("stored"))
        row_free, tail0 = sem("row_free"), sem("tail0")

        def nat(d, rows=NP):
            return d[0:(NT - 1) * P].rearrange("(t p) c -> p t c", p=P)

        def bcast(v, n):
            return v.unsqueeze(2).to_broadcast([v.shape[0], v.shape[1], n])

        def empty_bank(eng, g, also=()):
            eng.wait_ge(filled, g + 1)
            return ps[g % 8]

        def tiles_of(key, per):
            return range(key[-1] * per, min(NT, key[-1] * per + per))

        passes = ["agg0", "agg10", "agg11", "agg12", "agg3"]
        GU = 2 * NT
        PU = len(GROUPS) * GU

        def unit(q):
            return q // PU, q % PU // GU, q % GU // 2, q % 2

        def unit_width(q):
            return len(unit_blocks(unit(q)[1], q % 2)) * BLK

        def wait_unit_used(eng, q):
            pi, gi, t, h = unit(q)
            if t == NT - 1:
                eng.wait_ge(filled, number[passes[pi], unit_keys(gi, h)[-1]] + 1)
            else:
                eng.wait_ge(ring_used, q + 1 - (q + 1) // GU * 2)

        lhs_r = {at: rounded(f"lhs_r{at // W_}", at, W_) for at in sorted({at for pair in lhs_at for at in pair})}
        rows_r = {at: rounded(f"rows_r{k}", at, UW) for k, at in enumerate(sorted({at for pair in rows_at for at in pair}))}

        def lhs_split(pi, part):
            return lhs_r[lhs_at[pi][part]][:, :].rearrange("p (t c) -> p t c", c=H)

        def rows_split(pi, q):
            return rows_r[rows_at[pi][q % ROWS]][:, :]

        def low_part(q):
            return ring_r[:, q % RING * UW:(q % RING + 1) * UW]

        def lhs_step(pi, s):
            return {0: 0, 2: NSPLIT, 3: NSPLIT + NPAIR, 4: NSPLIT + 2 * NPAIR}[pi] + s + 1

        def high_rows(q):
            pi, _, t, _ = unit(q)
            w = unit_width(q)
            if pi == 4:
                nc.scalar.wait_ge(att_mul, q - 4 * PU + 1)
            else:
                nc.scalar.wait_ge(ring_full[q % RING], 16 * (q // RING + 1))
            if q >= ROWS:
                wait_unit_used(nc.scalar, q - ROWS)
            high = rows_split(pi, q)[:, 0:w]
            if pi in (0, 4):
                nc.scalar.activation(high, ring[q % RING][:, 0:w], ACT.Copy).then_inc(rows_high, 1)
            else:
                nc.scalar.activation(high, ring[q % RING][:, 0:w], ACT.Identity,
                                     scale=dinv[:, t:t + 1]).then_inc(rows_high, 1)

        def low_rows(q):
            pi, _, t, _ = unit(q)
            w = unit_width(q)
            rows, high, low = ring[q % RING][:, 0:w], rows_split(pi, q)[:, 0:w].bitcast(F32), low_part(q)[:, 0:w]
            nc.vector.wait_ge(rows_high, q + 1)
            if pi in (0, 4):
                nc.vector.tensor_tensor(low, rows, high, ALU.subtract).then_inc(rows_low, 1)
            else:
                nc.vector.scalar_tensor_tensor(low, rows, dinv[:, t:t + 1], high, ALU.mult,
                                               ALU.subtract).then_inc(rows_low, 1)

        def low_pass(pi, skip, drain):
            for q in range(pi * PU + skip, (pi + 1) * PU):
                if q % PU == GU + DRAIN_AT:
                    drain(0)
                low_rows(q)
            drain(1)

        block = ctx.enter_context(nc.Block())

        @block.sync
        def _(sp):
            sp.wait_ge(memset_done, 1)
            for dst_t, dram, s in ((x_nat, x, x_loaded), (er_nat, edge_rep[0:N], er_loaded)):
                sp.dma_start(dst_t[:, 0:NT - 1, :], nat(dram)).then_inc(s, 16)
                sp.dma_start(dst_t[0:48, NT - 1, :], dram[(NT - 1) * P:(NT - 1) * P + 48]).then_inc(s, 16)
                sp.dma_start(dst_t[48:LAST, NT - 1, :], dram[(NT - 1) * P + 48:N]).then_inc(s, 16)
                if s is x_loaded:
                    sp.dma_start(w1[:, :, :], W1.rearrange("(j p) n -> p j n", p=P)).then_inc(w1_loaded, 16)
            for raw, dram in ((raw_src, src), (raw_dst, dst), (raw_w, edge_weight)):
                sp.dma_start(raw[0:P - 1, :], dram[0:(P - 1) * PER].rearrange("(p c) -> p c", c=PER)).then_inc(raw_ready, 16)
                sp.dma_start(raw[P - 1:P, 0:LASTE], dram[(P - 1) * PER:E].unsqueeze(0)).then_inc(raw_ready, 16)
            sp.wait_ge(memset_done, 2)
            for t in range(NT):
                sp.dma_start(counts_rows[t * P:(t + 1) * P], zeros[:, :]).then_inc(zeroed_c, 16)
            sp.dma_start(counts[SPARE:SPARE + P], zeros[:, 0:1]).then_inc(zeroed_c, 16)
            for tab in (tab_p, tab_q):
                sp.dma_start(tab[N:NP], zeros[0:NP - N, 0:H]).then_inc(tables_stored, 16)
            for k, (tab, nat_t) in enumerate(((tab_p, p_nat), (tab_q, g_nat))):
                sp.wait_ge(centred, k + 1)
                sp.dma_start(nat(tab), nat_t[:, 0:NT - 1, :]).then_inc(tables_stored, 16)
                sp.dma_start(tab[(NT - 1) * P:(NT - 1) * P + 48], nat_t[0:48, NT - 1, :]).then_inc(tables_stored, 16)
                sp.dma_start(tab[(NT - 1) * P + 48:N], nat_t[48:LAST, NT - 1, :]).then_inc(tables_stored, 16)
            sp.wait_ge(row_free, 1)
            sp.dma_start(g1row, g1.unsqueeze(0).to_broadcast([P, H])).then_inc(late_rows, 16)
            sp.dma_start(b1row, b1.unsqueeze(0).to_broadcast([P, H])).then_inc(late_rows, 16)

            sp.dma_start(w2a[:, :, :], W2a.rearrange("(j p) n -> p j n", p=P)).then_inc(w_loaded, 16)
            sp.dma_start(w2b[:, :, :], W2b.rearrange("(j p) n -> p j n", p=P)).then_inc(w_loaded, 16)
            sp.dma_start(lin0[:, :, :], lin0_w.rearrange("(j p) n -> p j n", p=P)).then_inc(w_loaded, 16)
            sp.dma_start(gatw[:, :, 0:H], gat_w.rearrange("(j p) n -> p j n", p=P)).then_inc(w_loaded, 16)
            sp.dma_start(w31[:, :, :], aW1.rearrange("(j p) n -> p j n", p=P)).then_inc(w_loaded, 16)
            sp.dma_start(w32[:, :, :], aW2.rearrange("(j p) n -> p j n", p=P)).then_inc(w_loaded, 16)
            for (name, n), v in zip(VECS, (g2a, b2a, g2b, b2b, lin0_b, ab1, wa1)):
                o = V0[name]
                sp.dma_start(vec[:, o:o + n], v.rearrange("(j p) -> p j", p=P)).then_inc(w_loaded, 16)
            sp.dma_start(epsc[:, 0:1], epsilon.unsqueeze(0).to_broadcast([P, 1])).then_inc(w_loaded, 16)
            sp.dma_start(epsc[:, 1:2], ba1.unsqueeze(0).to_broadcast([P, 1])).then_inc(w_loaded, 16)
            sp.dma_start(epsc[:, 2:3], ba2.unsqueeze(0).to_broadcast([P, 1])).then_inc(w_loaded, 16)

            sp.dma_start(weights[SPARE:SPARE + P], zeros[:, 0:1]).then_inc(zeroed_w, 16)

            def load_unit(q):
                pi, gi, t, h = unit(q)
                rows = counts_rows if pi in (0, 4) else weights_rows
                c0 = unit_blocks(gi, h)[0] * BLK
                if q >= RING:
                    wait_unit_used(sp, q - RING)
                sp.dma_start(ring[q % RING][:, 0:unit_width(q)],
                             rows[t * P:(t + 1) * P, c0:c0 + unit_width(q)]).then_inc(ring_full[q % RING], 16)

            def prefetch():
                sp.wait_ge(count_added, 16 * CH)
                sp.wait_ge(m_sum, CH)
                for q in range(RING):
                    load_unit(q)

            def stream(pi):
                if pi == 1:
                    sp.wait_ge(weight_added, 16 * CH)
                    sp.dma_start(conv[:, :, :], conv_w.rearrange("l (j p) n -> p (l j) n", p=P)).then_inc(conv_loaded, 16)
                for q in range(pi * PU + (RING if pi == 0 else 0), (pi + 1) * PU):
                    load_unit(q)

            weights_steps = weights[0:SPARE].rearrange("(i p c) o -> i p (c o)", p=P, c=ZW)
            zw = ZW // 4

            def store_z(i):
                for h in range(2):
                    n = 2 * i + h
                    for k in (1, 3):
                        wait(sp, z_ready, HALF * n + k)
                        piece = 2 * h + k // 2
                        sp.dma_start(weights_steps[bass.ds(i, 1), :, piece * zw:(piece + 1) * zw].rearrange("i p c -> (i p) c"),
                                     zeros[:, 0:zw]).then_inc(zeroed_w, 16)
                        if piece < COPIES:
                            sp.dma_start(msum[piece][bass.ds(P * i, P)], zeros[:, 0:H]).then_inc(zeroed_w, 16)
                    wait(sp, z_ready, HALF * (n + 1))
                    sp.dma_start(zbuf[:, bass.ds(HALF * n, HALF), :],
                                 zz[:, h * HALF:(h + 1) * HALF, 0:H]).then_inc(z_stored[h], 16)
            loop(sp, ITER, store_z)

            for h in range(2):
                sp.wait_ge(z_stored[h], 16 * ITER)
            sp.wait_ge(stat_done, CH)
            sp.wait_ge(z_ready, CH)

            def load_z(i):
                for h in range(2):
                    n = 2 * i + h
                    wait(sp, m_sum, HALF * (n - 1) if isinstance(n, int) else HALF * (n - 1))
                    sp.dma_start(zin[:, h * HALF:(h + 1) * HALF, :],
                                 zbuf[:, bass.ds(HALF * n, HALF), :]).then_inc(z_loaded[h], 16)
            loop(sp, ITER, load_z)

            prefetch()
            for c in range(COPIES):
                sp.wait_ge(m_added[c], 16 * chain_total(c))
            sp.wait_ge(m_eq, CH)
            sp.wait_ge(m_out, CH)
            for s in range(NSPLIT):
                if s >= 3:
                    sp.wait_ge(lhs_in, lhs_step(0, s - 3))
                for c, r in enumerate((RB, RE, RD)):
                    sp.dma_start(view(r, NT, H)[:, s * LG:(s + 1) * LG, :],
                                 msum[c][s * LG * P:(s + 1) * LG * P].rearrange("(t p) c -> p t c", p=P)).then_inc(en_loaded[s], 16)

            for pi in range(4):
                stream(pi)
                if pi == 0:
                    sp.wait_ge(filled, number["Q", (12,)] + 1)
                    sp.dma_start(attn[:, 0, :], attn_l.rearrange("h d -> (h d)").unsqueeze(0).to_broadcast([P, H])).then_inc(gat_loaded, 16)
                    sp.dma_start(attn[:, 1, :], attn_r.rearrange("h d -> (h d)").unsqueeze(0).to_broadcast([P, H])).then_inc(gat_loaded, 16)
            sp.wait_ge(drained_a, nth[number["lg", (-(-NT // 4) - 1,)]])
            sp.dma_start(tab_l.rearrange("(t p) c -> p t c", p=P), xt_nat[:, :, H:H + HEADS]).then_inc(l_stored, 16)
            for s in range(NSPLIT):
                sp.wait_ge(drained_a, nth[number["xt", (((s + 1) * LG - 1) // 2,)]])
                sp.dma_start(tab_x[s * LG * P:(s + 1) * LG * P].rearrange("(t p) c -> p t c", p=P),
                             xt_nat[:, s * LG:(s + 1) * LG, :]).then_inc(xt_stored, 16)
            sp.wait_ge(filled, number["h3", (JH - 1, NB - 1)] + 1)
            sp.dma_start(ab2row, ab2.unsqueeze(0).to_broadcast([P, H])).then_inc(gat_loaded, 16)
            sp.dma_start(wa2row, wa2.unsqueeze(0).to_broadcast([P, H])).then_inc(gat_loaded, 16)
            stream(4)
            for k, t0 in enumerate(range(0, NT - 1, OUTT)):
                sp.wait_ge(drained_v, nth[number["back3", ((t0 + OUTT - 1) // 2,)]])
                sp.dma_start(out[t0 * P:(t0 + OUTT) * P].rearrange("(t p) c -> p t c", p=P),
                             x_nat[:, t0:t0 + OUTT, :]).then_inc(stored, 16)
            sp.wait_ge(drained_v, nth[number["back3", (NPAIR - 1,)]])
            sp.dma_start(out[(NT - 1) * P:(NT - 1) * P + 48], x_nat[0:48, NT - 1, :]).then_inc(stored, 16)
            sp.dma_start(out[(NT - 1) * P + 48:N], x_nat[48:LAST, NT - 1, :]).then_inc(stored, 16)
            sp.wait_ge(stored, 16 * ((NT - 1) // OUTT + 2))

        @block.gpsimd
        def _(pool):
            pool.memset(ident[:, :], 0.0).then_inc(consts_ready, 1)
            pool.memset(ones[:, :], 1.0).then_inc(consts_ready, 1)
            pool.wait_ge(consts_ready, 2)
            pool.affine_select(out=ident[:, :], in_=ident[:, :], compare_op=ALU.not_equal, fill=1.0,
                               base=0, pattern=[[-1, P]], channel_multiplier=1).then_inc(consts_ready, 1)
            pool.iota(cols[:, :], [[1, P]], base=0, channel_multiplier=0, allow_small_or_imprecise_dtypes=True).then_inc(consts_ready, 1)
            pool.affine_select(out=prior[:, :], in_=ones[:, :], compare_op=ALU.is_gt, fill=0.0,
                               base=0, pattern=[[-1, P]], channel_multiplier=1).then_inc(consts_ready, 1)
            pool.memset(rank[:, 0:1], 0.0).then_inc(consts_ready, 1)
            pool.iota(rank[:, 1:2], [[0, 1]], base=SPARE, channel_multiplier=1, allow_small_or_imprecise_dtypes=True).then_inc(consts_ready, 1)
            pool.iota(rank[:, 2:3], [[0, 1]], base=NP, channel_multiplier=1, allow_small_or_imprecise_dtypes=True).then_inc(consts_ready, 1)

            pool.wait_ge(tables_stored, 16 * 8)
            pool.wait_ge(zeroed_c, 16 * (NT + 1))

            def edges(i):
                for h in range(2):
                    n = 2 * i + h
                    wait(pool, prep_done, n + 1)
                    wait(pool, cell_ready, n + 1)
                    for k in range(HALF):
                        j = h * HALF + k
                        c = 2 * HALF * i + j
                        wait(pool, z_ready, c - 2 * HALF + 1)
                        pool.sem_inc(pool_go, 1)
                        for buf, tab, f in ((gp, tab_p, 0), (gq, tab_q, 1)):
                            pool.indirect_dma_start(
                                buf[:, j, :], None, tab,
                                bass.IndirectOffsetOnAxis(ap=pair_ix[:, 2 * j + f:2 * j + f + 1], axis=0),
                            ).then_inc(gathered[j], 16)
                        wait(pool, count_added, 16 * c)
                        pool.sem_inc(pool_go, 1)
                        pool.indirect_dma_start(
                            counts, bass.IndirectOffsetOnAxis(ap=cell_ix[:, j:j + 1], axis=0),
                            vals[:, j:j + 1], None, compute_op=ALU.add,
                        ).then_inc(count_added, 16)
            loop(pool, ITER, edges)

            slots = Signal(pool_slots)

            def weight_slots(o, w, n):
                pool.tensor_copy(w_vals[:, o:o + n], wval[:, bass.ds(w, n)])
                pool.wait_ge(slots.sem, slots.on(pool.tensor_copy(w_ix[:, o:o + n], wcell[:, bass.ds(w, n)])))

            def add_weights(o, w):
                wait(pool, weight_added, 16 * w)
                pool.sem_inc(pool_go, 1)
                pool.indirect_dma_start(
                    weights, bass.IndirectOffsetOnAxis(ap=w_ix[:, o:o + 1], axis=0),
                    w_vals[:, o:o + 1], None, compute_op=ALU.add,
                ).then_inc(weight_added, 16)

            pool.wait_ge(zeroed_w, 16 * (1 + ITER * (4 + COPIES)))
            pool.wait_ge(cell_ready, NHALF + 1)

            pool.sem_inc(pool_go, 1)
            weight_slots(HALF, 0, WPRE)
            for w in range(WPRE):
                add_weights(HALF + w, w)

            def messages(i):
                for h in range(2):
                    n = 2 * i + h
                    w0 = WPRE + WP2 * i + (len(EXTRA[0]) if h else 0)
                    wait(pool, slots_ready, n + 1)
                    for k in range(HALF):
                        j = h * HALF + k
                        wait(pool, m_out, 2 * HALF * i + j + 1)
                        wait(pool, m_added[j % COPIES], 16 * chain_before(i, j))
                        pool.sem_inc(pool_go, 1)
                        pool.indirect_dma_start(
                            msum[j % COPIES], bass.IndirectOffsetOnAxis(ap=m_ix[:, j:j + 1], axis=0),
                            mo[:, j, :], None, compute_op=ALU.add,
                        ).then_inc(m_added[j % COPIES], 16)
                        if k in EXTRA[h]:
                            w = EXTRA[h].index(k)
                            add_weights(h * HALF + w, w0 + w)
            loop(pool, ITER, messages)

            def tail_half(n, h):
                w = WPRE + ITER * WP2 + HALF * n
                pool.wait_ge(weight_added, 16 * (w - len(EXTRA[1])))
                pool.sem_inc(pool_go, 1)
                weight_slots(h * HALF, w, HALF)
                for k in range(HALF):
                    add_weights(h * HALF + k, w + k)

            def tail(i):
                tail_half(2 * i, 0)
                tail_half(2 * i + 1, 1)
            loop(pool, WTAIL // 2, tail, [slots])
            tail_half(WTAIL - 1, 0)

            pool.memset(i_src[:, :], N).then_inc(gi_cleared, 1)
            pool.memset(i_dst[:, :], N).then_inc(gi_cleared, 1)
            pool.wait_ge(gi_cleared, 2)
            full = (NT - 1) * P
            for ix, dram in ((i_src, src), (i_dst, dst)):
                pool.dma_start(ix[:, 0:NT - 1], dram[0:full].rearrange("(t p) -> p t", p=P)).then_inc(gi_ready, 16)
                pool.dma_start(ix[0:LAST, NT - 1:NT], dram[full:N].unsqueeze(1)).then_inc(gi_ready, 16)
            pool.wait_ge(gi_ready, 64)
            pool.wait_ge(l_stored, 16)
            for t in range(NT):
                pool.indirect_dma_start(el[:, t, :], None, tab_l,
                                        bass.IndirectOffsetOnAxis(ap=i_src[:, t:t + 1], axis=0)).then_inc(edge_l, 16)
            pool.wait_ge(xt_stored, 16 * NSPLIT)
            for t in range(NT):
                pool.indirect_dma_start(xt_edge[:, t, :], None, tab_x,
                                        bass.IndirectOffsetOnAxis(ap=i_dst[:, t:t + 1], axis=0)).then_inc(edge_x[t // LG], 16)
            pool.wait_ge(ln_out, 4 * NT)
            pool.tensor_tensor(x_nat, x_nat, g_nat, ALU.add).then_inc(x_plus, 1)

        @block.scalar
        def _(act):
            act_step = Signal(ctx.enter_context(nc.semaphore("act_step")))

            def emptied(ins):
                ins.then_inc(drained_a, 1)

            def layernorm(k, before=lambda q: None, stage=None, dest=None):
                def apply(q):
                    act.wait_ge(ln_scale, k * (NT // LG) + q + 1)
                    for t in range(q * LG, (q + 1) * LG):
                        act.activation(g_nat[:, t, :], x_nat[:, t, :], ACT.Relu, bias=sc[:, 3, t:t + 1],
                                       scale=sc[:, 2, t:t + 1]).then_inc(ln_out, 1)
                    if stage:
                        copy_groups(q * LG // 4)

                copied = [0]

                def copy_groups(upto):
                    for g in range(copied[0], upto):
                        ts = tiles_of((g,), 4)
                        for j in range(JH):
                            bank = empty_bank(act, number[stage, (j, g)])
                            emptied(act.activation(dest[:, j, ts[0] * P:(ts[-1] + 1) * P], bank[:, 0:len(ts) * P], ACT.Copy))
                        if stage == "gT2" and g:
                            copy_logits(g - 1)
                    copied[0] = upto

                for q in range(NT // LG):
                    before(q)
                    act.wait_ge(ln_var, k * (NT // LG) + q + 1)
                    ts = slice(q * LG, (q + 1) * LG)
                    act.activation(sc[:, 1, ts], sc[:, 0, ts], ACT.Sqrt).then_inc(ln_std, 1)
                    if q:
                        apply(q - 1)
                apply(NT // LG - 1)
                if stage:
                    copy_groups(-(-NT // 4))
                if stage == "gT2":
                    copy_logits(-(-NT // 4) - 1)

            def copy_logits(g):
                ts = tiles_of((g,), 4)
                bank = empty_bank(act, number["lg", (g,)])
                emptied(act.activation(xt_nat[:, ts[0]:ts[-1] + 1, H:XW],
                                       bank[:, 0:len(ts) * 2 * HEADS].rearrange("p (t c) -> p t c", c=2 * HEADS), ACT.Copy))

            def copy_pairs(stage, dest):
                for g in range(-(-NT // 2)):
                    q = number[stage, (g,)]
                    bank = empty_bank(act, q)
                    ts = tiles_of((g,), 2)
                    emptied(act.activation(dest[:, ts[0]:ts[-1] + 1, :],
                                           bank[:, 0:len(ts) * H].rearrange("p (t c) -> p t c", c=H), ACT.Copy))

            layernorm(0)
            copy_pairs("P", p_nat)
            act.wait_ge(drained_v, nth[number["hT", (JH - 1, 6)]])
            copy_pairs("Q", g_nat)

            def squares(i):
                for h in range(2):
                    n = 2 * i + h
                    wait(act, stat_done, HALF * (n - 1))
                    for k in range(HALF):
                        j = h * HALF + k
                        wait(act, z_ready, 2 * HALF * i + j + 1)
                        act.activation(zz[:, j, H:2 * H], zz[:, j, 0:H], ACT.Square).then_inc(sq_ready, 1)
            loop(act, ITER, squares)
            act.wait_ge(bn_var, 1)
            act.activation(arow, arow, ACT.Sqrt).then_inc(bn_std, 1)
            act.wait_ge(deg_var, 1)
            act.activation(sc[:, 1, :], sc[:, 0, :], ACT.Sqrt).then_inc(deg_std, 1)

            def relu_half(n, h):
                wait(act, affine, n + 1)
                act.activation(zin[:, h * HALF:(h + 1) * HALF, :], zin[:, h * HALF:(h + 1) * HALF, :],
                               ACT.Relu).then_inc(relu_done, 1)

            def sums(i):
                for h in range(2):
                    n = 2 * i + h
                    for k in range(HALF):
                        j = h * HALF + k
                        c = 2 * HALF * i + j
                        wait(act, m_sum, c + 1)
                        wait(act, m_added[j % COPIES], 16 * (chain_before(i, j) + 1 - chain_per(j % COPIES)))
                        act.activation(mo[:, j, :], sum_bank[j % 2][:, 0:H], ACT.Copy).then_inc(m_out, 1)
                    if h == 0:
                        relu_half(n + 1, 1)
                    else:
                        relu_half(n + 1, 0)
            relu_half(0, 0)
            loop(act, ITER - 1, sums)
            i = ITER - 1
            for h in range(2):
                for k in range(HALF):
                    j = h * HALF + k
                    c = 2 * HALF * i + j
                    act.wait_ge(m_sum, c + 1)
                    act.wait_ge(m_added[j % COPIES], 16 * (chain_before(i, j) + 1 - chain_per(j % COPIES)))
                    act.activation(mo[:, j, :], sum_bank[j % 2][:, 0:H], ACT.Copy).then_inc(m_out, 1)
                if h == 0:
                    relu_half(NHALF - 1, 1)

            def high_lhs(pi, s, dest, got):
                act.wait_ge(lhs_in, lhs_step(pi, s))
                act.activation(dest, got, ACT.Copy).then_inc(lhs_high, 1)

            def high_step(pi, s):
                ts = slice(s * LG, (s + 1) * LG)
                high_lhs(pi, s, lhs_split(pi, 0)[:, ts, :], view(lhs_at[pi][1], NT, H)[:, ts, :])

            def high_pass(pi, skip):
                for q in range(pi * PU + skip, (pi + 1) * PU):
                    high_rows(q)

            for q in range(PU):
                if q % ROWS == 0 and q // ROWS < NSPLIT:
                    high_step(0, q // ROWS)
                high_rows(q)

            for stage, dest, nj in (("h2", h2T, 2 * JH), ("h3", h3T, JH)):
                if stage == "h3":
                    act.wait_ge(filled, number["h2", (2 * JH - 1, NB - 1)] + 1)
                for j in range(nj):
                    for b in range(NB):
                        bank = empty_bank(act, number[stage, (j, b)])
                        emptied(act.activation(dest[:, j, b * BLK:(b + 1) * BLK], bank[:, 0:BLK], ACT.Copy))
                r = 0 if stage == "h2" else 1
                act.wait_ge(bnn_var, r + 1)
                act.activation(sc[:, 1, 0:nj], sc[:, 0, 0:nj], ACT.Sqrt).then_inc(bnn_std, 1)
                act.wait_ge(bnn_scale, r + 1)
                for j in range(nj):
                    act.activation(dest[:, j, 0:LD], dest[:, j, 0:LD], ACT.Relu, bias=sc[:, 3, j:j + 1],
                                   scale=sc[:, 2, j:j + 1]).then_inc(bnn_relu, 1)

            layernorm(1, stage="gT1", dest=gT)
            act.wait_ge(w_loaded, 16 * LOADS)
            act.wait_ge(bnn_relu, 3 * JH)
            act.wait_ge(filled, number["h3", (JH - 1, NB - 1)] + 1)
            for j in range(JH):
                for b in range(NB):
                    bank = empty_bank(act, number["x0", (j, b)])
                    emptied(act.activation(x0T[:, j, b * BLK:(b + 1) * BLK], bank[:, 0:BLK], ACT.Relu,
                                           bias=vec[:, V0["lin0_b"] + j:V0["lin0_b"] + j + 1]))
            for q in range(PU, PU + ROWS):
                high_rows(q)
            for li in range(3):
                for gi in range(NPAIR) if li else ():
                    ts = slice(2 * gi, min(NT, 2 * gi + 2))
                    high_lhs(1 + li, gi, lhs_split(1, 0)[:, ts, :], out_pair[gi % 2][:, 0:ts.stop - ts.start, :])
                high_pass(1 + li, ROWS)
                if li < 2:
                    for q in range((2 + li) * PU, (2 + li) * PU + ROWS):
                        high_rows(q)

            layernorm(2, stage="gT2", dest=gT2)
            copy_pairs("xt", xt_nat[:, :, 0:H])

            def exponentials(q):
                for s in ((0, 1) if q == 0 else (q + 1,)):
                    if s < NSPLIT:
                        act.wait_ge(exp_in, s + 1)
                        ts = slice(s * LG, (s + 1) * LG)
                        act.activation(al[:, ts, :], al[:, ts, :], ACT.Exp).then_inc(exp_out, 1)

            layernorm(3, exponentials, "gT3", gT)
            act.wait_ge(x_plus, 1)
            for s in range(NSPLIT):
                high_step(4, s)
            for j in range(JH):
                for b in range(NB):
                    bank = empty_bank(act, number["xi", (j, b)])
                    emptied(act.activation(xiT[:, j, b * BLK:(b + 1) * BLK], bank[:, 0:BLK], ACT.Identity,
                                           bias=vec[:, V0["ab1"] + j:V0["ab1"] + j + 1]))
            for b in range(NB):
                bank = empty_bank(act, number["a1", (b,)])
                emptied(act.activation(a1row[:, b * BLK:(b + 1) * BLK], bank[:, 0:BLK], ACT.Identity,
                                       bias=epsc[:, 1:2]))
            act.wait_ge(drained_a, nth[number["a1", (NB - 1,)]])

            def sigmoid(u):
                if u >= ROWS:
                    act.wait_ge(att_mul, u - ROWS + 1)
                _, gi, t, h = unit(u)
                if gi == 0 and h == 0 and t % LG == 0:
                    act.wait_ge(xj_ready, t // LG + 1)
                c0 = unit_blocks(gi, h)[0] * BLK
                act.activation(att[u % ROWS][:, 0:unit_width(u)], a1row[:, c0:c0 + unit_width(u)], ACT.Sigmoid,
                               bias=a2[:, t:t + 1]).then_inc(att_sig, 1)

            for u in range(AHEAD):
                sigmoid(u)
            for u in range(PU):
                if u + AHEAD < PU:
                    sigmoid(u + AHEAD)
                high_rows(4 * PU + u)

        @block.tensor
        def _(pe):
            def open_bank(g):
                if g >= 8:
                    who = plan[g - 8][2]
                    pe.wait_ge(drained[who], nth[g - 8])
                return ps[g % 8]

            def to_T(stage, src_nat, done, base, behind=None):
                for gi in range(-(-NT // 4)):
                    for j in range(JH):
                        bank = open_bank(number[stage, (j, gi)])
                        ts = tiles_of((gi,), 4)
                        for t in ts:
                            if done is not None:
                                pe.wait_ge(done, base + t + 1)
                            m = pe.transpose(bank[:, (t - ts[0]) * P:(t - ts[0] + 1) * P],
                                             src_nat[:, t, j * P:(j + 1) * P], ident[:, :])
                        m.then_inc(filled, 1)
                    if behind and gi:
                        behind(gi - 1)
                if behind:
                    behind(gi)

            def node_rows(stage, lhs, rhs, width=H, per=2, nk=JH, base=0, block_ready=None):
                for gi in range(-(-NT // per)):
                    bank = open_bank(number[stage, (gi,)])
                    ts = tiles_of((gi,), per)
                    if block_ready:
                        wait_block(block_ready, min(NB - 1, ((ts[-1] + 1) * P - 1) // BLK))
                    for t in ts:
                        for k in range(nk):
                            m = pe.matmul(bank[:, (t - ts[0]) * width:(t - ts[0] + 1) * width],
                                          lhs[:, k, t * P:(t + 1) * P], rhs[:, base + k, :],
                                          start=(k == 0), stop=(k == nk - 1))
                    m.then_inc(filled, 1)

            def wait_block(name, b):
                for b0, nb in GROUPS:
                    if b0 <= b < b0 + nb:
                        pe.wait_ge(drained_v, nth[number[name, (b0, JH - 1, b)]])

            def node_cols(stage, w, rhs, nj, nk, ready=None, block_ready=None):
                for j in range(nj):
                    for b in range(NB):
                        bank = open_bank(number[stage, (j, b)])
                        if block_ready and j == 0:
                            wait_block(block_ready, b)
                        for k in range(nk):
                            if ready is not None and j == 0 and b == 0:
                                pe.wait_ge(*ready(k))
                            m = pe.matmul(bank[:, 0:BLK], w[:, k, j * P:(j + 1) * P], rhs[:, k, b * BLK:(b + 1) * BLK],
                                          start=(k == 0), stop=(k == nk - 1))
                        m.then_inc(filled, 1)

            def back(stage, src_T, block_ready=None, tail=None):
                for gi in range(-(-NT // 2)):
                    bank = open_bank(number[stage, (gi,)])
                    ts = tiles_of((gi,), 2)
                    if block_ready:
                        wait_block(block_ready, min(NB - 1, ((ts[-1] + 1) * P - 1) // BLK))
                    if tail and gi == NPAIR - 1:
                        pe.wait_ge(tail, 1)
                    for t in ts:
                        for j in range(JH):
                            o = (t - ts[0]) * H + j * P
                            m = pe.transpose(bank[:, o:o + P], src_T[:, j, t * P:(t + 1) * P], ident[:, :])
                    m.then_inc(filled, 1)

            def dense(pi):
                name = passes[pi]
                for q in range(pi * PU, (pi + 1) * PU):
                    _, gi, t, h = unit(q)
                    blocks = unit_blocks(gi, h)
                    if gi == 0 and h == 0:
                        if pi == 1:
                            pe.wait_ge(drained_v, nth[number["x0n", (t // 2,)]])
                        else:
                            pe.wait_ge(lhs_low, lhs_step(pi, t // LG if pi in (0, 4) else t // 2))
                    pe.wait_ge(rows_low, q + 1)
                    high, low = rows_split(pi, q), low_part(q)
                    for j in range(JH):
                        lhs = [lhs_split(pi, part)[:, t, j * P:(j + 1) * P] for part in range(2)]
                        for part, rows in ((0, high), (0, low), (1, high)):
                            for b in blocks:
                                g = number[name, (GROUPS[gi][0], j, b)]
                                first = t == 0 and part == 0 and rows is high
                                last = t == NT - 1 and part == 1
                                bank = open_bank(g) if first else ps[g % 8]
                                c = (b - blocks[0]) * BLK
                                m = pe.matmul(bank[:, 0:BLK], lhs[part], rows[:, c:c + BLK], start=first, stop=last)
                                if last:
                                    m.then_inc(filled, 1)
                    if t < NT - 1:
                        m.then_inc(ring_used, 1)

            pe.wait_ge(consts_ready, 8)
            to_T("hT", g_nat, ln_out, 0)
            pe.wait_ge(w1_loaded, 16)
            pe.wait_ge(drained_v, nth[number["hT", (JH - 1, 6)]])
            node_rows("P", gT, w1)
            pe.wait_ge(er_loaded, 48)
            to_T("erT", er_nat, None, 0)
            pe.wait_ge(drained_v, nth[number["erT", (JH - 1, 6)]])
            node_rows("Q", erT, w1, base=JH)
            for k, nat_t in enumerate((p_nat, g_nat)):
                bank = open_bank(number["mean", (k,)])
                pe.wait_ge(drained_a, nth[number["P" if k == 0 else "Q", (12,)]])
                for t in range(NT):
                    m = pe.matmul(bank[:, 0:H], ones[:, :], nat_t[:, t, :], start=(t == 0), stop=(t == NT - 1))
                m.then_inc(filled, 1)
            g = number["mean", (1,)]
            pe.wait_ge(drained_v, nth[g])
            pe.wait_ge(drained_a, nth[number["Q", (12,)]])

            cnt_bank, deg_bank, stat_bank = ps[2], ps[3], ps[4]
            pe.wait_ge(memset_done, 3)
            pe.matmul(deg_bank[:, 0:NT], junk[:, :], ones[:, 0:NT], start=True, stop=False, skip_group_check=True)
            pe.matmul(stat_bank[:, :], junk[:, :], x_nat[:, 0:2, :], start=True, stop=False, skip_group_check=True)

            def chunk_rows(n, h, k):
                c = HALF * n + k
                if k == 0:
                    wait(pe, prep_done, n + 1)
                wait(pe, eq_ready, rows_value(n - 1, k))
                bank = row_slot(k)
                pe.matmul(bank[:, 0:P], slot[:, h, k, 0:1].to_broadcast([P, P]), ident[:, :], start=True, stop=True)
                pe.matmul(bank[:, P:2 * P], slot[:, h, k, 1:2].to_broadcast([P, P]), ident[:, :],
                          start=True, stop=True).then_inc(rows_ready, 1)

            def chunk_counts(n, h, k):
                c = HALF * n + k
                s = (h * HALF + k) % 2
                if k == 0:
                    wait(pe, cell_ready, n)
                wait(pe, eq_ready, c + 1)
                pe.matmul(cnt_bank[:, 2 * k:2 * k + 2], eqp[s], cw[:, h, k, :], start=True, stop=True,
                          skip_group_check=True)
                pe.matmul(deg_bank[:, 0:NT], low[s], high[:, s, :], start=False, stop=False,
                          skip_group_check=True).then_inc(cnt_done, 1)

            def chunk_stats(c, j):
                wait(pe, sq_ready, c + 1)
                pe.matmul(stat_bank[:, :], ones[:, :], zz[:, j, :], start=False, stop=False,
                          skip_group_check=True).then_inc(stat_done, 1)

            def rows_ahead(n, h, k):
                if k % 2 == 0:
                    for kk in range(0 if k == 0 else k + 2, min(k + 4, HALF)):
                        chunk_rows(n, h, kk)

            for k in range(HALF):
                rows_ahead(0, 0, k)
                chunk_counts(0, 0, k)

            def phase1(i):
                for h in range(2):
                    n = 2 * i + h
                    for k in range(HALF):
                        rows_ahead(n + 1, 1 - h, k)
                        chunk_counts(n + 1, 1 - h, k)
                        if k >= LAG:
                            chunk_stats(2 * HALF * i + h * HALF + k - LAG, h * HALF + k - LAG)
                    for k in range(HALF - LAG, HALF):
                        chunk_stats(2 * HALF * i + h * HALF + k, h * HALF + k)
            loop(pe, ITER, phase1)

            pe.wait_ge(bn_var, 1)
            pe.wait_ge(deg_var, 1)

            def phase2(i):
                for h in range(2):
                    n = 2 * i + h
                    for k in range(HALF):
                        j = h * HALF + k
                        c = 2 * HALF * i + j
                        if k == 0:
                            wait(pe, m_prep, n + 1)
                            for kk in range(HALF):
                                m_row(n, h, kk)
                            wait(pe, relu_done, n + 1)
                        wait(pe, m_eq, c + 1)
                        wait(pe, m_out, c - 1)
                        pe.matmul(sum_bank[j % 2][:, 0:H], eqm[k], zin[:, j, :], start=True, stop=True).then_inc(m_sum, 1)

            def m_row(n, h, k):
                wait(pe, m_eq, rows_value(n - 1, k))
                pe.matmul(row_slot(k)[:, 0:P], mslot[:, h, k:k + 1].to_broadcast([P, P]), ident[:, :],
                          start=True, stop=True).then_inc(m_rows, 1)
            loop(pe, ITER, phase2)

            dense(0)
            pe.wait_ge(w_loaded, 16 * LOADS)
            node_cols("h2", w2a, uT, 2 * JH, JH, block_ready="agg0")
            node_cols("h3", w2b, h2T, JH, 2 * JH, ready=lambda k: (bnn_relu, k + 1))
            pe.wait_ge(bnn_relu, 3 * JH)
            pe.wait_ge(tail0, 1)
            back("back0", h3T)

            to_T("gT1", g_nat, ln_out, NT)
            pe.wait_ge(drained_a, nth[number["gT1", (JH - 1, 6)]])
            node_cols("x0", lin0, gT, JH, JH)
            pe.wait_ge(drained_a, nth[number["x0", (JH - 1, NB - 1)]])
            pe.wait_ge(sup_tail, 1)
            back("x0n", x0T)
            for gi in range(-(-NT // 4)):
                bank = open_bank(number["dinv", (gi,)])
                ts = tiles_of((gi,), 4)
                for t in ts:
                    m = pe.matmul(bank[:, (t - ts[0]) * P:(t - ts[0] + 1) * P],
                                  dinv[:, t:t + 1].to_broadcast([P, P]), ident[:, :], start=True, stop=True)
                m.then_inc(filled, 1)
            for li in range(3):
                dense(1 + li)
                if li == 0:
                    pe.wait_ge(conv_loaded, 16)
                node_rows(f"cv{li}", supT, conv, base=li * JH, block_ready=f"agg1{li}")

            pe.wait_ge(gat_w_ready, 2 * JH)

            def logit_group(g):
                pe.wait_ge(drained_a, nth[number["gT2", (JH - 1, g)]])
                bank = open_bank(number["lg", (g,)])
                ts = tiles_of((g,), 4)
                for t in ts:
                    for k in range(JH):
                        o = (t - ts[0]) * 2 * HEADS
                        m = pe.matmul(bank[:, o:o + 2 * HEADS], gT2[:, k, t * P:(t + 1) * P],
                                      gatw[:, k, H:XW], start=(k == 0), stop=(k == JH - 1))
                m.then_inc(filled, 1)

            to_T("gT2", g_nat, ln_out, 2 * NT, behind=logit_group)
            node_rows("xt", gT2, gatw[:, :, 0:H])

            to_T("gT3", g_nat, ln_out, 3 * NT)
            pe.wait_ge(drained_a, nth[number["gT3", (JH - 1, 6)]])
            node_rows("xj", gT, w32)
            node_cols("xi", w31, gT, JH, JH)
            for b in range(NB):
                bank = open_bank(number["a1", (b,)])
                for k in range(JH):
                    pe.wait_ge(xi_ready, k * NB + b + 1)
                    m = pe.matmul(bank[:, 0:BLK], vec[:, V0["wa1"] + k:V0["wa1"] + k + 1].to_broadcast([P, P]),
                                  xiT[:, k, b * BLK:(b + 1) * BLK], start=(k == 0), stop=(k == JH - 1))
                m.then_inc(filled, 1)
            dense(4)
            back("back3", oT, block_ready="agg3", tail=out_t)

        @block.vector
        def _(v):
            step = Signal(ctx.enter_context(nc.semaphore("dve_step")))
            loop_signals = [step]

            def do(ins):
                v.wait_ge(step.sem, step.on(ins))

            def emptied(ins):
                ins.then_inc(drained_v, 1)

            def after(g):
                v.wait_ge(drained_v, nth[g])

            def layernorm(k, ready=lambda q: None):
                def scales(q):
                    ts = slice(q * LG, (q + 1) * LG)
                    v.wait_ge(ln_std, k * (NT // LG) + q + 1)
                    do(v.reciprocal(sc[:, 2, ts], sc[:, 1, ts]))
                    v.scalar_tensor_tensor(sc[:, 3, ts], mv[:, ts, 0], -1.0, sc[:, 2, ts], ALU.mult, ALU.mult).then_inc(ln_scale, 1)
                for q in range(NT // LG):
                    ready(q)
                    ts = slice(q * LG, (q + 1) * LG)
                    for t in range(q * LG, (q + 1) * LG):
                        last = v.bn_stats(stats[:, t, :], x_nat[:, t, :])
                    do(last)
                    for t in range(q * LG, (q + 1) * LG):
                        last = v.bn_aggr(mv[:, t, :], stats[:, t, :])
                    do(last)
                    v.tensor_scalar(sc[:, 0, ts], mv[:, ts, 1], BN_EPS, None, ALU.add).then_inc(ln_var, 1)
                    if q:
                        scales(q - 1)
                scales(NT // LG - 1)

            def copy_T(stage, dest):
                for gi in range(-(-NT // 4)):
                    for j in range(JH):
                        bank = empty_bank(v, number[stage, (j, gi)])
                        ts = tiles_of((gi,), 4)
                        emptied(v.tensor_copy(dest[:, j, ts[0] * P:(ts[-1] + 1) * P], bank[:, 0:len(ts) * P]))

            def pair_bank(stage, gi):
                bank = empty_bank(v, number[stage, (gi,)])
                ts = tiles_of((gi,), 2)
                return slice(ts[0], ts[-1] + 1), bank[:, 0:len(ts) * H].rearrange("p (t c) -> p t c", c=H)

            def step_pairs(q):
                return range(-(-q * LG // 2), -(-min(NT, (q + 1) * LG) // 2))

            def add_pairs(stage, pairs):
                for gi in pairs:
                    ts, got = pair_bank(stage, gi)
                    emptied(v.tensor_tensor(x_nat[:, ts, :], x_nat[:, ts, :], got, ALU.add))
                after(number[stage, (pairs[-1],)])

            v.memset(x_nat[:, NT - 1, :], 0.0)
            v.memset(er_nat[:, NT - 1, :], 0.0).then_inc(memset_done, 1)
            v.memset(zeros, 0.0).then_inc(memset_done, 1)
            v.memset(junk, 0.0).then_inc(memset_done, 1)
            v.wait_ge(x_loaded, 48)
            layernorm(0)
            copy_T("hT", gT)
            copy_T("erT", erT)
            for k, nat_t in enumerate((p_nat, g_nat)):
                bank = empty_bank(v, number["mean", (k,)])
                v.tensor_scalar(mean_row, bank[:, 0:H], 1.0 / N, None, ALU.mult).then_inc(drained_v, 1)
                after(number["mean", (k,)])
                v.tensor_tensor(nat_t, nat_t, mean_row.unsqueeze(1).to_broadcast([P, NT, H]), ALU.subtract).then_inc(centred, 1)
                v.wait_ge(centred, k + 1)

            v.wait_ge(raw_ready, 96)
            v.wait_ge(filled, number["Q", (12,)] + 1)
            do(v.memset(table[:, :, 0:2], float(N)))
            do(v.memset(table[:, :, 2:3], 0.0))
            do(v.memset(table[:, :, 3:FIELDS], 0.0))
            for f, raw in ((0, raw_src), (1, raw_dst), (2, raw_w)):
                for prt, n, o in ((slice(0, P), LASTE, 0), (slice(0, 96), PER - LASTE, LASTE),
                                  (slice(96, P - 1), PER - LASTE, LASTE)):
                    do(v.tensor_copy(table[prt, o:o + n, f], raw[prt, o:o + n]))
            do(v.tensor_copy(tmp_i, table[:, :, 1]))
            do(v.tensor_scalar(tmp_i, tmp_i, 7, None, ALU.arith_shift_right))
            do(v.tensor_copy(table[:, :, 4], tmp_i))
            do(v.scalar_tensor_tensor(table[:, :, 3], table[:, :, 4], -float(P), table[:, :, 1], ALU.mult, ALU.add))
            v.wait_ge(consts_ready, 8)
            for f, hi, lo in ((5, 1, 0), (6, 0, 1)):
                do(v.scalar_tensor_tensor(table[:, :, f], table[:, :, hi], float(LD), table[:, :, lo], ALU.mult, ALU.add))
                do(v.tensor_scalar(table[:, :, f], table[:, :, f], rank[:, 1:2], None, ALU.subtract))
            do(v.memset(cw[:, :, :, 0:1], 1.0))
            v.memset(stats[:, 0, 0:1], 0.0).then_inc(row_free, 1)

            def prep(n, h):
                wait(v, cnt_done, HALF * (n - 1))
                cs = bass.ds(HALF * n, HALF)
                do(v.tensor_copy(slot[:, h], table[:, cs, :]))
                v.tensor_copy(cw[:, h, :, 1], slot[:, h, :, 2])
                v.tensor_copy(pair_ix[:, 2 * h * HALF:2 * (h + 1) * HALF].rearrange("p (k f) -> p k f", f=2),
                              slot[:, h, :, 0:2]).then_inc(prep_done, 1)

            def equal(n, h, k):
                c = HALF * n + k
                s = (h * HALF + k) % 2
                bank = row_slot(k)
                wait(v, rows_ready, rows_value(n, k))
                wait(v, cnt_done, c - 1)
                sd = step.on(v.tensor_scalar(eqd[s], bank[:, P:2 * P], slot[:, h, k, 1:2], None, ALU.is_equal))
                v.tensor_scalar(low[s], cols[:, :], slot[:, h, k, 3:4], slot[:, h, k, 2:3], ALU.is_equal, ALU.mult)
                v.tensor_scalar(high[:, s, :], cols[:, 0:NT], slot[:, h, k, 4:5], None, ALU.is_equal)
                v.wait_ge(step.sem, sd)
                v.scalar_tensor_tensor(eqp[s], bank[:, 0:P], slot[:, h, k, 0:1], eqd[s], ALU.is_equal,
                                       ALU.mult).then_inc(eq_ready, 1)
                do(v.tensor_tensor_reduce(junk, eqd[s], prior[:, :], 1.0, 0.0, ALU.mult, ALU.add, first_d[:, h, k:k + 1]))
                wait(v, eq_ready, c + 1)
                do(v.tensor_tensor_reduce(junk, eqp[s], prior[:, :], 1.0, 0.0, ALU.mult, ALU.add, first_p[:, h, k:k + 1]))

            def cells(n, h):
                cs = bass.ds(HALF * n, HALF)
                wait(v, cnt_done, HALF * (n + 1))
                wait(v, count_added, 16 * HALF * (n - 1))
                got = ps[2][:, 0:2 * HALF].rearrange("p (k f) -> p k f", f=2)
                v.tensor_copy(vals[:, h * HALF:(h + 1) * HALF], got[:, :, 0])
                v.tensor_copy(wval[:, cs], got[:, :, 1])
                v.tensor_scalar(first_p[:, h, :], first_p[:, h, :], 0.0, None, ALU.is_equal)
                v.tensor_scalar(mslot[:, h, :], slot[:, h, :, 1], rank[:, 2:3], None, ALU.subtract)
                do(v.tensor_scalar(first_d[:, h, :], first_d[:, h, :], 0.0, None, ALU.is_equal))
                v.tensor_tensor(mslot[:, h, :], mslot[:, h, :], first_d[:, h, :], ALU.mult)
                v.tensor_tensor(cell_f[:, h, :, 0], slot[:, h, :, 5], first_p[:, h, :], ALU.mult)
                do(v.tensor_tensor(cell_f[:, h, :, 1], slot[:, h, :, 6], first_p[:, h, :], ALU.mult))
                v.tensor_scalar(midx[:, cs], mslot[:, h, :], rank[:, 2:3], None, ALU.add)
                v.tensor_scalar(wcell[:, cs], cell_f[:, h, :, 1], rank[:, 1:2], None, ALU.add)
                v.tensor_scalar(cell_ix[:, h * HALF:(h + 1) * HALF], cell_f[:, h, :, 0],
                                rank[:, 1:2], None, ALU.add).then_inc(cell_ready, 1)

            def add_z(i, h, k):
                j = h * HALF + k
                n = 2 * i + h
                wait(v, gathered[j], 32 * (i + 1))
                if k == 0:
                    wait(v, z_stored[h], 16 * i)
                    wait(v, stat_done, HALF * (n - 1))
                v.tensor_tensor(zz[:, j, 0:H], gp[:, j, :], gq[:, j, :], ALU.add).then_inc(z_ready, 1)

            prep(0, 0)
            for k in range(HALF):
                equal(0, 0, k)
            cells(0, 0)

            def phase1(i):
                for h in range(2):
                    n = 2 * i + h
                    prep(n + 1, 1 - h)
                    for k in range(HALF):
                        equal(n + 1, 1 - h, k)
                        if k >= LAG:
                            add_z(i, h, k - LAG)
                    cells(n + 1, 1 - h)
                    for k in range(HALF - LAG, HALF):
                        add_z(i, h, k)
            loop(v, ITER, phase1, loop_signals)

            v.wait_ge(stat_done, CH)
            v.wait_ge(late_rows, 32)
            v.wait_ge(cell_ready, NHALF + 1)
            do(v.tensor_scalar(brow, ps[4][:, 0:H], 1.0 / E, None, ALU.mult))
            do(v.tensor_tensor(arow, brow, brow, ALU.mult))
            do(v.scalar_tensor_tensor(arow, ps[4][:, H:2 * H], 1.0 / E, arow, ALU.mult, ALU.subtract))
            do(v.tensor_scalar(arow, arow, 0.0, None, ALU.max))
            v.tensor_scalar(arow, arow, BN_EPS, None, ALU.add).then_inc(bn_var, 1)
            v.wait_ge(cnt_done, HALF * (NHALF + 1))
            do(v.tensor_scalar(dinv[:, :], ps[3][:, 0:NT], 0.0, None, ALU.is_gt))
            do(v.tensor_tensor(sc[:, 2, :], ps[3][:, 0:NT], dinv[:, :], ALU.mult))
            do(v.tensor_tensor(sc[:, 2, :], sc[:, 2, :], dinv[:, :], ALU.subtract))
            v.tensor_scalar(sc[:, 0, :], sc[:, 2, :], 1.0, None, ALU.add).then_inc(deg_var, 1)
            v.wait_ge(bn_std, 1)
            do(v.reciprocal(arow, arow))
            do(v.tensor_tensor(arow, arow, g1row, ALU.mult))
            do(v.tensor_tensor(brow, brow, arow, ALU.mult))
            do(v.tensor_tensor(brow, b1row, brow, ALU.subtract))
            v.wait_ge(deg_std, 1)
            do(v.reciprocal(sc[:, 2, :], sc[:, 1, :]))
            do(v.tensor_tensor(dinv[:, :], dinv[:, :], sc[:, 2, :], ALU.mult))

            def m_half(n, h, i_of):
                wait(v, m_sum, HALF * (n - 1))
                v.tensor_copy(mslot[:, h, :], table[:, bass.ds(HALF * n, HALF), 1]).then_inc(m_prep, 1)
                hs = slice(h * HALF, (h + 1) * HALF)
                wait(v, z_loaded[h], 16 * (i_of + 1))
                do(v.tensor_tensor(zin[:, hs, :], zin[:, hs, :], arow.unsqueeze(1).to_broadcast([P, HALF, H]), ALU.mult))
                v.tensor_tensor(zin[:, hs, :], zin[:, hs, :], brow.unsqueeze(1).to_broadcast([P, HALF, H]),
                                ALU.add).then_inc(affine, 1)
                for c in range(COPIES):
                    last = max(j for j in range((h + 1) * HALF) if j % COPIES == c)
                    wait(v, m_added[c], 16 * (chain_before(i_of, last) + 1 - chain_per(c)))
                wait(v, weight_added, 16 * (WPRE + WP2 * (i_of - 1) + (WP2 if h else len(EXTRA[0]))))
                nw = len(EXTRA[h])
                ws = bass.ds(WPRE + WP2 * i_of + (len(EXTRA[0]) if h else 0), nw)
                v.tensor_copy(m_ix[:, hs], midx[:, bass.ds(HALF * n, HALF)])
                v.tensor_copy(w_vals[:, h * HALF:h * HALF + nw], wval[:, ws])
                v.tensor_copy(w_ix[:, h * HALF:h * HALF + nw], wcell[:, ws]).then_inc(slots_ready, 1)

            def m_equal(i, h):
                for k in range(HALF):
                    j = h * HALF + k
                    c = 2 * HALF * i + j
                    wait(v, m_rows, rows_value(2 * i + h, k))
                    wait(v, m_sum, c - HALF + 1)
                    v.tensor_scalar(eqm[k], row_slot(k)[:, 0:P], mslot[:, h, k:k + 1], None, ALU.is_equal).then_inc(m_eq, 1)

            m_half(0, 0, 0)

            def phase2(i):
                m_equal(i, 0)
                m_half(2 * i + 1, 1, i)
                m_equal(i, 1)
                m_half(2 * i + 2, 0, i + 1)
            loop(v, ITER - 1, phase2, loop_signals)
            m_equal(ITER - 1, 0)
            m_half(NHALF - 1, 1, ITER - 1)
            m_equal(ITER - 1, 1)

            def low_lhs(pi, s, ts, got):
                v.wait_ge(lhs_high, lhs_step(pi, s))
                v.tensor_tensor(lhs_split(pi, 1)[:, ts, :], got, lhs_split(pi, 0)[:, ts, :].bitcast(F32),
                                ALU.subtract).then_inc(lhs_low, 1)

            def low_step(pi, s):
                ts = slice(s * LG, (s + 1) * LG)
                low_lhs(pi, s, ts, view(lhs_at[pi][1], NT, H)[:, ts, :])

            def low_pair(pi, gi):
                ts = slice(2 * gi, min(NT, 2 * gi + 2))
                low_lhs(pi, gi, ts, out_pair[gi % 2][:, 0:ts.stop - ts.start, :])

            def sum_copies(s):
                ts = slice(s * LG, (s + 1) * LG)
                en = view(RE, NT, H)[:, ts, :]
                v.wait_ge(en_loaded[s], 16 * COPIES)
                do(v.tensor_tensor(en, en, g_nat[:, ts, :], ALU.add))
                v.tensor_tensor(en, en, view(RD, NT, H)[:, ts, :], ALU.add).then_inc(lhs_in, 1)

            def drain_agg0(gi):
                for key in group_keys(gi):
                    bank = empty_bank(v, number["agg0", key])
                    _, j, b = key
                    bs = slice(b * BLK, (b + 1) * BLK)
                    emptied(v.scalar_tensor_tensor(uT[:, j, bs], gT[:, j, bs], epsc[:, 3:4], bank[:, 0:BLK],
                                                   ALU.mult, ALU.add))

            for s in range(NSPLIT):
                sum_copies(s)
                low_step(0, s)
                for q in range(s * ROWS, (s + 1) * ROWS):
                    low_rows(q)
            v.wait_ge(w_loaded, 16 * LOADS)
            do(v.tensor_scalar(epsc[:, 3:4], epsc[:, 0:1], 1.0, None, ALU.add))

            low_pass(0, NSPLIT * ROWS, drain_agg0)
            v.wait_ge(gat_loaded, 32)
            for k, (side, j) in enumerate((side, j) for side in range(2) for j in range(JH)):
                do(v.tensor_tensor(attn_tmp[:, 0, :], gatw[:, j, 0:H], attn[:, side, :], ALU.mult))
                v.tensor_reduce(gatw[:, j, H + side * HEADS:H + (side + 1) * HEADS],
                                attn_tmp[:, 0, :].rearrange("p (h d) -> p h d", h=HEADS), AX_X, ALU.add).then_inc(gat_w_ready, 1)
                v.wait_ge(gat_w_ready, k + 1)
            for r, (stage, src_T, nj, gam, bet) in enumerate((("h2", h2T, 2 * JH, "g2a", "b2a"), ("h3", h3T, JH, "g2b", "b2b"))):
                for j in range(nj):
                    for b in range(NB):
                        v.wait_ge(drained_a, nth[number[stage, (j, b)]])
                        last = v.bn_stats(stats[:, j * NB + b, :], src_T[:, j, b * BLK:min(N, (b + 1) * BLK)])
                do(last)
                for j in range(nj):
                    last = v.bn_aggr(mv[:, j, :], stats[:, j * NB:(j + 1) * NB, :])
                do(last)
                v.tensor_scalar(sc[:, 0, 0:nj], mv[:, 0:nj, 1], BN_EPS, None, ALU.add).then_inc(bnn_var, 1)
                v.wait_ge(bnn_std, r + 1)
                do(v.reciprocal(sc[:, 2, 0:nj], sc[:, 1, 0:nj]))
                do(v.tensor_tensor(sc[:, 2, 0:nj], sc[:, 2, 0:nj], vec[:, V0[gam]:V0[gam] + nj], ALU.mult))
                do(v.tensor_tensor(sc[:, 3, 0:nj], mv[:, 0:nj, 0], sc[:, 2, 0:nj], ALU.mult))
                v.tensor_tensor(sc[:, 3, 0:nj], vec[:, V0[bet]:V0[bet] + nj], sc[:, 3, 0:nj], ALU.subtract).then_inc(bnn_scale, 1)
            v.memset(h3T[:, :, LD:NP], 0.0).then_inc(tail0, 1)

            layernorm(1, lambda q: add_pairs("back0", step_pairs(q)))
            v.wait_ge(filled, number["h3", (JH - 1, NB - 1)] + 1)
            v.memset(x0T[:, :, LD:NP], 0.0)
            v.memset(supT[:, :, LD:NP], 0.0).then_inc(sup_tail, 1)
            v.wait_ge(filled, number["x0", (JH - 1, NB - 1)] + 1)
            for gi in range(NPAIR):
                ts, got = pair_bank("x0n", gi)
                do(v.tensor_copy(lhs_split(1, 0)[:, ts, :], got))
                emptied(v.tensor_tensor(lhs_split(1, 1)[:, ts, :], got, lhs_split(1, 0)[:, ts, :].bitcast(F32),
                                        ALU.subtract))
            for gi in range(-(-NT // 4)):
                bank = empty_bank(v, number["dinv", (gi,)])
                o = gi * 4 * P
                end = min(o + 4 * P, LD)
                pieces = [(row, lo, max(o, lo), min(end, hi)) for row, lo, hi in ((dinv_row, 0, DR), (dinv_end, DR, LD))
                          if max(o, lo) < min(end, hi)]
                for row, lo, a, z in pieces:
                    ins = v.tensor_scalar(row[:, a - lo:z - lo], bank[:, a - o:z - o], 1.0 - ALPHA, None, ALU.mult)
                    if z < end:
                        do(ins)
                emptied(ins)
            after(number["dinv", (6,)])

            def drain_agg1(li, gi):
                for key in group_keys(gi):
                    bank = empty_bank(v, number[f"agg1{li}", key])
                    _, j, b = key
                    bs = slice(b * BLK, (b + 1) * BLK)
                    scale_row = dinv_row[:, bs] if b < NB - 1 else dinv_end
                    do(v.tensor_tensor(supT[:, j, bs], bank[:, 0:BLK], scale_row, ALU.mult))
                    emptied(v.scalar_tensor_tensor(supT[:, j, bs], x0T[:, j, bs], ALPHA, supT[:, j, bs],
                                                   ALU.mult, ALU.add))

            for q in range(PU, PU + ROWS):
                low_rows(q)
            for li in range(3):
                low_pass(1 + li, ROWS, lambda gi: drain_agg1(li, gi))
                if li < 2:
                    for q in range((2 + li) * PU, (2 + li) * PU + ROWS):
                        low_rows(q)
                for gi in range(NPAIR) if li < 2 else ():
                    ts, got = pair_bank(f"cv{li}", gi)
                    pair = out_pair[gi % 2][:, 0:ts.stop - ts.start, :]
                    if gi >= 2:
                        v.wait_ge(lhs_low, lhs_step(2 + li, gi - 2))
                    emptied(v.scalar_tensor_tensor(pair, got, 0.0, lhs_split(1, 0)[:, ts, :].bitcast(F32), ALU.max, ALU.add))
                    after(number[f"cv{li}", (gi,)])
                    v.tensor_tensor(pair, pair, lhs_split(1, 1)[:, ts, :].bitcast(F32), ALU.add).then_inc(lhs_in, 1)
                    if gi:
                        low_pair(2 + li, gi - 1)
                if li < 2:
                    low_pair(2 + li, NPAIR - 1)

            def last_layer(q):
                for gi in step_pairs(q):
                    ts, got = pair_bank("cv2", gi)
                    pair = out_pair[gi % 2][:, 0:ts.stop - ts.start, :]
                    emptied(v.scalar_tensor_tensor(pair, got, 0.0, lhs_split(1, 0)[:, ts, :].bitcast(F32), ALU.max, ALU.add))
                    do(v.tensor_tensor(x_nat[:, ts, :], x_nat[:, ts, :], lhs_split(1, 1)[:, ts, :].bitcast(F32), ALU.add))
                    after(number["cv2", (gi,)])
                    do(v.tensor_tensor(x_nat[:, ts, :], x_nat[:, ts, :], pair, ALU.add))

            layernorm(2, last_layer)

            def logits(q):
                ts = slice(q * LG, (q + 1) * LG)
                v.wait_ge(edge_l, 16 * NT)
                v.wait_ge(edge_x[q], 16 * LG)
                do(v.tensor_tensor(al[:, ts, :], el[:, ts, :], xt_edge[:, ts, H + HEADS:XW], ALU.add))
                do(v.scalar_tensor_tensor(al[:, ts, :], al[:, ts, :], 0.01, al[:, ts, :], ALU.mult, ALU.max))
                do(v.tensor_reduce(am[:, 0, ts], al[:, ts, :], AX_X, ALU.max))
                v.tensor_tensor(al[:, ts, :], al[:, ts, :], bcast(am[:, 0, ts], HEADS), ALU.subtract).then_inc(exp_in, 1)

            def mix_heads(q):
                for s in ((0, 1) if q == 0 else (q + 1,)):
                    if s < NSPLIT:
                        logits(s)
                ts = slice(q * LG, (q + 1) * LG)
                v.wait_ge(exp_out, q + 1)
                do(v.tensor_reduce(am[:, 0, ts], al[:, ts, :], AX_X, ALU.add))
                do(v.reciprocal(am[:, 1, ts], am[:, 0, ts]))
                do(v.tensor_tensor(al[:, ts, :], al[:, ts, :], bcast(am[:, 1, ts], HEADS), ALU.mult))
                for hd in range(HEADS):
                    last = v.tensor_tensor(mix[:, ts, hd * OC:(hd + 1) * OC], xt_edge[:, ts, hd * OC:(hd + 1) * OC],
                                           al[:, ts, hd:hd + 1].to_broadcast([P, LG, OC]), ALU.mult)
                do(last)
                do(v.tensor_tensor(mix[:, ts, 0:2 * OC], mix[:, ts, 0:2 * OC], mix[:, ts, 2 * OC:H], ALU.add))
                do(v.tensor_tensor(mix[:, ts, 0:OC], mix[:, ts, 0:OC], mix[:, ts, OC:2 * OC], ALU.add))
                for hd in range(HEADS):
                    last = v.tensor_tensor(x_nat[:, ts, hd * OC:(hd + 1) * OC], x_nat[:, ts, hd * OC:(hd + 1) * OC],
                                           mix[:, ts, 0:OC], ALU.add)
                do(last)

            v.wait_ge(xt_stored, 16 * NSPLIT)
            layernorm(3, mix_heads)
            v.wait_ge(gat_loaded, 64)
            products = [w2a_flat[:, k * H:(k + 1) * H] for k in range(4)] + [w2b[:, 2, :]]
            for s in range(NSPLIT):
                ts = slice(s * LG, (s + 1) * LG)
                for gi in step_pairs(s):
                    pair, got = pair_bank("xj", gi)
                    n = pair.stop - pair.start
                    emptied(v.tensor_tensor(xj_nat[:, pair, :], got, ab2row.unsqueeze(1).to_broadcast([P, n, H]), ALU.add))
                after(number["xj", (step_pairs(s)[-1],)])
                v.scalar_tensor_tensor(xj_nat[:, ts, :], xj_nat[:, ts, :], 0.2, xj_nat[:, ts, :], ALU.mult,
                                       ALU.max).then_inc(lhs_in, 1)
                v.wait_ge(lhs_in, lhs_step(4, s))
                for t in range(s * LG, (s + 1) * LG):
                    last = v.tensor_tensor_reduce(products[t % LG], xj_nat[:, t, :], wa2row, 1.0, 0.0, ALU.mult,
                                                  ALU.add, a2[:, t:t + 1])
                do(last)
                v.tensor_scalar(a2[:, ts], a2[:, ts], epsc[:, 2:3], None, ALU.add).then_inc(xj_ready, 1)
                if s:
                    low_step(4, s - 1)
            low_step(4, NSPLIT - 1)
            for j in range(JH):
                for b in range(NB):
                    v.wait_ge(drained_a, nth[number["xi", (j, b)]])
                    bs = slice(b * BLK, (b + 1) * BLK)
                    v.scalar_tensor_tensor(xiT[:, j, bs], xiT[:, j, bs], 0.2, xiT[:, j, bs], ALU.mult,
                                           ALU.max).then_inc(xi_ready, 1)

            def drain_out(gi):
                for key in group_keys(gi):
                    bank = empty_bank(v, number["agg3", key])
                    _, j, b = key
                    emptied(v.tensor_copy(oT[:, j, b * BLK:(b + 1) * BLK], bank[:, 0:BLK]))


            def count_att(u):
                q, w = 4 * PU + u, unit_width(u)
                v.wait_ge(att_sig, u + 1)
                v.wait_ge(ring_full[q % RING], 16 * (q // RING + 1))
                v.tensor_tensor(ring[q % RING][:, 0:w], att[u % ROWS][:, 0:w], ring[q % RING][:, 0:w],
                                ALU.mult).then_inc(att_mul, 1)

            for u in range(AHEAD):
                count_att(u)
            for u in range(PU):
                if u + AHEAD < PU:
                    count_att(u + AHEAD)
                if u == GU + DRAIN_AT:
                    drain_out(0)
                low_rows(4 * PU + u)
            drain_out(1)
            v.memset(oT[:, :, LD:NP], 0.0).then_inc(out_t, 1)
            v.wait_ge(x_plus, 1)
            add_pairs("back3", range(NPAIR))


_INS = ['x', 'src', 'dst', 'edge_weight', 'L0_gnn_edge_rep', 'L0_gnn_W1', 'L0_gnn_g1', 'L0_gnn_b1', 'L0_gnn_W2a',
        'L0_gnn_g2a', 'L0_gnn_b2a', 'L0_gnn_W2b', 'L0_gnn_g2b', 'L0_gnn_b2b', 'L0_gnn_epsilon', 'L1_gnn_lin0_w',
        'L1_gnn_lin0_b', 'L1_gnn_conv_w', 'L2_gnn_weight', 'L2_gnn_attn_l', 'L2_gnn_attn_r', 'L3_gnn_W1',
        'L3_gnn_b1', 'L3_gnn_W2', 'L3_gnn_b2', 'L3_gnn_wa1', 'L3_gnn_ba1', 'L3_gnn_wa2', 'L3_gnn_ba2']


def kernel(**inputs):
    import numpy as _np
    import concourse.bacc as _bacc
    from concourse import mybir as _mybir
    from concourse.bass_utils import run_bass_kernel_spmd as _run

    nc = _bacc.Bacc("TRN2", target_bir_lowering=False, num_devices=1)
    arrays, args = {}, []
    for name in _INS:
        a = _np.ascontiguousarray(inputs[name])
        if a.ndim == 0:
            a = a.reshape(1)
        arrays[f"in_{name}_dram"] = a
        args.append(nc.dram_tensor(f"in_{name}_dram", a.shape, _mybir.dt.from_np(a.dtype), kind="ExternalInput").ap())
    args.append(nc.dram_tensor("out_0_dram", (N, H), F32, kind="ExternalOutput").ap())
    gnn_kernel(nc, *args)
    r = _run(nc, [arrays], core_ids=[0])
    return r.results[0]["out_0_dram"]
```
